# Optimizing a Trainium2 kernel written in Bass

```python
import numpy as np
import jax
import jax.numpy as jnp

def _softmax(x, axis=-1):
    return jax.nn.softmax(x, axis=axis)

def _gelu(x):
    return jax.nn.gelu(x, approximate=True)

def _silu(x):
    return jax.nn.silu(x)

def _sigmoid(x):
    return jax.nn.sigmoid(x)

def _layernorm(x, axis=-1, eps=1e-05):
    m = jnp.mean(x, axis=axis, keepdims=True)
    v = jnp.var(x, axis=axis, keepdims=True)
    return (x - m) / jnp.sqrt(v + eps)

def _scatter_add(tgt, idx, src, axis=0):
    return tgt.at[idx].add(src)

def _segment_sum(src, seg, n):
    return jax.ops.segment_sum(src, seg, n)
kernel_name = 'mk_recurrent_d2_jaxref_r8_e3ce61'

def setup_inputs(seed: int=0):
    np.random.seed(seed)
    _w = jnp.asarray

    def _L0_attn_setup():
        import jax, jax.numpy as jnp
        import numpy as np
        key = jax.random.key(seed)
        k1, k2, k3, k4, k5 = jax.random.split(key, 5)
        B, L, D = (4, 512, 128)
        return {'x': jax.random.normal(k1, (B, L, D), dtype=jnp.float32), 'phazor': jax.random.normal(k2, (D, 2), dtype=jnp.float32), 'phazor_init': jax.random.normal(k3, (D, 2), dtype=jnp.float32), 'last_conv_re': jax.random.normal(k4, (D,), dtype=jnp.float32), 'last_conv_im': jax.random.normal(k5, (D,), dtype=jnp.float32)}
    _L0_attn_in = _L0_attn_setup()

    def _L0_ffn_setup():
        import jax, jax.numpy as jnp
        import numpy as np
        H = 128
        E = 32
        TOP_K = 4
        I = 96
        I_SH = 256
        SCALE = 0.02
        key = jax.random.key(seed)
        ks = jax.random.split(key, 9)
        inp = {'hidden_states': jax.random.normal(ks[0], (2, 64, H), dtype=jnp.float32), 'router_w': jax.random.normal(ks[1], (H, E), dtype=jnp.float32) * SCALE, 'w_gate': jax.random.normal(ks[2], (E, H, I), dtype=jnp.float32) * SCALE, 'w_up': jax.random.normal(ks[3], (E, H, I), dtype=jnp.float32) * SCALE, 'w_down': jax.random.normal(ks[4], (E, I, H), dtype=jnp.float32) * SCALE, 'sh_gate': jax.random.normal(ks[5], (H, I_SH), dtype=jnp.float32) * SCALE, 'sh_up': jax.random.normal(ks[6], (H, I_SH), dtype=jnp.float32) * SCALE, 'sh_down': jax.random.normal(ks[7], (I_SH, H), dtype=jnp.float32) * SCALE, 'sh_gate_w': jax.random.normal(ks[8], (H, 1), dtype=jnp.float32) * SCALE}
        return inp
    _L0_ffn_in = _L0_ffn_setup()

    def _L1_attn_setup():
        import jax, jax.numpy as jnp
        import numpy as np
        DIM = 128
        B, S = (4, 512)
        key = jax.random.key(seed)
        ks = jax.random.split(key, 7)
        s = 1.0 / np.sqrt(DIM)
        return {'x': jax.random.normal(ks[0], (B, S, DIM), dtype=jnp.float32), 'wq': jax.random.uniform(ks[1], (DIM, DIM), minval=-s, maxval=s, dtype=jnp.float32), 'bq': jax.random.uniform(ks[2], (DIM,), minval=-s, maxval=s, dtype=jnp.float32), 'wk': jax.random.uniform(ks[3], (DIM, DIM), minval=-s, maxval=s, dtype=jnp.float32), 'bk': jax.random.uniform(ks[4], (DIM,), minval=-s, maxval=s, dtype=jnp.float32), 'wv': jax.random.uniform(ks[5], (DIM, DIM), minval=-s, maxval=s, dtype=jnp.float32), 'bv': jax.random.uniform(ks[6], (DIM,), minval=-s, maxval=s, dtype=jnp.float32)}
    _L1_attn_in = _L1_attn_setup()

    def _L1_ffn_setup():
        import jax, jax.numpy as jnp
        import numpy as np
        E = 8
        TOP_K = 2
        H = 128
        I = 64
        B, S = (2, 256)

        def _moe_forward(hidden_states, w_gate, w_fc, w_proj):
            b, s, h = hidden_states.shape
            x = hidden_states.reshape(-1, h)
            T = x.shape[0]
            router_logits = x @ w_gate.T
            topk_vals, topk_idx = jax.lax.top_k(router_logits, TOP_K)
            router_weights = jax.nn.softmax(topk_vals.astype(jnp.float32), axis=-1).astype(x.dtype)
            gates = jnp.zeros((T, E), x.dtype).at[jnp.arange(T)[:, None], topk_idx].add(router_weights)
            hmid = jax.nn.gelu(jnp.einsum('th,eih->tei', x, w_fc), approximate=False)
            y = jnp.einsum('tei,ehi->teh', hmid, w_proj)
            out = jnp.einsum('teh,te->th', y, gates)
            return out.reshape(b, s, h)
        key = jax.random.key(seed)
        k0, k1, k2, k3 = jax.random.split(key, 4)
        std = 0.02
        return {'hidden_states': jax.random.normal(k0, (B, S, H), dtype=jnp.float32), 'w_gate': jax.random.normal(k1, (E, H), dtype=jnp.float32) * std, 'w_fc': jax.random.normal(k2, (E, I, H), dtype=jnp.float32) * std, 'w_proj': jax.random.normal(k3, (E, H, I), dtype=jnp.float32) * (std / np.sqrt(48.0))}
    _L1_ffn_in = _L1_ffn_setup()
    _d = {'L0_attn_x': _L0_attn_in['x'], 'L0_attn_phazor': _L0_attn_in['phazor'], 'L0_attn_phazor_init': _L0_attn_in['phazor_init'], 'L0_attn_last_conv_re': _L0_attn_in['last_conv_re'], 'L0_attn_last_conv_im': _L0_attn_in['last_conv_im'], 'L0_ffn_router_w': _L0_ffn_in['router_w'], 'L0_ffn_w_gate': _L0_ffn_in['w_gate'], 'L0_ffn_w_up': _L0_ffn_in['w_up'], 'L0_ffn_w_down': _L0_ffn_in['w_down'], 'L0_ffn_sh_gate': _L0_ffn_in['sh_gate'], 'L0_ffn_sh_up': _L0_ffn_in['sh_up'], 'L0_ffn_sh_down': _L0_ffn_in['sh_down'], 'L0_ffn_sh_gate_w': _L0_ffn_in['sh_gate_w'], 'L1_attn_wq': _L1_attn_in['wq'], 'L1_attn_bq': _L1_attn_in['bq'], 'L1_attn_wk': _L1_attn_in['wk'], 'L1_attn_bk': _L1_attn_in['bk'], 'L1_attn_wv': _L1_attn_in['wv'], 'L1_attn_bv': _L1_attn_in['bv'], 'L1_ffn_w_gate': _L1_ffn_in['w_gate'], 'L1_ffn_w_fc': _L1_ffn_in['w_fc'], 'L1_ffn_w_proj': _L1_ffn_in['w_proj']}
    _x0 = _d['L0_attn_x']
    _d['L0_attn_x'] = jax.random.normal(jax.random.fold_in(jax.random.key(seed), 1), (16, 256, 128), dtype=_x0.dtype)
    del _x0
    return _d

def reference(L0_attn_x, L0_attn_phazor, L0_attn_phazor_init, L0_attn_last_conv_re, L0_attn_last_conv_im, L0_ffn_router_w, L0_ffn_w_gate, L0_ffn_w_up, L0_ffn_w_down, L0_ffn_sh_gate, L0_ffn_sh_up, L0_ffn_sh_down, L0_ffn_sh_gate_w, L1_attn_wq, L1_attn_bq, L1_attn_wk, L1_attn_bk, L1_attn_wv, L1_attn_bv, L1_ffn_w_gate, L1_ffn_w_fc, L1_ffn_w_proj):

    def _L0_attn_ref(x, phazor, phazor_init, last_conv_re, last_conv_im):
        import jax, jax.numpy as jnp
        import numpy as np
        B, L, D = x.shape
        in_dtype = x.dtype
        x = x.astype(jnp.float32)
        ph = jax.lax.complex(phazor[:, 0], phazor[:, 1])
        ph_init = jax.lax.complex(phazor_init[:, 0], phazor_init[:, 1])
        last_conv = jax.lax.complex(last_conv_re, last_conv_im)
        mag = jnp.abs(ph)
        ph = ph / mag * jnp.exp(-mag)
        t = jnp.arange(L)[:, None]
        prog = ph[None, :] ** t
        filt = prog * ph_init[None, :]
        filt_fft = jnp.fft.fft(filt, n=2 * L, axis=0)
        x_fft = jnp.fft.fft(x, n=2 * L, axis=1)
        conv = jnp.fft.ifft(filt_fft[None, :, :] * x_fft, axis=1)[:, :L, :]
        conv_with_past = conv + last_conv[None, None, :] * prog[None, :, :] * ph[None, None, :]
        return conv_with_past.real.astype(in_dtype)

    def _L0_ffn_ref(hidden_states, router_w, w_gate, w_up, w_down, sh_gate, sh_up, sh_down, sh_gate_w):
        import jax, jax.numpy as jnp
        import numpy as np
        H = 128
        E = 32
        TOP_K = 4
        I = 96
        I_SH = 256
        SCALE = 0.02
        orig_shape = hidden_states.shape
        x = hidden_states.reshape(-1, H)
        logits = x @ router_w
        probs = jax.nn.softmax(logits, axis=-1)
        topk_w, topk_idx = jax.lax.top_k(probs, TOP_K)
        topk_w = topk_w / jnp.sum(topk_w, axis=-1, keepdims=True)
        combine = jnp.sum(jax.nn.one_hot(topk_idx, E, dtype=x.dtype) * topk_w[..., None], axis=1)
        g = jnp.einsum('th,ehi->tei', x, w_gate)
        u = jnp.einsum('th,ehi->tei', x, w_up)
        act = jax.nn.silu(g) * u
        eo = jnp.einsum('tei,eih->teh', act, w_down)
        routed = jnp.einsum('te,teh->th', combine, eo)
        sh = jax.nn.silu(x @ sh_gate) * (x @ sh_up) @ sh_down
        sh = sh * jax.nn.sigmoid(x @ sh_gate_w)
        return (routed + sh).reshape(orig_shape)

    def _L1_attn_ref(x, wq, bq, wk, bk, wv, bv):
        import jax, jax.numpy as jnp
        import numpy as np
        DIM = 128
        B, S = (4, 512)
        scale = x.shape[-1] ** (-0.5)
        q = x @ wq.T + bq
        k = x @ wk.T + bk
        v = x @ wv.T + bv
        scores = jnp.einsum('bqd,bkd->bqk', q, k) * scale
        attn = jax.nn.softmax(scores, axis=-1)
        return jnp.einsum('bqk,bkd->bqd', attn, v)

    def _L1_ffn_ref(hidden_states, w_gate, w_fc, w_proj):
        import jax, jax.numpy as jnp
        import numpy as np
        E = 8
        TOP_K = 2
        H = 128
        I = 64
        B, S = (2, 256)

        def _moe_forward(hidden_states, w_gate, w_fc, w_proj):
            b, s, h = hidden_states.shape
            x = hidden_states.reshape(-1, h)
            T = x.shape[0]
            router_logits = x @ w_gate.T
            topk_vals, topk_idx = jax.lax.top_k(router_logits, TOP_K)
            router_weights = jax.nn.softmax(topk_vals.astype(jnp.float32), axis=-1).astype(x.dtype)
            gates = jnp.zeros((T, E), x.dtype).at[jnp.arange(T)[:, None], topk_idx].add(router_weights)
            hmid = jax.nn.gelu(jnp.einsum('th,eih->tei', x, w_fc), approximate=False)
            y = jnp.einsum('tei,ehi->teh', hmid, w_proj)
            out = jnp.einsum('teh,te->th', y, gates)
            return out.reshape(b, s, h)
        return _moe_forward(hidden_states, w_gate, w_proj=w_proj, w_fc=w_fc)
    x = L0_attn_x
    xn = _layernorm(x, axis=-1)
    s = _L0_attn_ref(xn, L0_attn_phazor, L0_attn_phazor_init, L0_attn_last_conv_re, L0_attn_last_conv_im)
    g = _silu(_L0_ffn_ref(xn, L0_ffn_router_w, L0_ffn_w_gate, L0_ffn_w_up, L0_ffn_w_down, L0_ffn_sh_gate, L0_ffn_sh_up, L0_ffn_sh_down, L0_ffn_sh_gate_w))
    x = x + s * g
    xn = _layernorm(x, axis=-1)
    s = _L1_attn_ref(xn, L1_attn_wq, L1_attn_bq, L1_attn_wk, L1_attn_bk, L1_attn_wv, L1_attn_bv)
    g = _silu(_L1_ffn_ref(xn, L1_ffn_w_gate, L1_ffn_w_fc, L1_ffn_w_proj))
    x = x + s * g
    return x

_drawn_inputs = setup_inputs


def setup_inputs(seed=0):
    import zlib

    import numpy as np

    out = dict(_drawn_inputs(seed))
    spreads = {}
    factors = {'L0_attn_phazor': 8.0,
     'L0_attn_phazor_init': 8.0,
     'L0_attn_last_conv_re': 64.0,
     'L0_attn_last_conv_im': 64.0,
     'L0_ffn_router_w': 8.0,
     'L0_ffn_w_gate': 8.0,
     'L0_ffn_w_up': 8.0,
     'L0_ffn_w_down': 8.0,
     'L0_ffn_sh_gate': 8.0,
     'L0_ffn_sh_up': 8.0,
     'L0_ffn_sh_down': 8.0,
     'L0_ffn_sh_gate_w': 8.0,
     'L1_attn_wq': 26.516,
     'L1_attn_bq': 64.0,
     'L1_attn_wk': 26.343,
     'L1_attn_wv': 26.65,
     'L1_attn_bv': 64.0,
     'L1_ffn_w_gate': 28.404,
     'L1_ffn_w_fc': 29.662,
     'L1_ffn_w_proj': 26.127,
     'L1_attn_bk': 8.0}
    for name, (base, spread) in spreads.items():
        noise = np.random.default_rng([zlib.crc32(name.encode()), seed]).standard_normal(out[name].shape)
        drawn = base * np.exp(spread * noise) if base else spread * noise
        out[name] = jnp.asarray(drawn.astype(out[name].dtype))
    for name, factor in factors.items():
        out[name] = (out[name] * factor).astype(out[name].dtype)
    return out
```

```python
from contextlib import ExitStack

import concourse.bass as bass
from concourse import mybir

ALU = mybir.AluOpType
ACT = mybir.ActivationFunctionType
AX = mybir.AxisListType
F32 = mybir.dt.float32
BF16 = mybir.dt.bfloat16
I32 = mybir.dt.int32
U32 = mybir.dt.uint32

P = 128
SEQ = 256
NSEQ = 16
NT = NSEQ * SEQ // P
GT = 4
NG = NT // GT
GW = GT * P
E0, I0, TOP0 = 32, 96, 4
ISH = 256
E1, I1 = 8, 64
CH1 = E1 * I1 // P
NH = 2
HT = NT // NH
ST = -(-(HT * P * TOP0 + E0 * (P - 1)) // P // GT) * GT
SG = ST // GT
EPS = 1e-5
SCALE = float(P) ** -0.5


class Chain:

    def __init__(self, eng, sem):
        self.eng, self.sem, self.n, self.base = eng, sem, 0, 0

    def link(self, ins):
        self.n += 1
        ins.then_inc(self.sem, 1)
        self.eng.wait_ge(self.sem, self.base + self.n)


def rounds(eng, count, unroll, body, chains=()):
    start = [c.n for c in chains]
    for s in range(unroll):
        body(s, s, True)
    per = [c.n - n for c, n in zip(chains, start)]
    if count > unroll:
        with eng.Fori(1, count // unroll) as i:
            for c, n, k in zip(chains, start, per):
                c.n, c.base = n, i * k
            for s in range(unroll):
                body(i * unroll + s, s, False)
            for c, n, k in zip(chains, start, per):
                assert c.n - n == k
    for c, n, k in zip(chains, start, per):
        c.n, c.base = n + k * (count // unroll), 0


def lagged(eng, sem, it, slot, first, lag, per=1):
    if not first or slot >= lag:
        eng.wait_ge(sem, (it - lag + 1) * per)


def rsqrt_steps(nc, link, y, v, t):
    yi, vi = y.bitcast(I32), v.bitcast(I32)
    link(nc.vector.tensor_scalar(yi, vi, 1, None, ALU.logical_shift_right))
    link(nc.vector.tensor_scalar(yi, yi, -1.0, float(0x5F3759DF), ALU.mult, ALU.add))
    for _ in range(4):
        link(nc.vector.tensor_tensor(t, y, y, ALU.mult))
        link(nc.vector.tensor_tensor(t, t, v, ALU.mult))
        link(nc.vector.tensor_scalar(t, t, -0.5, 1.5, ALU.mult, ALU.add))
        link(nc.vector.tensor_tensor(y, y, t, ALU.mult))


def build(nc, x, phazor, phazor_init, last_re, last_im, router_w, w_gate, w_up, w_down, sh_gate, sh_up,
          sh_down, sh_gate_w, wq, bq, wk, bk, wv, bv, w_gate1, w_fc, w_proj, out):
    slot_rows = [nc.dram_tensor(f"slot_rows{r}", [ST * P, P], F32, kind="Internal").ap() for r in range(NH)]
    expert_rows = [nc.dram_tensor(f"expert_rows{r}", [ST * P, P], F32, kind="Internal").ap() for r in range(NH)]
    slot_groups = [t.rearrange("(g p j) d -> g p (j d)", p=P, j=GT) for t in slot_rows]
    expert_groups = [t.rearrange("(g p j) d -> g p (j d)", p=P, j=GT) for t in expert_rows]
    x_rows = x.rearrange("b (t p) d -> p (b t) d", p=P)
    out_rows = out.rearrange("b (t p) d -> b p t d", p=P)

    ctx = ExitStack()
    with ctx:
        def sb(name, shape, dt=F32):
            return ctx.enter_context(nc.sbuf_tensor(name, shape, dt))

        def sem(name):
            return ctx.enter_context(nc.semaphore(name))

        x_tok = sb("x_tok", [P, NT, P])
        xn_tok = sb("xn_tok", [P, NT, P])
        xnT = sb("xnT", [P, NT * P])
        shT = sb("shT", [P, NT * P])
        w_gu = sb("w_gu", [P, E0, 2 * I0])
        w_dn = sb("w_dn", [I0, E0 * P])
        logits = sb("logits", [P, NT, E0])
        top_w = sb("top_w", [P, NT * TOP0])
        slot_of = sb("slot_of", [P, NT * TOP0], I32)
        tile_expert = sb("tile_expert", [1, NH * ST], I32)
        ident = sb("ident", [P, P])
        ones = sb("ones", [P, P])
        rw = sb("rw", [P, E0])
        shg = sb("shg", [P, ISH])
        shu = sb("shu", [P, ISH])
        shd = sb("shd", [P, ISH // P, P])
        shgw = sb("shgw", [P, 1])
        shgw_b = sb("shgw_b", [P, P])
        raw1 = sb("raw1", [P, 3, P])
        raw_fc = sb("raw_fc", [P, CH1, P])
        raw_pr = sb("raw_pr", [P, E1, I1])
        raw_g1 = sb("raw_g1", [E1, P])
        w1T = sb("w1T", [P, 3, P])
        fcT = sb("fcT", [P, CH1, P])
        prT = sb("prT", [P, CH1, P])
        g1T = sb("g1T", [P, E1])
        bqk = sb("bqk", [P, 2])
        bv_b = sb("bv_b", [P, P])
        expert_sel = sb("expert_sel", [E1, CH1, P])
        zeros = sb("zeros", [P, 2048])
        iota_e = sb("iota_e", [P, E0])
        iota_t1 = sb("iota_t1", [P, SEQ])
        iota_p = sb("iota_p", [P, 1])
        before = sb("before", [P, P], BF16)
        ones_bf = sb("ones_bf", [P, P], BF16)
        not_first = sb("not_first", [P, E0, HT])
        phz = sb("phz", [P, 6])
        cs = sb("cs", [P, 16])
        cos_t = sb("cos_t", [P, SEQ])
        sin_t = sb("sin_t", [P, SEQ])
        out_c = sb("out_c", [P, SEQ])
        out_s = sb("out_s", [P, SEQ])
        past = sb("past", [P, SEQ])
        decay_t1 = sb("decay_t1", [P, SEQ])
        decay = sb("decay", [P, GW])
        tab_tmp = sb("tab_tmp", [P, SEQ])
        stats = sb("stats", [P, NT, 6])
        mean = sb("mean", [P, NT])
        var = sb("var", [P, NT])
        rstd = sb("rstd", [P, NT])
        rtmp = sb("rtmp", [P, NT])
        xs = [sb(f"xs{u}", [P, GT, P]) for u in range(2)]
        xTs = [sb(f"xTs{u}", [P, GW]) for u in range(2)]
        top8 = sb("top8", [P, HT, 8])
        top8_i = sb("top8_i", [P, HT, 8], U32)
        top_f = sb("top_f", [P, HT * TOP0])
        tw = sb("tw", [P, HT, TOP0])
        tsum = sb("tsum", [P, HT])
        onehot = sb("onehot", [P, HT * TOP0, E0])
        mask = sb("mask", [P, HT, E0], BF16)
        tot_em = sb("tot_em", [P, E0, HT])
        cum_em = sb("cum_em", [P, E0, HT])
        pos = sb("pos", [P, HT, E0])
        cnt_i = sb("cnt_i", [P, E0], I32)
        tiles_e = sb("tiles_e", [P, E0])
        tile_end = sb("tile_end", [P, E0])
        tile_cmp = sb("tile_cmp", [P, E0])
        tile_ex = sb("tile_ex", [P, 1])
        slot_i = sb("slot_i", [P, HT * TOP0], I32)
        slot_a = sb("slot_a", [P, HT * TOP0], I32)
        hs_t = sb("hs_t", [P, 2, GW])
        hs_h = sb("hs_h", [P, 2, GW])
        gl_t = sb("gl_t", [P, GW])
        rec_a = sb("rec_a", [P, GW])
        rec_b = sb("rec_b", [P, GW])
        rows = [t[:].rearrange("p a d -> p (a d)") for t in xs] + [t[:] for t in xTs]
        eo = [zeros[:, u * GT * P:(u + 1) * GT * P] for u in range(4)]
        exT = [raw_fc[:].rearrange("p c d -> p (c d)"), raw_pr[:].rearrange("p e i -> p (e i)")]
        sg = [sb(f"sg{u}", [P, GT, I0]) for u in range(2)]
        act = [sb(f"act{u}", [P, GT, I0]) for u in range(2)]
        actT = [sb(f"actT{u}", [I0, GT * P]) for u in range(2)]
        gath = [onehot[:].rearrange("p n e -> p (n e)")[:, u * 2 * TOP0 * P:(u + 1) * 2 * TOP0 * P]
                .rearrange("p (n d) -> p n d", d=P) for u in range(2)]
        f_sb = tab_tmp
        f_th = decay_t1
        m_sb = cos_t
        x1 = [t[:].rearrange("p (a d) -> p a d", a=2) for t in (out_c, out_s)]
        xn1 = rec_b[:, 0:SEQ].rearrange("p (a d) -> p a d", a=2)
        xn1T = [decay[:, u * SEQ:(u + 1) * SEQ] for u in range(2)]
        st1 = sb("st1", [P, 2, 6])
        mv1 = sb("mv1", [P, 2, 2])
        v1 = sb("v1", [P, 2])
        r1 = sb("r1", [P, 2])
        t1 = sb("t1", [P, 2])
        qk_sb = gl_t[:].rearrange("p (a n) -> p a n", a=2)
        v_sb = past[:].rearrange("p (a d) -> p a d", a=2)
        lg1 = sb("lg1", [P, 2, E1])
        g8 = sb("g8", [P, 2, 8])
        g8_i = sb("g8_i", [P, 2, 8], U32)
        g8_f = sb("g8_f", [P, 2, 2])
        gd = sb("gd", [P, 2])
        gth = sb("gth", [P, 2])
        gw2 = sb("gw2", [P, 2, 2])
        gates = sb("gates", [P, 2, E1])
        gates2 = sb("gates2", [P, 2, E1])
        gT = sb("gT", [E1, SEQ])
        hg = hs_h[:].rearrange("p a (b n) -> p (a b) n", n=SEQ)
        mx = sb("mx", [P, 2])
        nmx = sb("nmx", [P, 2])
        den = sb("den", [P, 2])
        rden = sb("rden", [P, 2])
        pr = hs_t[:, 0, :].rearrange("p (a n) -> p a n", a=2)
        pT = hs_t[:, 1, :].rearrange("p (a n) -> p a n", a=2)
        mth = sin_t
        mg = sb("mg", [P, 2, P])
        fin = [rec_a[:, u * SEQ:(u + 1) * SEQ].rearrange("p (a d) -> p a d", a=2) for u in range(2)]

        ps = ctx.enter_context(nc.psum_tensor("ps", [P, 8, 512], F32))

        def bank(n, width=512):
            return ps[:, n, 0:width]

        x_in = sem("x_in")
        w_in = sem("w_in")
        we_in = sem("we_in")
        zero_set = sem("zero_set")
        filled = [sem(f"filled{r}") for r in range(NH)]
        ident_0 = sem("ident_0")
        pool_c = sem("pool_c")
        dve_c = sem("dve_c")
        dve_link = sem("dve_link")
        act_link = sem("act_link")
        pool_link = sem("pool_link")
        wT_ps = sem("wT_ps")
        wT_sb = sem("wT_sb")
        xn_ready = sem("xn_ready")
        xs_kept = sem("xs_kept")
        xT_ps = sem("xT_ps")
        xT_sb = sem("xT_sb")
        xT_kept = sem("xT_kept")
        lg_ps = sem("lg_ps")
        lg_sb = sem("lg_sb")
        tw_in = sem("tw_in")
        tw_exp = sem("tw_exp")
        mask_ready = sem("mask_ready")
        rank_ps = sem("rank_ps")
        ex_ready = sem("ex_ready")
        exT_row = sem("exT_row")
        routed = sem("routed")
        sent = [sem(f"sent{r}") for r in range(NH)]
        mag_ready = sem("mag_ready")
        exp_ready = sem("exp_ready")
        sh_ps = sem("sh_ps")
        sh_th = sem("sh_th")
        sh_hid = sem("sh_hid")
        sh_dn = sem("sh_dn")
        sh_done = sem("sh_done")
        rows_in = [sem(f"rows_in{u}") for u in range(4)]
        e_xT = sem("e_xT")
        e_xTs = sem("e_xTs")
        e_gu = sem("e_gu")
        e_sg = sem("e_sg")
        e_act = sem("e_act")
        e_aT = sem("e_aT")
        e_aTs = sem("e_aTs")
        e_dn = sem("e_dn")
        e_out = sem("e_out")
        e_stored = [sem(f"e_stored{u}") for u in range(4)]
        g_in = [sem(f"g_in{u}") for u in range(2)]
        c_w = sem("c_w")
        c_rt = sem("c_rt")
        c_f = sem("c_f")
        c_fth = sem("c_fth")
        c_m = sem("c_m")
        c_mT = sem("c_mT")
        c_x1 = sem("c_x1")
        c_xn = sem("c_xn")
        c_xnT = sem("c_xnT")
        c_xnTs = sem("c_xnTs")
        d_qk = sem("d_qk")
        d_v = sem("d_v")
        d_h = sem("d_h")
        d_qks = sem("d_qks")
        d_vs = sem("d_vs")
        d_hg = sem("d_hg")
        d_gd = sem("d_gd")
        d_gth = sem("d_gth")
        d_gate = sem("d_gate")
        d_gT = sem("d_gT")
        d_gTs = sem("d_gTs")
        d_gb = sem("d_gb")
        d_hs = sem("d_hs")
        d_s = sem("d_s")
        d_nmx = sem("d_nmx")
        d_p = sem("d_p")
        d_pT = sem("d_pT")
        d_pTs = sem("d_pTs")
        d_o = sem("d_o")
        d_moe = sem("d_moe")
        d_mth = sem("d_mth")
        d_fin = sem("d_fin")
        stored = [sem(f"stored{u}") for u in range(2)]

        N_W = 19
        block = ctx.enter_context(nc.Block())

        @block.sync
        def _(sp):
            for g in range(NG):
                sp.dma_start(x_tok[:, g * GT:(g + 1) * GT, :], x_rows[:, g * GT:(g + 1) * GT, :]).then_inc(x_in, 16)
            n = 0
            for dst, src in (
                (rw[:], router_w),
                (raw_g1[:], w_gate1),
                (shg[:], sh_gate),
                (shu[:], sh_up),
                (shd[:], sh_down.rearrange("(c p) h -> p c h", p=P)),
                (shgw[:], sh_gate_w),
                (phz[:, 0:2], phazor),
                (phz[:, 2:4], phazor_init),
                (phz[:, 4:5], last_re.rearrange("(d a) -> d a", a=1)),
                (phz[:, 5:6], last_im.rearrange("(d a) -> d a", a=1)),
                (raw1[:, 0, :], wq),
                (raw1[:, 1, :], wk),
                (raw1[:, 2, :], wv),
                (bqk[:, 0:1], bq.rearrange("(d a) -> d a", a=1)),
                (bqk[:, 1:2], bk.rearrange("(d a) -> d a", a=1)),
                (bv_b[:], bv.rearrange("(a d) -> a d", a=1).to_broadcast([P, P])),
                (raw_fc[:], w_fc.rearrange("(c e) i h -> (e i) c h", c=CH1)),
                (raw_pr[:], w_proj.rearrange("e h i -> h e i")),
            ):
                sp.dma_start(dst, src).then_inc(w_in, 16)
                n += 1
            assert n == N_W - 1
            sp.wait_ge(zero_set, 1)
            per = ST * P * P // P
            for r in range(NH):
                flat = slot_rows[r].rearrange("(p q) d -> p (q d)", p=P)
                for c in range(per // 2048):
                    sp.dma_start(flat[:, c * 2048:(c + 1) * 2048], zeros[:]).then_inc(filled[r], 16)
                if r == 0:
                    sp.dma_start(w_gu[:, :, 0:I0], w_gate.rearrange("e h i -> h e i")).then_inc(we_in, 16)
                    sp.dma_start(w_gu[:, :, I0:2 * I0], w_up.rearrange("e h i -> h e i")).then_inc(we_in, 16)
                    sp.dma_start(w_dn[:].rearrange("i (e h) -> i e h", e=E0),
                                 w_down.rearrange("e i h -> i e h")).then_inc(we_in, 16)

            def store(r, it, slot):
                sp.wait_ge(e_out, r * SG + it + 1)
                sp.dma_start(expert_groups[r][bass.ds(it, 1), :, :].rearrange("a p n -> (a p) n"),
                             eo[slot]).then_inc(e_stored[slot], 16)

            def load(r, it, slot):
                if not (isinstance(it, int) and it < 4 and r == 0):
                    sp.wait_ge(e_xT, r * SG + it - 4 + 1)
                sp.dma_start(rows[slot], slot_groups[r][bass.ds(it, 1), :, :]
                             .rearrange("a p n -> (a p) n")).then_inc(rows_in[slot], 16)

            for r in range(NH):
                sp.wait_ge(sent[r], 16 * HT * TOP0)
                for s in range(4):
                    load(r, s, s)
                    if r:
                        store(r - 1, SG - 4 + s, s)
                with sp.Fori(1, SG // 4) as i:
                    for s in range(4):
                        load(r, i * 4 + s, s)
                        store(r, (i - 1) * 4 + s, s)
            for s in range(4):
                store(NH - 1, SG - 4 + s, s)

            def store_out(it, slot, first):
                sp.wait_ge(d_fin, it + 1)
                sp.dma_start(out_rows[bass.ds(it, 1), :, :, :].rearrange("a p t d -> (a p) t d"),
                             fin[slot]).then_inc(stored[slot], 16)
            rounds(sp, NSEQ, 2, store_out)
            for s in range(2):
                sp.wait_ge(stored[s], 16 * NSEQ // 2)

        @block.gpsimd
        def _(pool):
            chain = Chain(pool, pool_link)
            g = nc.gpsimd
            chain.link(g.memset(ident[:], 0.0))
            g.affine_select(out=ident[:], in_=ident[:], compare_op=ALU.not_equal, fill=1.0, base=0,
                            pattern=[[-1, P]], channel_multiplier=1).then_inc(pool_c, 1)
            chain.link(g.memset(before[:], 1.0))
            g.affine_select(out=before[:], in_=before[:], compare_op=ALU.is_gt, fill=0.0, base=0,
                            pattern=[[1, P]], channel_multiplier=-1).then_inc(pool_c, 1)
            g.iota(iota_e[:], [[1, E0]], base=0, channel_multiplier=0,
                   allow_small_or_imprecise_dtypes=True).then_inc(pool_c, 1)
            g.iota(iota_t1[:], [[1, SEQ]], base=1, channel_multiplier=0,
                   allow_small_or_imprecise_dtypes=True).then_inc(pool_c, 1)
            g.iota(iota_p[:], [[1, 1]], base=0, channel_multiplier=1,
                   allow_small_or_imprecise_dtypes=True).then_inc(pool_c, 1)
            chain.link(g.memset(expert_sel[:], 1.0))
            chain.link(g.affine_select(out=expert_sel[:], in_=expert_sel[:], compare_op=ALU.is_ge, fill=0.0,
                                       base=0, pattern=[[P, CH1], [1, P]], channel_multiplier=-I1))
            g.affine_select(out=expert_sel[:], in_=expert_sel[:], compare_op=ALU.is_ge, fill=0.0,
                            base=I1 - 1, pattern=[[-P, CH1], [-1, P]], channel_multiplier=I1).then_inc(pool_c, 1)

            def keep(it, slot, first):
                pool.wait_ge(xn_ready, it + 1)
                g.tensor_copy(xn_tok[:, bass.ds(it * GT, GT), :], xs[slot][:]).then_inc(xs_kept, 1)
                pool.wait_ge(xT_sb, it + 1)
                g.tensor_copy(xnT[:, bass.ds(it * GW, GW)], xTs[slot][:]).then_inc(xT_kept, 1)
            rounds(pool, NG, 2, keep)
            pool.wait_ge(xs_kept, NG)
            pool.wait_ge(xT_kept, NG)

            for r in range(NH):
                pool.wait_ge(routed, r + 1)
                pool.wait_ge(filled[r], 16 * (ST * P // 2048))
                for t in range(HT):
                    for k in range(TOP0):
                        n = (r * HT + t) * TOP0 + k
                        g.indirect_dma_start(
                            out=slot_rows[r], out_offset=bass.IndirectOffsetOnAxis(ap=slot_of[:, n:n + 1], axis=0),
                            in_=xn_tok[:, r * HT + t, :], in_offset=None).then_inc(sent[r], 16)

            for b in range(NSEQ):
                r = b // (NSEQ // NH)
                if b % (NSEQ // NH) == 0:
                    for u in range(4):
                        pool.wait_ge(e_stored[u], 16 * (r + 1) * SG // 4)
                if b >= 2:
                    pool.wait_ge(c_rt, b - 1)
                for j in range(2 * TOP0):
                    n = b * 2 * TOP0 + j
                    g.indirect_dma_start(
                        out=gath[b % 2][:, j, :], out_offset=None, in_=expert_rows[r],
                        in_offset=bass.IndirectOffsetOnAxis(ap=slot_of[:, n:n + 1], axis=0)).then_inc(g_in[b % 2], 16)

        @block.tensor
        def _(pe):
            pe.wait_ge(pool_c, 1)
            pe.wait_ge(w_in, 16 * (N_W - 1))
            for j in range(3):
                last = pe.transpose(ps[:, 7, j * P:(j + 1) * P], raw1[:, j, :], ident[:])
            last.then_inc(wT_ps, 1)
            for j in range(CH1):
                last = pe.transpose(ps[:, 6, j * P:(j + 1) * P], raw_fc[:, j, :], ident[:])
            last.then_inc(wT_ps, 1)
            for j in range(CH1):
                last = pe.transpose(ps[:, 5, j * P:(j + 1) * P],
                                    raw_pr[:].rearrange("h e i -> h (e i)")[:, j * P:(j + 1) * P], ident[:])
            last.then_inc(wT_ps, 1)
            pe.transpose(ps[:, 4, 0:E1], raw_g1[:], ident[0:E1, 0:E1]).then_inc(wT_ps, 1)

            def stage_a(it, slot, first):
                pe.wait_ge(xn_ready, it + 1)
                lagged(pe, xT_sb, it, slot, first, 2)
                for j in range(GT):
                    mm = pe.transpose(ps[:, slot, j * P:(j + 1) * P], xs[slot][:, j, :], ident[:])
                mm.then_inc(xT_ps, 1)
                pe.wait_ge(xT_sb, it + 1)
                lagged(pe, lg_sb, it, slot, first, 2)
                for j in range(GT):
                    mm = pe.matmul(ps[:, 2 + slot, j * E0:(j + 1) * E0], xTs[slot][:, j * P:(j + 1) * P], rw[:],
                                   start=True, stop=True)
                mm.then_inc(lg_ps, 1)
            rounds(pe, NG, 2, stage_a)

            pe.wait_ge(wT_sb, 4)
            pe.wait_ge(pool_c, 6)
            pe.wait_ge(dve_c, 1)
            for r in range(NH):
                pe.wait_ge(mask_ready, r + 1)
                if r:
                    pe.wait_ge(routed, r)
                pe.matmul(bank(4), before[:], mask[:].rearrange("p t e -> p (t e)"), start=True, stop=True)
                pe.matmul(bank(5), ones_bf[:], mask[:].rearrange("p t e -> p (t e)"),
                          start=True, stop=True).then_inc(rank_ps, 1)
                pe.wait_ge(ex_ready, r + 1)
                pe.transpose(ps[0:1, 6, 0:ST], tile_ex[0:ST, :], ident[0:ST, 0:ST]).then_inc(exT_row, 1)

            pe.wait_ge(lg_sb, NG)
            pe.wait_ge(xT_kept, NG)
            pe.wait_ge(routed, NH)

            def stage_s(it, slot, first):
                lagged(pe, sh_hid, it, slot, first, 1)
                for c in range(2):
                    pe.matmul(bank(c), shg[:, c * P:(c + 1) * P], xnT[:, bass.ds(it * GW, GW)],
                              start=True, stop=True)
                for c in range(2):
                    pe.matmul(bank(2 + c), shu[:, c * P:(c + 1) * P], xnT[:, bass.ds(it * GW, GW)],
                              start=True, stop=True)
                lagged(pe, sh_done, it, slot, first, 1)
                pe.matmul(bank(4), shgw_b[:], xnT[:, bass.ds(it * GW, GW)], start=True, stop=True).then_inc(sh_ps, 1)
                pe.wait_ge(sh_hid, it + 1)
                for c in range(2):
                    mm = pe.matmul(bank(5), shd[:, c, :], hs_h[:, c, :], start=(c == 0), stop=(c == 1))
                mm.then_inc(sh_dn, 1)
            rounds(pe, NG, 1, stage_s)

            pe.wait_ge(sh_done, NG)
            pe.wait_ge(we_in, 48)
            pe.wait_ge(routed, NH)

            def ids(at):
                _, v = nc.values_load_multi_w_load_instructions(
                    tile_expert[0:1, bass.ds(at, GT)], engines=[mybir.EngineType.PE], min_val=0, max_val=E0 - 1,
                    skip_runtime_bounds_check_because="VectorE clamps the ids to E0 - 1")
                return v

            N = NH * SG

            def rows_T(n, slot, fills, first):
                pe.wait_ge(rows_in[slot], fills * 16)
                if not first:
                    pe.wait_ge(e_xTs, n)
                for j in range(GT):
                    mm = pe.transpose(ps[:, 0, j * P:(j + 1) * P], rows[slot][:, j * P:(j + 1) * P], ident[:])
                mm.then_inc(e_xT, 1)

            def act_T(n, u, first):
                pe.wait_ge(e_act, n + 1)
                if not first:
                    pe.wait_ge(e_aTs, n)
                for j in range(GT):
                    mm = pe.transpose(ps[0:I0, 5, j * P:(j + 1) * P], act[u][:, j, :], ident[:])
                mm.then_inc(e_aT, 1)

            def down(n, u, first):
                e = ids(n * GT)
                pe.wait_ge(e_aTs, n + 1)
                if not first:
                    pe.wait_ge(e_out, n)
                for j in range(GT):
                    mm = pe.matmul(ps[:, 6, j * P:(j + 1) * P], actT[u][:, j * P:(j + 1) * P],
                                   w_dn[:, bass.ds(e[j] * P, P)], start=True, stop=True)
                mm.then_inc(e_dn, 1)

            def gate_up(n, u, first):
                e = ids(n * GT)
                pe.wait_ge(e_xTs, n + 1)
                if not first:
                    pe.wait_ge(e_act, n - 1)
                for j in range(GT):
                    mm = pe.matmul(ps[:, 1 + 2 * u + j // 2, (j % 2) * 256:(j % 2) * 256 + 2 * I0],
                                   exT[u][:, j * P:(j + 1) * P],
                                   w_gu[:, bass.ds(e[j], 1), :].rearrange("p a n -> p (a n)"),
                                   start=True, stop=True)
                mm.then_inc(e_gu, 1)

            def stage_e(n, slot, rnd, first):
                gate_up(n, slot % 2, first and slot < 2)
                if not first or slot > 0:
                    act_T(n - 1, (slot + 1) % 2, first and slot == 1)
                if not isinstance(n, int) or n + 1 < N:
                    rows_T(n + 1, (slot + 1) % 4, rnd + (2 if slot == 3 else 1), False)
                if not first or slot > 0:
                    down(n - 1, (slot + 1) % 2, first and slot == 1)

            rows_T(0, 0, 1, True)
            for s in range(4):
                stage_e(s, s, 0, True)
            with pe.Fori(1, N // 4 - 1) as i:
                for s in range(4):
                    stage_e(i * 4 + s, s, i, False)
            for s in range(4):
                stage_e(N - 4 + s, s, N // 4 - 1, False)
            act_T(N - 1, 1, False)
            down(N - 1, 1, False)

            def routed_sum(b, u):
                pe.wait_ge(c_w, b + 1)
                for j in range(2):
                    for k in range(TOP0):
                        mm = pe.matmul(ps[:, 0, j * P:(j + 1) * P], gath[u][:, j * TOP0 + k, :], ident[:],
                                       start=(k == 0), stop=(k == TOP0 - 1))
                mm.then_inc(c_rt, 1)

            def turn_m(b):
                pe.wait_ge(c_m, b + 1)
                for j in range(2):
                    mm = pe.transpose(ps[:, 7, j * P:(j + 1) * P], m_sb[:, j * P:(j + 1) * P], ident[:])
                mm.then_inc(c_mT, 1)

            def turn_xn(b):
                pe.wait_ge(c_xn, b + 1)
                for j in range(2):
                    mm = pe.transpose(ps[:, 7, 256 + j * P:256 + (j + 1) * P], xn1[:, j, :], ident[:])
                mm.then_inc(c_xnT, 1)

            routed_sum(0, 0)
            turn_m(0)
            turn_xn(0)

            def stage_c(b, u, first, more=True):
                pe.wait_ge(c_xnTs, b + 1)
                lagged(pe, d_pTs, b, u, first, 1)
                for j in range(2):
                    mm = pe.matmul(ps[:, 2, j * SEQ:(j + 1) * SEQ], w1T[:, j, :], xn1T[u], start=True, stop=True)
                mm.then_inc(d_qk, 1)
                lagged(pe, d_hs, b, u, first, 1)
                for j in range(2):
                    pe.matmul(ps[:, 1, j * P:(j + 1) * P], xn1T[u][:, j * P:(j + 1) * P], w1T[:, 2, :],
                              start=True, stop=True)
                for j in range(2):
                    mm = pe.matmul(ps[:, 1, 256 + j * E1:256 + (j + 1) * E1], xn1T[u][:, j * P:(j + 1) * P], g1T[:],
                                   start=True, stop=True)
                mm.then_inc(d_v, 1)
                lagged(pe, d_hg, b, u, first, 1)
                for c in range(CH1):
                    mm = pe.matmul(ps[:, 4 + c // 2, (c % 2) * SEQ:(c % 2 + 1) * SEQ], fcT[:, c, :], xn1T[u],
                                   start=True, stop=True)
                mm.then_inc(d_h, 1)
                pe.wait_ge(d_qks, b + 1)
                lagged(pe, d_fin, b, u, first, 1)
                for j in range(2):
                    mm = pe.matmul(ps[:, 6, j * SEQ:(j + 1) * SEQ], qk_sb[:, 0, j * P:(j + 1) * P], qk_sb[:, 1, :],
                                   start=True, stop=True)
                mm.then_inc(d_s, 1)
                if more:
                    routed_sum(b + 1, 1 - u)
                pe.wait_ge(d_gate, b + 1)
                for j in range(2):
                    mm = pe.transpose(ps[0:E1, 3, j * P:(j + 1) * P], gates[:, j, :], ident[:])
                mm.then_inc(d_gT, 1)
                pe.wait_ge(d_p, b + 1)
                for k in range(2):
                    for j in range(2):
                        mm = pe.transpose(ps[:, 2, k * SEQ + j * P:k * SEQ + (j + 1) * P],
                                          pr[:, j, k * P:(k + 1) * P], ident[:])
                mm.then_inc(d_pT, 1)
                if more:
                    turn_m(b + 1)
                pe.wait_ge(d_gTs, b + 1)
                pe.wait_ge(d_vs, b + 1)
                if more:
                    pe.wait_ge(c_f, b + 2)
                for c in range(CH1):
                    mm = pe.matmul(ps[:, c // 2, (c % 2) * SEQ:(c % 2 + 1) * SEQ], expert_sel[:, c, :], gT[:],
                                   start=True, stop=True)
                mm.then_inc(d_gb, 1)
                pe.wait_ge(d_pTs, b + 1)
                for j in range(2):
                    for k in range(2):
                        mm = pe.matmul(ps[:, 6, j * P:(j + 1) * P], pT[:, k, j * P:(j + 1) * P], v_sb[:, k, :],
                                       start=(k == 0), stop=(k == 1))
                mm.then_inc(d_o, 1)
                pe.wait_ge(d_hs, b + 1)
                for j in range(2):
                    for c in range(CH1):
                        mm = pe.matmul(ps[:, 3, j * P:(j + 1) * P], hg[:, c, j * P:(j + 1) * P], prT[:, c, :],
                                       start=(c == 0), stop=(c == CH1 - 1))
                mm.then_inc(d_moe, 1)
                if more:
                    turn_xn(b + 1)
            rounds(pe, NSEQ - 2, 2, stage_c)
            stage_c(NSEQ - 2, 0, False)
            stage_c(NSEQ - 1, 1, False, more=False)

        @block.scalar
        def _(sc):
            a = nc.scalar
            chain = Chain(sc, act_link)
            sc.wait_ge(wT_ps, 4)
            a.copy(w1T[:].rearrange("p a b -> p (a b)"), bank(7, 384)).then_inc(wT_sb, 1)
            a.copy(fcT[:].rearrange("p a b -> p (a b)"), bank(6)).then_inc(wT_sb, 1)
            a.copy(prT[:].rearrange("p a b -> p (a b)"), bank(5)).then_inc(wT_sb, 1)
            a.copy(g1T[:], bank(4, E1)).then_inc(wT_sb, 1)

            def stage_a(it, slot, first):
                sc.wait_ge(xT_ps, it + 1)
                lagged(sc, lg_ps, it, slot, first, 2)
                lagged(sc, xT_kept, it, slot, first, 2)
                a.copy(xTs[slot][:], bank(slot)).then_inc(xT_sb, 1)
                sc.wait_ge(lg_ps, it + 1)
                a.copy(logits[:, bass.ds(it * GT, GT), :].rearrange("p t e -> p (t e)"),
                       bank(2 + slot, GT * E0)).then_inc(lg_sb, 1)
            rounds(sc, NG, 2, stage_a)

            for r in range(NH):
                sc.wait_ge(tw_in, r + 1)
                a.activation(tw[:], tw[:], ACT.Exp).then_inc(tw_exp, 1)

            sc.wait_ge(mag_ready, 1)
            sc.wait_ge(pool_c, 6)
            a.activation(cs[:, 4:5], cs[:, 3:4], ACT.Exp).then_inc(exp_ready, 1)
            a.activation(decay_t1[:], iota_t1[:], ACT.Exp, scale=cs[:, 3:4]).then_inc(exp_ready, 1)

            def stage_s(it, slot, first):
                sc.wait_ge(sh_ps, it + 1)
                lagged(sc, sh_done, it, slot, first, 1)
                a.activation(hs_t[:], ps[:, 0:2, :], ACT.Tanh, scale=0.5)
                a.activation(gl_t[:], bank(4), ACT.Tanh, scale=0.5).then_inc(sh_th, 1)
            rounds(sc, NG, 1, stage_s)

            def copy_xT(n, u):
                sc.wait_ge(e_xT, n + 1)
                if not (isinstance(n, int) and n < 2):
                    sc.wait_ge(e_gu, n - 1)
                a.copy(exT[u], bank(0)).then_inc(e_xTs, 1)

            def silu_gate(n, u):
                sc.wait_ge(e_gu, n + 1)
                if not (isinstance(n, int) and n < 2):
                    sc.wait_ge(e_act, n - 1)
                a.activation(sg[u][:].rearrange("p (a b) i -> p a b i", a=2),
                             ps[:, 1 + 2 * u:3 + 2 * u, :].rearrange("p a (b i) -> p a b i", b=2)[:, :, :, 0:I0],
                             ACT.Silu).then_inc(e_sg, 1)

            def copy_out(n, slot4, first):
                sc.wait_ge(e_dn, n + 1)
                if not first:
                    sc.wait_ge(e_stored[slot4], stored_before[0] * 16)
                a.copy(eo[slot4], bank(6)).then_inc(e_out, 1)

            stored_before = [None]
            for r in range(NH):
                sc.wait_ge(filled[r], 16 * (ST * P // 2048))
            copy_xT(0, 0)

            def stage_e(n, slot, first):
                if not first or slot > 0:
                    prev = (slot + 3) % 4
                    stored_before[0] = round_[0] - 1 if slot == 0 else round_[0]
                    copy_out_first = first or (slot == 0 and second[0])
                    silu_gate(n, slot % 2)
                    copy_xT(n + 1, (slot + 1) % 2)
                    copy_out(n - 1, prev, copy_out_first)
                else:
                    silu_gate(n, slot % 2)
                    copy_xT(n + 1, (slot + 1) % 2)
            round_, second = [0], [False]
            N = NH * SG
            for s in range(4):
                stage_e(s, s, True)
            round_, second = [1], [True]
            for s in range(4):
                stage_e(4 + s, s, False)
            second = [False]
            with sc.Fori(2, N // 4 - 1) as i:
                round_[0] = i
                for s in range(4):
                    stage_e(i * 4 + s, s, False)
            round_ = [N // 4 - 1]
            for s in range(3):
                stage_e(N - 4 + s, s, False)
            silu_gate(N - 1, 1)
            stored_before[0] = N // 4 - 1
            copy_out(N - 2, 2, False)
            copy_out(N - 1, 3, False)

            def tanh_f(b):
                sc.wait_ge(c_f, b + 1)
                a.activation(f_th[:], f_sb[:], ACT.Tanh, scale=0.5).then_inc(c_fth, 1)

            def copy_xn(b, u):
                sc.wait_ge(c_xnT, b + 1)
                if not (isinstance(b, int) and b < 2):
                    sc.wait_ge(d_h, b - 1)
                a.copy(xn1T[u], ps[:, 7, 256:512]).then_inc(c_xnTs, 1)
            tanh_f(0)
            copy_xn(0, 0)

            def stage_c(b, u, first, more=True):
                sc.wait_ge(d_qk, b + 1)
                lagged(sc, d_s, b, u, first, 1)
                for j in range(2):
                    last = a.activation(qk_sb[:, j, :], ps[:, 2, j * SEQ:(j + 1) * SEQ], ACT.Identity,
                                        bias=bqk[:, j:j + 1])
                last.then_inc(d_qks, 1)
                sc.wait_ge(d_h, b + 1)
                lagged(sc, d_moe, b, u, first, 1)
                a.activation(hg, ps[:, 4:6, :].rearrange("p a (b n) -> p (a b) n", b=2), ACT.Gelu).then_inc(d_hg, 1)
                sc.wait_ge(d_gd, b + 1)
                a.activation(gth[:], gd[:], ACT.Tanh, scale=0.5).then_inc(d_gth, 1)
                if more:
                    tanh_f(b + 1)
                sc.wait_ge(d_nmx, b + 1)
                lagged(sc, d_pT, b, u, first, 1)
                for j in range(2):
                    last = a.activation(pr[:, j, :], ps[:, 6, j * SEQ:(j + 1) * SEQ], ACT.Exp,
                                        bias=nmx[:, j:j + 1], scale=SCALE, accum_out=den[:, j:j + 1])
                last.then_inc(d_p, 1)
                sc.wait_ge(d_pT, b + 1)
                lagged(sc, d_o, b, u, first, 1)
                a.copy(hs_t[:, 1, :], bank(2)).then_inc(d_pTs, 1)
                sc.wait_ge(d_moe, b + 1)
                lagged(sc, d_fin, b, u, first, 1)
                a.activation(mth[:], bank(3, SEQ), ACT.Tanh, scale=0.5).then_inc(d_mth, 1)
                if more:
                    copy_xn(b + 1, 1 - u)
            rounds(sc, NSEQ - 2, 2, stage_c)
            stage_c(NSEQ - 2, 0, False)
            stage_c(NSEQ - 1, 1, False, more=False)

        @block.vector
        def _(dve):
            v = nc.vector
            chain = Chain(dve, dve_link)
            link = chain.link
            v.memset(zeros[:], 0.0).then_inc(zero_set, 1)
            v.memset(ones_bf[:], 1.0)
            v.memset(ones[:], 1.0)
            link(v.memset(not_first[:], 1.0))
            link(v.memset(not_first[:, :, 0:1], 0.0))
            dve.wait_ge(w_in, 16 * (N_W - 1))
            v.tensor_scalar(shgw_b[:], ones[:], shgw[:, 0:1], None, ALU.mult).then_inc(dve_c, 1)
            dve.wait_ge(x_in, 16 * NG)

            with dve.Fori(0, NG) as i:
                for j in range(GT):
                    v.bn_stats(stats[:, bass.ds(i * GT + j, 1), :].rearrange("p a s -> p (a s)"),
                               x_tok[:, bass.ds(i * GT + j, 1), :].rearrange("p a d -> p (a d)"))
            link(v.memset(rtmp[:], 0.0))
            link(v.tensor_tensor(mean[:], stats[:, :, 1], stats[:, :, 4], ALU.add))
            link(v.tensor_scalar(mean[:], mean[:], 0.5, None, ALU.mult))
            link(v.tensor_tensor(rtmp[:], stats[:, :, 1], stats[:, :, 4], ALU.subtract))
            link(v.tensor_tensor(rtmp[:], rtmp[:], rtmp[:], ALU.mult))
            link(v.tensor_scalar(rtmp[:], rtmp[:], 0.25, EPS, ALU.mult, ALU.add))
            link(v.tensor_tensor(var[:], stats[:, :, 2], stats[:, :, 5], ALU.add))
            link(v.scalar_tensor_tensor(out=var[:], in0=var[:], scalar=1.0 / P, in1=rtmp[:], op0=ALU.mult, op1=ALU.add))
            rsqrt_steps(nc, link, rstd[:], var[:], rtmp[:])

            def stage_a(it, slot, first):
                lagged(dve, xs_kept, it, slot, first, 2)
                lagged(dve, xT_ps, it, slot, first, 2)
                for j in range(GT):
                    last = v.tensor_scalar(xs[slot][:, j, :],
                                           x_tok[:, bass.ds(it * GT + j, 1), :].rearrange("p a d -> p (a d)"),
                                           mean[:, bass.ds(it * GT + j, 1)], rstd[:, bass.ds(it * GT + j, 1)],
                                           ALU.subtract, ALU.mult)
                last.then_inc(xn_ready, 1)
            rounds(dve, NG, 2, stage_a)

            dve.wait_ge(pool_c, 6)
            for r in range(NH):
                T0 = r * HT
                dve.wait_ge(lg_sb, (r + 1) * NG // NH)
                for t in range(HT):
                    v.max(top8[:, t, :], logits[:, T0 + t, :])
                link(v.memset(tsum[:], 0.0))
                for t in range(HT):
                    last = v.max_index(top8_i[:, t, :], top8[:, t, :], logits[:, T0 + t, :])
                link(last)
                v.tensor_tensor(tw[:], top8[:, :, 0:TOP0], top8[:, :, 0:1].to_broadcast([P, HT, TOP0]),
                                ALU.subtract).then_inc(tw_in, 1)
                link(v.tensor_copy(top_f[:].rearrange("p (t k) -> p t k", k=TOP0), top8_i[:, :, 0:TOP0]))
                link(v.tensor_tensor(onehot[:], iota_e[:].rearrange("p (a e) -> p a e", a=1).to_broadcast([P, HT * TOP0, E0]),
                                     top_f[:].rearrange("p (t a) -> p t a", a=1).to_broadcast([P, HT * TOP0, E0]),
                                     ALU.is_equal))
                with nc.allow_low_precision("sums of one 1 and zeros"):
                    v.tensor_reduce(mask[:], onehot[:].rearrange("p (t k) e -> p t e k", k=TOP0), AX.X,
                                    ALU.add).then_inc(mask_ready, 1)
                dve.wait_ge(tw_exp, r + 1)
                link(v.tensor_reduce(tsum[:], tw[:], AX.X, ALU.add))
                link(v.reciprocal(tsum[:], tsum[:]))
                v.tensor_tensor(top_w[:, T0 * TOP0:(T0 + HT) * TOP0].rearrange("p (t k) -> p t k", k=TOP0), tw[:],
                                tsum[:].rearrange("p (t a) -> p t a", a=1).to_broadcast([P, HT, TOP0]), ALU.mult)
                dve.wait_ge(rank_ps, r + 1)
                link(v.tensor_copy(tot_em[:], bank(5).rearrange("p (t e) -> p e t", t=HT)))
                link(v.tensor_tensor_scan(cum_em[:].rearrange("p e t -> p (e t)"), not_first[:].rearrange("p e t -> p (e t)"),
                                          tot_em[:].rearrange("p e t -> p (e t)"), 0.0, ALU.mult, ALU.add))
                link(v.tensor_scalar(cnt_i[:], cum_em[:, :, HT - 1], float(P - 1), None, ALU.add))
                link(v.tensor_scalar(cnt_i[:], cnt_i[:], 7, None, ALU.logical_shift_right))
                link(v.tensor_copy(tiles_e[:], cnt_i[:]))
                link(v.tensor_tensor_scan(tile_end[:], ones[:, 0:E0], tiles_e[:], 0.0, ALU.mult, ALU.add))
                link(v.tensor_scalar(tile_cmp[0:ST, :], tile_end[0:ST, :], iota_p[0:ST, 0:1], None, ALU.is_le))
                link(v.tensor_reduce(tile_ex[0:ST, :], tile_cmp[0:ST, :], AX.X, ALU.add))
                v.tensor_scalar(tile_ex[0:ST, :], tile_ex[0:ST, :], float(E0 - 1), None, ALU.min).then_inc(ex_ready, 1)
                link(v.tensor_tensor(tiles_e[:], tile_end[:], tiles_e[:], ALU.subtract))
                link(v.tensor_scalar(tiles_e[:], tiles_e[:], float(P), None, ALU.mult))
                link(v.tensor_tensor(cum_em[:], cum_em[:], tot_em[:], ALU.subtract))
                link(v.tensor_tensor(cum_em[:], cum_em[:],
                                     tiles_e[:].rearrange("p (e a) -> p e a", a=1).to_broadcast([P, E0, HT]), ALU.add))
                link(v.tensor_tensor(pos[:], bank(4).rearrange("p (t e) -> p t e", t=HT),
                                     cum_em[:].rearrange("p e t -> p t e"), ALU.add))
                oh4 = onehot[:].rearrange("p (t k) e -> p t k e", k=TOP0)
                for k in range(TOP0):
                    last = v.tensor_tensor(oh4[:, :, k, :], oh4[:, :, k, :], pos[:], ALU.mult)
                link(last)
                link(v.tensor_reduce(top_f[:], onehot[:], AX.X, ALU.add))
                sl = slot_of[:, T0 * TOP0:(T0 + HT) * TOP0]
                link(v.tensor_copy(slot_i[:], top_f[:]))
                link(v.tensor_scalar(sl, slot_i[:], 9, 9, ALU.logical_shift_right, ALU.logical_shift_left))
                link(v.tensor_scalar(slot_a[:], slot_i[:], P - 1, 2, ALU.bitwise_and, ALU.logical_shift_left))
                link(v.tensor_tensor(sl, sl, slot_a[:], ALU.add))
                link(v.tensor_scalar(slot_a[:], slot_i[:], 7, GT - 1, ALU.logical_shift_right, ALU.bitwise_and))
                link(v.tensor_tensor(sl, sl, slot_a[:], ALU.add))
                dve.wait_ge(exT_row, r + 1)
                v.tensor_copy(tile_expert[:, r * ST:(r + 1) * ST], ps[0:1, 6, 0:ST]).then_inc(routed, 1)

            def col(n):
                return cs[:, n:n + 1]

            def cmul(re, im, ar, ai, br, bi, tmp):
                link(v.tensor_tensor(tmp, ai, bi, ALU.mult))
                link(v.scalar_tensor_tensor(out=re, in0=ar, scalar=br, in1=tmp, op0=ALU.mult, op1=ALU.subtract))
                link(v.tensor_tensor(tmp, ai, br, ALU.mult))
                link(v.scalar_tensor_tensor(out=im, in0=ar, scalar=bi, in1=tmp, op0=ALU.mult, op1=ALU.add))

            link(v.tensor_tensor(col(9), phz[:, 1:2], phz[:, 1:2], ALU.mult))
            link(v.scalar_tensor_tensor(out=col(0), in0=phz[:, 0:1], scalar=phz[:, 0:1], in1=col(9),
                                        op0=ALU.mult, op1=ALU.add))
            rsqrt_steps(nc, link, col(12), col(0), col(9))
            link(v.tensor_tensor(col(1), phz[:, 0:1], col(12), ALU.mult))
            link(v.tensor_tensor(col(2), phz[:, 1:2], col(12), ALU.mult))
            link(v.tensor_tensor(col(3), col(0), col(12), ALU.mult))
            link(v.tensor_scalar(col(3), col(3), -1.0, None, ALU.mult))
            v.memset(cos_t[:, 0:1], 1.0).then_inc(mag_ready, 1)
            link(v.memset(sin_t[:, 0:1], 0.0))
            link(v.tensor_copy(cs[:, 5:7], cs[:, 1:3]))
            n = 1
            while n < SEQ:
                link(v.tensor_scalar(tab_tmp[:, 0:n], sin_t[:, 0:n], col(6), None, ALU.mult))
                link(v.scalar_tensor_tensor(out=cos_t[:, n:2 * n], in0=cos_t[:, 0:n], scalar=col(5),
                                            in1=tab_tmp[:, 0:n], op0=ALU.mult, op1=ALU.subtract))
                link(v.tensor_scalar(tab_tmp[:, 0:n], sin_t[:, 0:n], col(5), None, ALU.mult))
                link(v.scalar_tensor_tensor(out=sin_t[:, n:2 * n], in0=cos_t[:, 0:n], scalar=col(6),
                                            in1=tab_tmp[:, 0:n], op0=ALU.mult, op1=ALU.add))
                cmul(col(7), col(8), col(5), col(6), col(5), col(6), col(9))
                link(v.tensor_copy(cs[:, 5:7], cs[:, 7:9]))
                n *= 2

            def ctab(dst, table_a, a, table_b, b, op):
                link(v.tensor_scalar(tab_tmp[:], table_b, b, None, ALU.mult))
                link(v.scalar_tensor_tensor(out=dst, in0=table_a, scalar=a, in1=tab_tmp[:], op0=ALU.mult, op1=op))
            ctab(out_c[:], cos_t[:], phz[:, 2:3], sin_t[:], phz[:, 3:4], ALU.subtract)
            ctab(out_s[:], sin_t[:], phz[:, 2:3], cos_t[:], phz[:, 3:4], ALU.add)
            cmul(col(10), col(11), phz[:, 4:5], phz[:, 5:6], col(1), col(2), col(9))
            ctab(past[:], cos_t[:], col(10), sin_t[:], col(11), ALU.subtract)
            dve.wait_ge(exp_ready, 2)
            link(v.tensor_tensor(past[:], past[:], decay_t1[:], ALU.mult))
            link(v.memset(decay[:], 1.0))
            link(v.tensor_scalar(decay[:], decay[:], col(4), None, ALU.mult))
            link(v.memset(decay[:].rearrange("p (b t) -> p b t", t=SEQ)[:, :, 0:1], 0.0))

            def both(table):
                return table[:].rearrange("p (a t) -> p a t", a=1).to_broadcast([P, GW // SEQ, SEQ])

            def view(buf):
                return buf.rearrange("p (a t) -> p a t", t=SEQ)

            def stage_s(it, slot, first):
                dve.wait_ge(sh_th, it + 1)
                lagged(dve, sh_dn, it, slot, first, 1)
                link(v.scalar_tensor_tensor(out=hs_h[:], in0=hs_t[:], scalar=1.0, in1=ps[:, 0:2, :],
                                            op0=ALU.add, op1=ALU.mult))
                v.tensor_tensor(hs_h[:], hs_h[:], ps[:, 2:4, :], ALU.mult).then_inc(sh_hid, 1)
                xg = xnT[:, bass.ds(it * GW, GW)]
                v.tensor_tensor(view(rec_a[:]), view(xg), both(cos_t), ALU.mult)
                link(v.tensor_tensor(view(rec_b[:]), view(xg), both(sin_t), ALU.mult))
                dve.wait_ge(sh_dn, it + 1)
                v.scalar_tensor_tensor(out=shT[:, bass.ds(it * GW, GW)], in0=gl_t[:], scalar=1.0, in1=bank(5),
                                       op0=ALU.add, op1=ALU.mult).then_inc(sh_done, 1)
                v.tensor_tensor_scan(rec_a[:], decay[:], rec_a[:], 0.0, ALU.mult, ALU.add)
                link(v.tensor_tensor_scan(rec_b[:], decay[:], rec_b[:], 0.0, ALU.mult, ALU.add))
                v.tensor_tensor(view(rec_a[:]), view(rec_a[:]), both(out_c), ALU.mult)
                link(v.tensor_tensor(view(rec_b[:]), view(rec_b[:]), both(out_s), ALU.mult))
                link(v.tensor_tensor(rec_a[:], rec_a[:], rec_b[:], ALU.add))
                link(v.tensor_tensor(view(xg), view(rec_a[:]), both(past), ALU.add))
            rounds(dve, NG, 1, stage_s, (chain,))

            def hidden(n, u):
                dve.wait_ge(e_sg, n + 1)
                if not (isinstance(n, int) and n < 2):
                    dve.wait_ge(e_aT, n - 1)
                v.tensor_tensor(act[u][:].rearrange("p (a b) i -> p a b i", a=2),
                                sg[u][:].rearrange("p (a b) i -> p a b i", a=2),
                                ps[:, 1 + 2 * u:3 + 2 * u, :].rearrange("p a (b i) -> p a b i", b=2)[:, :, :, I0:2 * I0],
                                ALU.mult).then_inc(e_act, 1)

            def copy_aT(n, u):
                dve.wait_ge(e_aT, n + 1)
                if not (isinstance(n, int) and n < 2):
                    dve.wait_ge(e_dn, n - 1)
                v.tensor_copy(actT[u][:], ps[0:I0, 5, :]).then_inc(e_aTs, 1)

            N = NH * SG
            hidden(0, 0)
            hidden(1, 1)
            copy_aT(0, 0)
            with dve.Fori(1, N // 2) as i:
                for s in range(2):
                    hidden(i * 2 + s, s)
                    copy_aT(i * 2 + s - 1, 1 - s)
            copy_aT(N - 1, 1)

            def take_wait():
                v.memset(rtmp[:, 1:2], 0.0)

            def weight_rows(b, u):
                dve.wait_ge(g_in[u], 16 * 2 * TOP0 * (half_b[0] + 1))
                v.tensor_tensor(gath[u], gath[u],
                                top_w[:, bass.ds(b * 2 * TOP0, 2 * TOP0)].rearrange("p (n a) -> p n a", a=1)
                                .to_broadcast([P, 2 * TOP0, P]), ALU.mult).then_inc(c_w, 1)

            def sum_f(b):
                dve.wait_ge(c_rt, b + 1)
                v.scalar_tensor_tensor(out=f_sb[:], in0=shT[:, bass.ds(b * SEQ, SEQ)], scalar=0.25,
                                       in1=bank(0, SEQ), op0=ALU.mult, op1=ALU.add).then_inc(c_f, 1)

            def gated_mix(b):
                dve.wait_ge(c_fth, b + 1)
                link(v.scalar_tensor_tensor(out=f_sb[:], in0=f_th[:], scalar=1.0, in1=f_sb[:],
                                            op0=ALU.add, op1=ALU.mult))
                v.tensor_tensor(m_sb[:], f_sb[:], xnT[:, bass.ds(b * SEQ, SEQ)], ALU.mult).then_inc(c_m, 1)

            def norm1(b, u):
                dve.wait_ge(c_mT, b + 1)
                link(v.scalar_tensor_tensor(out=x1[u], in0=ps[:, 7, 0:SEQ].rearrange("p (a d) -> p a d", a=2),
                                            scalar=0.5, in1=x_tok[:, bass.ds(b * 2, 2), :],
                                            op0=ALU.mult, op1=ALU.add))
                for j in range(2):
                    last = v.bn_stats(st1[:, j, :], x1[u][:, j, :])
                link(last)
                take_wait()
                for j in range(2):
                    last = v.bn_aggr(mv1[:, j, :], st1[:, j, :])
                link(last)
                link(v.tensor_scalar(v1[:], mv1[:, :, 1], EPS, None, ALU.add))
                rsqrt_steps(nc, link, r1[:], v1[:], t1[:])
                for j in range(2):
                    last = v.tensor_scalar(xn1[:, j, :], x1[u][:, j, :], mv1[:, j, 0:1], r1[:, j:j + 1],
                                           ALU.subtract, ALU.mult)
                last.then_inc(c_xn, 1)

            half_b = [0]
            weight_rows(0, 0)
            sum_f(0)
            gated_mix(0)
            norm1(0, 0)

            def stage_c(b, u, first, more=True):
                if more:
                    half_b[0] = nb_half[0] if u == 0 else nb_half[0] + 1
                    weight_rows(b + 1, 1 - u)
                dve.wait_ge(d_v, b + 1)
                lagged(dve, d_o, b, u, first, 1)
                v.tensor_tensor(v_sb, ps[:, 1, 0:SEQ].rearrange("p (a d) -> p a d", a=2),
                                bv_b[:].rearrange("p (a d) -> p a d", a=1).to_broadcast([P, 2, P]), ALU.add)
                v.tensor_copy(lg1[:].rearrange("p a e -> p (a e)"), ps[:, 1, 256:256 + 2 * E1]).then_inc(d_vs, 1)
                dve.wait_ge(d_vs, b + 1)
                take_wait()
                for j in range(2):
                    last = v.max(g8[:, j, :], lg1[:, j, :])
                link(last)
                take_wait()
                for j in range(2):
                    last = v.max_index(g8_i[:, j, :], g8[:, j, :], lg1[:, j, :])
                link(last)
                v.tensor_tensor(gd[:], g8[:, :, 0], g8[:, :, 1], ALU.subtract).then_inc(d_gd, 1)
                link(v.tensor_copy(g8_f[:], g8_i[:, :, 0:2]))
                dve.wait_ge(d_s, b + 1)
                link(v.tensor_reduce(mx[:], ps[:, 6, :].rearrange("p (a n) -> p a n", a=2), AX.X, ALU.max))
                v.tensor_scalar(nmx[:], mx[:], -SCALE, None, ALU.mult).then_inc(d_nmx, 1)
                if more:
                    sum_f(b + 1)
                dve.wait_ge(d_gth, b + 1)
                v.tensor_scalar(gw2[:, :, 0], gth[:], 0.5, 0.5, ALU.mult, ALU.add)
                link(v.tensor_scalar(gw2[:, :, 1], gth[:], -0.5, 0.5, ALU.mult, ALU.add))
                lagged(dve, d_gT, b, u, first, 1)
                for j in range(2):
                    v.tensor_scalar(gates[:, j, :], iota_e[:, 0:E1], g8_f[:, j, 0:1], gw2[:, j, 0:1],
                                    ALU.is_equal, ALU.mult)
                    last = v.tensor_scalar(gates2[:, j, :], iota_e[:, 0:E1], g8_f[:, j, 1:2], gw2[:, j, 1:2],
                                           ALU.is_equal, ALU.mult)
                link(last)
                v.tensor_tensor(gates[:], gates[:], gates2[:], ALU.add).then_inc(d_gate, 1)
                if more:
                    gated_mix(b + 1)
                dve.wait_ge(d_gT, b + 1)
                v.tensor_copy(gT[:], ps[0:E1, 3, 0:SEQ]).then_inc(d_gTs, 1)
                if more:
                    norm1(b + 1, 1 - u)
                dve.wait_ge(d_gb, b + 1)
                dve.wait_ge(d_hg, b + 1)
                v.tensor_tensor(hg, hg, ps[:, 0:2, :].rearrange("p a (b n) -> p (a b) n", b=2),
                                ALU.mult).then_inc(d_hs, 1)
                dve.wait_ge(d_p, b + 1)
                link(v.reciprocal(rden[:], den[:]))
                dve.wait_ge(d_mth, b + 1)
                link(v.scalar_tensor_tensor(out=mg[:].rearrange("p a d -> p (a d)"), in0=mth[:], scalar=1.0,
                                            in1=bank(3, SEQ), op0=ALU.add, op1=ALU.mult))
                dve.wait_ge(d_o, b + 1)
                for j in range(2):
                    last = v.scalar_tensor_tensor(out=mg[:, j, :], in0=ps[:, 6, j * P:(j + 1) * P],
                                                  scalar=rden[:, j:j + 1], in1=mg[:, j, :], op0=ALU.mult, op1=ALU.mult)
                link(last)
                if not first:
                    dve.wait_ge(stored[u], 16 * nb_half[0])
                v.scalar_tensor_tensor(out=fin[u], in0=mg[:], scalar=0.5, in1=x1[u],
                                       op0=ALU.mult, op1=ALU.add).then_inc(d_fin, 1)

            nb_half = [0]
            start = chain.n
            for s in range(2):
                stage_c(s, s, True)
            per = chain.n - start
            with dve.Fori(1, NSEQ // 2 - 1) as i:
                chain.n, chain.base = start, i * per
                nb_half[0] = i
                for s in range(2):
                    stage_c(i * 2 + s, s, False)
                assert chain.n - start == per
            chain.n, chain.base = start + per * (NSEQ // 2 - 1), 0
            nb_half[0] = NSEQ // 2 - 1
            stage_c(NSEQ - 2, 0, False)
            stage_c(NSEQ - 1, 1, False, more=False)


_INS = ['L0_attn_x', 'L0_attn_phazor', 'L0_attn_phazor_init', 'L0_attn_last_conv_re', 'L0_attn_last_conv_im',
        'L0_ffn_router_w', 'L0_ffn_w_gate', 'L0_ffn_w_up', 'L0_ffn_w_down', 'L0_ffn_sh_gate', 'L0_ffn_sh_up',
        'L0_ffn_sh_down', 'L0_ffn_sh_gate_w', 'L1_attn_wq', 'L1_attn_bq', 'L1_attn_wk', 'L1_attn_bk',
        'L1_attn_wv', 'L1_attn_bv', 'L1_ffn_w_gate', 'L1_ffn_w_fc', 'L1_ffn_w_proj']
_OUTS = [((NSEQ, SEQ, P), 'float32')]


def kernel(**inputs):
    import numpy as _np
    import concourse.bacc as _bacc
    from concourse import mybir as _mybir
    from concourse.bass_utils import run_bass_kernel_spmd as _run

    nc = _bacc.Bacc("TRN2", target_bir_lowering=False, num_devices=1)
    arrays, args = {}, []
    for name in _INS:
        a = _np.ascontiguousarray(inputs[name])
        arrays[f"in_{name}_dram"] = a
        args.append(nc.dram_tensor(f"in_{name}_dram", a.shape, _mybir.dt.from_np(a.dtype), kind="ExternalInput").ap())
    for i, (shape, dtype) in enumerate(_OUTS):
        dt = _mybir.dt.from_np(_np.dtype(dtype))
        args.append(nc.dram_tensor(f"out_{i}_dram", shape, dt, kind="ExternalOutput").ap())
    build(nc, *args)
    r = _run(nc, [arrays], core_ids=[0])
    got = tuple(r.results[0][f"out_{i}_dram"] for i in range(len(_OUTS)))
    return got[0]
```

```python
from contextlib import ExitStack

import concourse.bass as bass
from concourse import mybir

ALU = mybir.AluOpType
ACT = mybir.ActivationFunctionType
AX = mybir.AxisListType
F32 = mybir.dt.float32
BF16 = mybir.dt.bfloat16
I32 = mybir.dt.int32
U32 = mybir.dt.uint32

P = 128
SEQ = 256
NSEQ = 16
NT = NSEQ * SEQ // P
GT = 4
NG = NT // GT
GW = GT * P
E0, I0, TOP0 = 32, 96, 4
ISH = 256
E1, I1 = 8, 64
CH1 = E1 * I1 // P
NH = 2
HT = NT // NH
ST = -(-(HT * P * TOP0 + E0 * (P - 1)) // P // GT) * GT
SG = ST // GT
NB = 4
BT = NB * SEQ // P
FSEQ = NSEQ // 2
C_NORM = 4
PRE = 4
EPS = 1e-5
SCALE = float(P) ** -0.5


class Chain:

    def __init__(self, eng, sem):
        self.eng, self.sem, self.n, self.base = eng, sem, 0, 0

    def mark(self, ins):
        self.n += 1
        ins.then_inc(self.sem, 1)
        return self.base + self.n

    def after(self, mark):
        self.eng.wait_ge(self.sem, mark)

    def link(self, ins):
        self.after(self.mark(ins))

    def link_beside(self, step, count):
        done = [0]

        def link(ins):
            m = self.mark(ins)
            if done[0] < count:
                step(done[0])
                done[0] += 1
            self.after(m)
        return link


def rounds(eng, count, unroll, body, chains=()):
    start = [c.n for c in chains]
    for s in range(unroll):
        body(s, s, True)
    per = [c.n - n for c, n in zip(chains, start)]
    if count > unroll:
        with eng.Fori(1, count // unroll) as i:
            for c, n, k in zip(chains, start, per):
                c.n, c.base = n, i * k
            for s in range(unroll):
                body(i * unroll + s, s, False)
            for c, n, k in zip(chains, start, per):
                assert c.n - n == k
    for c, n, k in zip(chains, start, per):
        c.n, c.base = n + k * (count // unroll), 0


def lagged(eng, sem, it, slot, first, lag, per=1):
    if not first or slot >= lag:
        eng.wait_ge(sem, (it - lag + 1) * per)


def turned(b):
    if b == -1:
        return FSEQ // 2 - 1
    return FSEQ // 2 + (b - C_NORM) // 2 if b in range(C_NORM, C_NORM + NSEQ - FSEQ, 2) else None


def gated(b):
    return {C_NORM - 2: 1, 2 * NB: 2, 3 * NB: 3}.get(b)


def rsqrt_steps(nc, link, y, v, h):
    w = y.shape[-1]
    yi, vi, half, t = y.bitcast(I32), v.bitcast(I32), h[:, 0:w], h[:, w:2 * w]
    link(nc.vector.tensor_scalar(yi, vi, 1, None, ALU.logical_shift_right))
    nc.vector.tensor_scalar(half, v, -0.5, None, ALU.mult)
    link(nc.vector.tensor_scalar(yi, yi, -1.0, float(0x5F3759DF), ALU.mult, ALU.add))
    for _ in range(3):
        link(nc.vector.tensor_tensor(t, y, y, ALU.mult))
        link(nc.vector.tensor_tensor(t, t, half, ALU.mult))
        link(nc.vector.scalar_tensor_tensor(out=y, in0=t, scalar=1.5, in1=y, op0=ALU.add, op1=ALU.mult))


def build(nc, x, phazor, phazor_init, last_re, last_im, router_w, w_gate, w_up, w_down, sh_gate, sh_up,
          sh_down, sh_gate_w, wq, bq, wk, bk, wv, bv, w_gate1, w_fc, w_proj, out):
    slot_rows = [nc.dram_tensor(f"slot_rows{r}", [ST * P, P], F32, kind="Internal").ap() for r in range(NH)]
    expert_rows = [nc.dram_tensor(f"expert_rows{r}", [ST * P, P], F32, kind="Internal").ap() for r in range(NH)]
    slot_groups = [t.rearrange("(g p j) d -> g p (j d)", p=P, j=GT) for t in slot_rows]
    expert_groups = [t.rearrange("(g p j) d -> g p (j d)", p=P, j=GT) for t in expert_rows]
    x_rows = x.rearrange("b (t p) d -> p (b t) d", p=P)
    out_rows = out.rearrange("b (t p) d -> b p t d", p=P)

    ctx = ExitStack()
    with ctx:
        def sb(name, shape, dt=F32):
            return ctx.enter_context(nc.sbuf_tensor(name, shape, dt))

        def sem(name):
            return ctx.enter_context(nc.semaphore(name))

        x_tok = sb("x_tok", [P, NT, P])
        xn_tok = sb("xn_tok", [P, NT, P])
        xnT = sb("xnT", [P, NT * P])
        sh_tok = sb("sh_tok", [P, NT, P])
        w_gu = sb("w_gu", [P, E0, 2 * I0])
        w_dn = sb("w_dn", [I0, E0 * P])
        logits = sb("logits", [P, NT, E0 + 1])
        top_w = sb("top_w", [P, NT * TOP0])
        slot_of = sb("slot_of", [P, NT * TOP0], I32)
        tile_expert = sb("tile_expert", [1, NH * ST], I32)
        ident = sb("ident", [P, P])
        ones = sb("ones", [P, P])
        rw = sb("rw", [P, E0 + 1])
        shg = sb("shg", [P, ISH])
        shu = sb("shu", [P, ISH])
        shd = sb("shd", [P, ISH // P, P])
        sh_gate_t = sb("sh_gate_t", [P, NT])
        raw1 = sb("raw1", [P, 3, P])
        raw_fc = sb("raw_fc", [P, CH1, P])
        raw_pr = sb("raw_pr", [P, E1, I1])
        raw_g1 = sb("raw_g1", [E1, P])
        w1T = sb("w1T", [P, 3, P])
        fcT = sb("fcT", [P, CH1, P])
        prT = sb("prT", [P, CH1, P])
        g1T = sb("g1T", [P, E1])
        bqk = sb("bqk", [P, 2])
        bv_r = sb("bv_r", [1, P])
        bv_all = sb("bv_all", [P, P])
        expert_sel = sb("expert_sel", [3 * E1, CH1, P], BF16)
        ident_bf = sb("ident_bf", [P, P], BF16)
        zeros = sb("zeros", [P, 2048])
        iota_e = sb("iota_e", [P, E0])
        iota_t1 = sb("iota_t1", [P, SEQ])
        iota_p = sb("iota_p", [P, 1])
        not_before = sb("not_before", [P, P], BF16)
        ones_bf = sb("ones_bf", [P, P], BF16)
        phz = sb("phz", [P, 6])
        cs = sb("cs", [P, 20])
        trig = sb("trig", [P, 2, SEQ + 1])
        out_cs = sb("out_cs", [P, 2, SEQ])
        past = sb("past", [P, SEQ])
        decay_t1 = sb("decay_t1", [P, SEQ])
        decay = sb("decay", [P, 2, SEQ])
        tab_tmp = sb("tab_tmp", [P, SEQ])
        stats = sb("stats", [P, NT, 6])
        mean = sb("mean", [P, NT])
        var = sb("var", [P, NT])
        rstd = sb("rstd", [P, NT])
        rtmp = sb("rtmp", [P, 2 * NT])
        top8 = sb("top8", [P, HT, 8])
        top8_i = sb("top8_i", [P, HT, 8], U32)
        top_f = sb("top_f", [P, HT * TOP0])
        tw = sb("tw", [P, HT, TOP0])
        tsum = sb("tsum", [P, HT])
        onehot = sb("onehot", [P, HT * TOP0, E0])
        mask = sb("mask", [P, HT, E0], BF16)
        route_tmp = sb("route_tmp", [P, 4, HT * E0])
        tot_em = route_tmp[:, 0, :].rearrange("p (e t) -> p e t", e=E0)
        cum_em = route_tmp[:, 1, :].rearrange("p (e t) -> p e t", e=E0)
        pos = route_tmp[:, 2, :].rearrange("p (t e) -> p t e", t=HT)
        not_first = route_tmp[:, 3, :].rearrange("p (e t) -> p e t", e=E0)
        cnt_i = sb("cnt_i", [P, E0], I32)
        tiles_e = sb("tiles_e", [P, E0])
        tile_end = sb("tile_end", [P, E0])
        tile_cmp = sb("tile_cmp", [P, E0])
        tile_ex = sb("tile_ex", [P, 1])
        slot_i = sb("slot_i", [P, HT * TOP0], I32)
        slot_a = sb("slot_a", [P, HT * TOP0], I32)
        hs_t = [sb(f"hs_t{u}", [P, 2, SEQ]) for u in range(2)]
        hs_h = [sb(f"hs_h{u}", [P, 2, SEQ]) for u in range(2)]
        rec = sb("rec", [P, 2, SEQ])
        rows_4 = sb("rows_4", [P, 4, GT * P])
        rows = [rows_4[:, u, :] for u in range(4)]
        eo = [zeros[:, u * GT * P:(u + 1) * GT * P] for u in range(4)]
        exT = [raw_fc[:].rearrange("p c d -> p (c d)"), raw_pr[:].rearrange("p e i -> p (e i)")]
        sg = [sb(f"sg{u}", [P, GT, I0]) for u in range(2)]
        act = [sb(f"act{u}", [P, GT, I0]) for u in range(2)]
        actT = [sb(f"actT{u}", [I0, GT * P]) for u in range(2)]
        gath = [buf[:, u * 2 * TOP0 * P:(u + 1) * 2 * TOP0 * P].rearrange("p (n d) -> p n d", d=P)
                for buf in (onehot[:].rearrange("p n e -> p (n e)"), route_tmp[:].rearrange("p a n -> p (a n)"))
                for u in range(2)]
        hg = [rows_4[:, 2 * u:2 * u + 2, :].rearrange("p a (b n) -> p (a b) n", n=SEQ) for u in range(2)]
        s_rec = tab_tmp
        xn1 = rec[:].rearrange("p c (a d) -> p (c a) d", d=P)
        xn1T = [hs_t[0][:, u, :] for u in range(2)]
        xn1T_pair = decay[:].rearrange("p a t -> p (a t)")
        f_sb = trig[:].rearrange("p a t -> p (a t)")[:, 0:2 * SEQ].rearrange("p (a d) -> p a d", d=P)
        f_act = out_cs[:].rearrange("p c (a d) -> p (c a) d", d=P)
        f_w = [sb(f"f_w{u}", [P, 2 * TOP0]) for u in range(2)]
        st1 = sb("st1", [P, 4, 6])
        mv1 = sb("mv1", [P, 4, 2])
        v1 = sb("v1", [P, 4])
        r1 = sb("r1", [P, 4])
        t1 = sb("t1", [P, 8])
        qk_sb = hs_h[0]
        v_sb = decay_t1[:].rearrange("p (a d) -> p a d", a=2)
        lg1 = sb("lg1", [P, NT, E1])
        g8, g8_i = top8[:, 0:BT, :], top8_i[:, 0:BT, :]
        g8_f = sb("g8_f", [P, BT, 2])
        gd = sb("gd", [P, BT])
        gth = sb("gth", [P, BT])
        gw2 = sb("gw2", [P, BT, 2])
        gates = sb("gates", [P, BT, E1])
        gates2 = sb("gates2", [P, BT, E1])
        gate_parts = sb("gate_parts", [P, BT, 3, E1], BF16)
        gT = [logits[:].rearrange("p t e -> p (t e)").bitcast(BF16)[0:3 * E1, u * BT * P:(u + 1) * BT * P]
              for u in range(2)]
        mx = sb("mx", [P, 2])
        nmx = sb("nmx", [P, 2])
        den = sb("den", [P, 2])
        rden = sb("rden", [P, 2])
        pr = hs_h[1]
        pT = hs_t[1]
        mth = sb("mth", [P, SEQ])
        mg = sb("mg", [P, 2, P])
        o_sb = [sb(f"o_sb{u}", [P, 2, P]) for u in range(2)]
        fin = [raw_fc[:, 2 * u:2 * u + 2, :] for u in range(2)]

        ps = ctx.enter_context(nc.psum_tensor("ps", [P, 8, 512], F32))

        def bank(n, width=512):
            return ps[:, n, 0:width]

        x_in = [sem(f"x_in{g}") for g in range(NG)]
        phz_in = sem("phz_in")
        rw_in = sem("rw_in")
        w_in = sem("w_in")
        we_in = sem("we_in")
        zero_set = sem("zero_set")
        filled = [sem(f"filled{r}") for r in range(NH)]
        ident_0 = sem("ident_0")
        pool_c = sem("pool_c")
        sel_in = sem("sel_in")
        dve_link = sem("dve_link")
        act_link = sem("act_link")
        pool_link = sem("pool_link")
        wT_ps = sem("wT_ps")
        wT_sb = sem("wT_sb")
        xn_ready = sem("xn_ready")
        xT_ps = sem("xT_ps")
        xT_sb = sem("xT_sb")
        lg_ps = sem("lg_ps")
        lg_sb = sem("lg_sb")
        tw_in = sem("tw_in")
        tw_exp = sem("tw_exp")
        mask_ready = sem("mask_ready")
        rank_ps = sem("rank_ps")
        ex_ready = sem("ex_ready")
        exT_row = sem("exT_row")
        routed = sem("routed")
        slots_ready = sem("slots_ready")
        sent = [sem(f"sent{r}") for r in range(NH)]
        mag_ready = sem("mag_ready")
        tables = sem("tables")
        exp_ready = sem("exp_ready")
        sh_ps = sem("sh_ps")
        sh_silu = sem("sh_silu")
        sh_gated = sem("sh_gated")
        sh_hid = sem("sh_hid")
        sh_dn = sem("sh_dn")
        sh_done = sem("sh_done")
        recurred = sem("recurred")
        s_ps = sem("s_ps")
        s_tok = sem("s_tok")
        rows_in = [sem(f"rows_in{u}") for u in range(4)]
        e_xT = sem("e_xT")
        e_xTs = sem("e_xTs")
        e_gu = sem("e_gu")
        e_sg = sem("e_sg")
        e_act = sem("e_act")
        e_aT = sem("e_aT")
        e_aTs = sem("e_aTs")
        e_dn = sem("e_dn")
        e_out = sem("e_out")
        e_stored = [sem(f"e_stored{u}") for u in range(4)]
        g_in = [sem(f"g_in{u}") for u in range(4)]
        xr_in = [sem(f"xr_in{u}") for u in range(2)]
        c_f = sem("c_f")
        c_fact = sem("c_fact")
        c_xn = sem("c_xn")
        c_xnT = sem("c_xnT")
        c_xn_kept = sem("c_xn_kept")
        c_lg = sem("c_lg")
        c_lgs = sem("c_lgs")
        d_qk = sem("d_qk")
        d_v = sem("d_v")
        d_h = sem("d_h")
        d_qks = sem("d_qks")
        d_vs = sem("d_vs")
        d_hg = sem("d_hg")
        d_gd = sem("d_gd")
        d_gth = sem("d_gth")
        d_gate = sem("d_gate")
        d_gT = sem("d_gT")
        d_gTs = sem("d_gTs")
        d_gb = sem("d_gb")
        d_hs = sem("d_hs")
        d_s = sem("d_s")
        d_nmx = sem("d_nmx")
        d_p = sem("d_p")
        d_pT = sem("d_pT")
        d_pTs = sem("d_pTs")
        d_o = sem("d_o")
        d_os = sem("d_os")
        d_moe = sem("d_moe")
        d_mth = sem("d_mth")
        d_fin = sem("d_fin")
        stored = [sem(f"stored{u}") for u in range(2)]

        N_W = 12
        N_FILL = 6
        RANKS_AFTER, IDS_AFTER = 2, 4
        E_NORM = NH * SG // 4 - FSEQ // 2 - 1
        block = ctx.enter_context(nc.Block())

        @block.sync
        def _(sp):
            for t, (a, b, src) in enumerate(((0, 2, phazor), (2, 4, phazor_init),
                                             (4, 5, last_re.rearrange("(d a) -> d a", a=1)),
                                             (5, 6, last_im.rearrange("(d a) -> d a", a=1)))):
                sp.dma_start(phz[:, a:b], src).then_inc(phz_in, 16)
            for g in range(NG):
                sp.dma_start(x_tok[:, g * GT:(g + 1) * GT, :],
                             x_rows[:, g * GT:(g + 1) * GT, :]).then_inc(x_in[g], 16)
            sp.dma_start(rw[:, 0:E0], router_w).then_inc(rw_in, 16)
            sp.dma_start(rw[:, E0:E0 + 1], sh_gate_w).then_inc(rw_in, 16)
            n = 0
            for dst, src in (
                (raw_g1[:], w_gate1),
                (shg[:], sh_gate),
                (shu[:], sh_up),
                (shd[:], sh_down.rearrange("(c p) h -> p c h", p=P)),
                (raw1[:, 0, :], wq),
                (raw1[:, 1, :], wk),
                (raw1[:, 2, :], wv),
                (bqk[:, 0:1], bq.rearrange("(d a) -> d a", a=1)),
                (bqk[:, 1:2], bk.rearrange("(d a) -> d a", a=1)),
                (bv_r[:], bv.rearrange("(a d) -> a d", a=1)),
                (raw_fc[:], w_fc.rearrange("(c e) i h -> (e i) c h", c=CH1)),
                (raw_pr[:], w_proj.rearrange("e h i -> h e i")),
            ):
                sp.dma_start(dst, src).then_inc(w_in, 16)
                n += 1
            assert n == N_W
            sp.wait_ge(pool_c, 7)
            for k in (1, 2):
                sp.dma_start(expert_sel[k * E1:(k + 1) * E1, :, :], expert_sel[0:E1, :, :]).then_inc(sel_in, 16)
            sp.wait_ge(zero_set, 1)
            for r in range(NH):
                flat = slot_rows[r].rearrange("(p c a n) d -> p c a (n d)", p=P, c=N_FILL, n=GT)
                for c in range(N_FILL):
                    sp.dma_start(flat[:, c, :, :], zeros[:, 0:GW].rearrange("p (a n) -> p a n", a=1)
                                 .to_broadcast([P, ST // GT // N_FILL, GW])).then_inc(filled[r], 16)
                if r == 0:
                    sp.dma_start(w_gu[:, :, 0:I0], w_gate.rearrange("e h i -> h e i")).then_inc(we_in, 16)
                    sp.dma_start(w_gu[:, :, I0:2 * I0], w_up.rearrange("e h i -> h e i")).then_inc(we_in, 16)
                    sp.dma_start(w_dn[:].rearrange("i (e h) -> i e h", e=E0),
                                 w_down.rearrange("e i h -> i e h")).then_inc(we_in, 16)

            def store(r, it, slot):
                sp.wait_ge(e_out, r * SG + it + 1)
                sp.dma_start(expert_groups[r][bass.ds(it, 1), :, :].rearrange("a p n -> (a p) n"),
                             eo[slot]).then_inc(e_stored[slot], 16)

            def load(r, it, slot):
                if not (isinstance(it, int) and it < 4 and r == 0):
                    sp.wait_ge(e_xT, r * SG + it - 4 + 1)
                sp.dma_start(rows[slot], slot_groups[r][bass.ds(it, 1), :, :]
                             .rearrange("a p n -> (a p) n")).then_inc(rows_in[slot], 16)

            for r in range(NH):
                sp.wait_ge(sent[r], 16 * HT * TOP0)
                for s in range(4):
                    load(r, s, s)
                    if r:
                        store(r - 1, SG - 4 + s, s)
                with sp.Fori(1, SG // 4) as i:
                    for s in range(4):
                        load(r, i * 4 + s, s)
                        store(r, (i - 1) * 4 + s, s)
            def load_xn(b, u):
                if isinstance(b, int) and b < 2:
                    sp.wait_ge(c_xn_kept, 1)
                else:
                    sp.wait_ge(d_h, b - 1)
                sp.dma_start(xn1T[u], xn_tok[:, bass.ds(b * 2, 2), :].rearrange("p a d -> p (a d)")).then_inc(xr_in[u], 16)

            def store_out(b, u):
                sp.wait_ge(d_fin, b + 1)
                sp.dma_start(out_rows[bass.ds(b, 1), :, :, :].rearrange("a p t d -> (a p) t d"),
                             fin[u]).then_inc(stored[u], 16)
            load_xn(0, 0)
            load_xn(1, 1)
            for s in range(4):
                store(NH - 1, SG - 4 + s, s)
            with sp.Fori(0, NSEQ // 2 - 1) as i:
                for u in range(2):
                    load_xn(i * 2 + u + 2, u)
                    store_out(i * 2 + u, u)
            for u in range(2):
                store_out(NSEQ - 2 + u, u)
            for s in range(2):
                sp.wait_ge(stored[s], 16 * NSEQ // 2)

        @block.gpsimd
        def _(pool):
            chain = Chain(pool, pool_link)
            g = nc.gpsimd
            chain.link(g.memset(ident[:], 0.0))
            g.affine_select(out=ident[:], in_=ident[:], compare_op=ALU.not_equal, fill=1.0, base=0,
                            pattern=[[-1, P]], channel_multiplier=1).then_inc(pool_c, 1)
            pool.wait_ge(pool_c, 1)
            chain.link(g.memset(not_before[:], 0.0))
            g.affine_select(out=not_before[:], in_=not_before[:], compare_op=ALU.is_gt, fill=-1.0, base=0,
                            pattern=[[1, P]], channel_multiplier=-1).then_inc(pool_c, 1)
            g.iota(iota_e[:], [[1, E0]], base=0, channel_multiplier=0,
                   allow_small_or_imprecise_dtypes=True).then_inc(pool_c, 1)
            g.iota(iota_t1[:], [[1, SEQ]], base=1, channel_multiplier=0,
                   allow_small_or_imprecise_dtypes=True).then_inc(pool_c, 1)
            g.iota(iota_p[:], [[1, 1]], base=0, channel_multiplier=1,
                   allow_small_or_imprecise_dtypes=True).then_inc(pool_c, 1)
            g.tensor_copy(ident_bf[:], ident[:]).then_inc(pool_c, 1)
            chain.link(g.memset(expert_sel[0:E1], 1.0))
            chain.link(g.affine_select(out=expert_sel[0:E1], in_=expert_sel[0:E1], compare_op=ALU.is_ge, fill=0.0,
                                       base=0, pattern=[[P, CH1], [1, P]], channel_multiplier=-I1))
            g.affine_select(out=expert_sel[0:E1], in_=expert_sel[0:E1], compare_op=ALU.is_ge, fill=0.0,
                            base=I1 - 1, pattern=[[-P, CH1], [-1, P]], channel_multiplier=I1).then_inc(pool_c, 1)

            def scaled(dst, table, by):
                return g.tensor_scalar(dst, table, by, None, ALU.mult)

            def cmul(re, im, ar, ai, br, bi, t0, t1):
                scaled(re, ar, br)
                scaled(im, ai, br)
                scaled(t0, ai, bi)
                chain.link(scaled(t1, ar, bi))
                g.tensor_tensor(re, re, t0, ALU.subtract)
                chain.link(g.tensor_tensor(im, im, t1, ALU.add))

            pool.wait_ge(phz_in, 64)
            pool.wait_ge(mag_ready, 1)
            g.memset(trig[:, 0, 0:1], 1.0)
            g.memset(trig[:, 1, 0:1], 0.0)
            g.memset(decay[:], 1.0)
            g.tensor_copy(trig[:, 0, 1:2], cs[:, 1:2])
            chain.link(g.tensor_copy(trig[:, 1, 1:2], cs[:, 2:3]))
            n = 1
            while n < SEQ:
                cmul(trig[:, 0, n + 1:2 * n + 1], trig[:, 1, n + 1:2 * n + 1],
                     trig[:, 0, 1:n + 1], trig[:, 1, 1:n + 1], trig[:, 0, n:n + 1], trig[:, 1, n:n + 1],
                     tab_tmp[:, 0:n], tab_tmp[:, n:2 * n])
                n *= 2
            cmul(out_cs[:, 0, :], out_cs[:, 1, :], trig[:, 0, 0:SEQ], trig[:, 1, 0:SEQ], phz[:, 2:3], phz[:, 3:4],
                 rec[:, 0, :], rec[:, 1, :])
            scaled(past[:], trig[:, 0, 1:SEQ + 1], phz[:, 4:5])
            chain.link(scaled(tab_tmp[:], trig[:, 1, 1:SEQ + 1], phz[:, 5:6]))
            chain.link(g.tensor_tensor(past[:], past[:], tab_tmp[:], ALU.subtract))
            pool.wait_ge(exp_ready, 2)
            g.tensor_tensor(past[:], past[:], decay_t1[:], ALU.mult)
            chain.link(scaled(decay[:], decay[:], cs[:, 4:5]))
            g.memset(decay[:, :, 0:1], 0.0).then_inc(tables, 1)

            for r in range(NH):
                pool.wait_ge(filled[r], 16 * N_FILL)
                for t in range(HT):
                    if t in (0, GT):
                        pool.wait_ge(slots_ready, r * 2 + 1 + t // GT)
                    for k in range(TOP0):
                        n = (r * HT + t) * TOP0 + k
                        g.indirect_dma_start(
                            out=slot_rows[r], out_offset=bass.IndirectOffsetOnAxis(ap=slot_of[:, n:n + 1], axis=0),
                            in_=xn_tok[:, r * HT + t, :], in_offset=None).then_inc(sent[r], 16)

            for b in range(NSEQ):
                r = b // (NSEQ // NH)
                if b % (NSEQ // NH) == 0:
                    for u in range(4):
                        pool.wait_ge(e_stored[u], 16 * (r + 1) * SG // 4)
                slot = b % 4 if b < FSEQ else b % 2
                before_b = b - 4 if b < FSEQ + 2 else b - 2
                if before_b >= 0:
                    pool.wait_ge(c_f, before_b + 1)
                for j in range(2 * TOP0):
                    n = b * 2 * TOP0 + j
                    g.indirect_dma_start(
                        out=gath[slot][:, j, :], out_offset=None, in_=expert_rows[r],
                        in_offset=bass.IndirectOffsetOnAxis(ap=slot_of[:, n:n + 1], axis=0)).then_inc(g_in[slot], 16)

        @block.tensor
        def _(pe):
            pe.wait_ge(pool_c, 1)
            pe.wait_ge(rw_in, 32)

            def logits_of(it):
                pe.wait_ge(xT_sb, it + 1)
                if it >= 2:
                    pe.wait_ge(lg_sb, it - 1)
                for j in range(GT):
                    mm = pe.matmul(ps[:, 2 + it % 2, j * (E0 + 1):(j + 1) * (E0 + 1)],
                                   xnT[:, (it * GT + j) * P:(it * GT + j + 1) * P], rw[:], start=True, stop=True)
                mm.then_inc(lg_ps, 1)

            def ranks(r):
                pe.wait_ge(pool_c, 7)
                pe.wait_ge(mask_ready, r + 1)
                pe.matmul(bank(6), not_before[:], mask[:].rearrange("p t e -> p (t e)"), start=True, stop=True)
                pe.matmul(bank(7), ones_bf[:], mask[:].rearrange("p t e -> p (t e)"),
                          start=True, stop=True).then_inc(rank_ps, 1)

            def tile_ids(r):
                pe.wait_ge(ex_ready, r + 1)
                pe.transpose(ps[0:1, 7, 0:ST], tile_ex[0:ST, :], ident[0:ST, 0:ST]).then_inc(exT_row, 1)

            def turn_half(r):
                for it in range(r * NG // NH, (r + 1) * NG // NH):
                    pe.wait_ge(xn_ready, it + 1)
                    if it >= 2:
                        pe.wait_ge(xT_sb, it - 1)
                    for j in range(GT):
                        mm = pe.transpose(ps[:, it % 2, j * P:(j + 1) * P], xn_tok[:, it * GT + j, :], ident[:])
                    mm.then_inc(xT_ps, 1)
                    if it % (NG // NH):
                        logits_of(it - 1)
                logits_of((r + 1) * NG // NH - 1)

            turn_half(0)
            ranks(0)
            tile_ids(0)

            pe.wait_ge(w_in, 16 * N_W)
            pe.wait_ge(lg_sb, NG // NH)
            for j in range(3):
                last = pe.transpose(ps[:, 2, j * P:(j + 1) * P], raw1[:, j, :], ident[:])
            last.then_inc(wT_ps, 1)
            for j in range(CH1):
                last = pe.transpose(ps[:, 3, j * P:(j + 1) * P], raw_fc[:, j, :], ident[:])
            last.then_inc(wT_ps, 1)
            for j in range(CH1):
                last = pe.transpose(ps[:, 4, j * P:(j + 1) * P],
                                    raw_pr[:].rearrange("h e i -> h (e i)")[:, j * P:(j + 1) * P], ident[:])
            last.then_inc(wT_ps, 1)
            pe.transpose(ps[:, 5, 0:E1], raw_g1[:], ident[0:E1, 0:E1])
            pe.matmul(ps[:, 5, P:2 * P], ones[0:1, :], bv_r[:], start=True, stop=True).then_inc(wT_ps, 1)

            pe.wait_ge(wT_sb, 4)

            def shared_in(it, u, first=False):
                if not first:
                    pe.wait_ge(sh_hid, it - 1)
                xg = xnT[:, bass.ds(it * SEQ, SEQ)]
                for c in range(2):
                    pe.matmul(ps[:, 2 * u, c * SEQ:(c + 1) * SEQ], shg[:, c * P:(c + 1) * P], xg,
                              start=True, stop=True)
                for c in range(2):
                    mm = pe.matmul(ps[:, 2 * u + 1, c * SEQ:(c + 1) * SEQ], shu[:, c * P:(c + 1) * P], xg,
                                   start=True, stop=True)
                mm.then_inc(sh_ps, 1)

            def shared_out(it, u):
                pe.wait_ge(sh_hid, it + 1)
                if not (isinstance(it, int) and it < 2):
                    pe.wait_ge(sh_done, it - 1)
                for j in range(2):
                    for c in range(2):
                        mm = pe.matmul(ps[:, 4 + u, j * P:(j + 1) * P], hs_h[u][:, c, j * P:(j + 1) * P],
                                       shd[:, c, :], start=(c == 0), stop=(c == 1))
                mm.then_inc(sh_dn, 1)

            def turn_s(b):
                pe.wait_ge(recurred, b + 1)
                if not (isinstance(b, int) and b == 0):
                    pe.wait_ge(s_tok, b)
                for j in range(2):
                    mm = pe.transpose(ps[:, 7, j * P:(j + 1) * P], s_rec[:, j * P:(j + 1) * P], ident[:])
                mm.then_inc(s_ps, 1)

            HS = NSEQ // NH
            shared_in(0, 0, True)
            for it in range(HS):
                if it + 1 < HS:
                    shared_in(it + 1, (it + 1) % 2, it == 0)
                shared_out(it, it % 2)
            turn_half(1)
            for b in range(PRE - 2):
                turn_s(b)
            pe.wait_ge(xT_sb, NG)
            pe.wait_ge(lg_sb, NG)
            shared_in(HS, 0)
            for it in range(HS, NSEQ):
                if it + 1 < NSEQ:
                    shared_in(it + 1, (it + 1) % 2)
                shared_out(it, it % 2)
                if it == HS + RANKS_AFTER:
                    pe.wait_ge(s_tok, PRE - 2)
                    ranks(1)
                if it == HS + IDS_AFTER:
                    tile_ids(1)

            pe.wait_ge(sh_done, NSEQ)
            pe.wait_ge(we_in, 48)
            pe.wait_ge(routed, NH)

            def ids(at):
                _, v = nc.values_load_multi_w_load_instructions(
                    tile_expert[0:1, bass.ds(at, GT)], engines=[mybir.EngineType.PE], min_val=0, max_val=E0 - 1,
                    skip_runtime_bounds_check_because="VectorE clamps the ids to E0 - 1")
                return v

            N = NH * SG

            def rows_T(n, slot, fills, first=False):
                pe.wait_ge(rows_in[slot], fills * 16)
                if not first:
                    pe.wait_ge(e_xTs, n)
                for j in range(GT):
                    mm = pe.transpose(ps[:, 0, j * P:(j + 1) * P], rows[slot][:, j * P:(j + 1) * P], ident[:])
                mm.then_inc(e_xT, 1)

            def act_T(n, u, first=False):
                pe.wait_ge(e_act, n + 1)
                if not first:
                    pe.wait_ge(e_aTs, n)
                for j in range(GT):
                    mm = pe.transpose(ps[0:I0, 5, j * P:(j + 1) * P], act[u][:, j, :], ident[:])
                mm.then_inc(e_aT, 1)

            def down(n, u, e, first=False):
                pe.wait_ge(e_aTs, n + 1)
                if not first:
                    pe.wait_ge(e_out, n)
                for j in range(GT):
                    mm = pe.matmul(ps[:, 6, j * P:(j + 1) * P], actT[u][:, j * P:(j + 1) * P],
                                   w_dn[:, bass.ds(e[j] * P, P)], start=True, stop=True)
                mm.then_inc(e_dn, 1)

            def gate_up(n, u, e, first=False):
                pe.wait_ge(e_xTs, n + 1)
                if not first:
                    pe.wait_ge(e_act, n - 1)
                for j in range(GT):
                    mm = pe.matmul(ps[:, 1 + 2 * u + j // 2, (j % 2) * 256:(j % 2) * 256 + 2 * I0],
                                   exT[u][:, j * P:(j + 1) * P],
                                   w_gu[:, bass.ds(e[j], 1), :].rearrange("p a n -> p (a n)"),
                                   start=True, stop=True)
                mm.then_inc(e_gu, 1)

            def turn_xn(p):
                pe.wait_ge(c_xn, p + 1)
                for j in range(4):
                    mm = pe.transpose(ps[:, 7, j * P:(j + 1) * P], xn1[:, j, :], ident[:])
                mm.then_inc(c_xnT, 1)

            def gate_logits(p):
                pe.wait_ge(c_xn_kept, p + 1)
                for j in range(4):
                    mm = pe.matmul(ps[:, 7, 2 * SEQ - (4 - j) * E1:2 * SEQ - (3 - j) * E1],
                                   xn1T_pair[:, j * P:(j + 1) * P], g1T[:], start=True, stop=True)
                return mm

            def turn_between(p):
                if p:
                    pe.wait_ge(c_lgs, p)
                turn_xn(p)

            def logits_between(p):
                gate_logits(p).then_inc(c_lg, 1)

            def stage_e(n, slot, rnd, first=False, turn=None):
                e_down = None if first and slot == 0 else ids((n - 1) * GT)
                e_next = ids((n + 1) * GT) if not isinstance(n, int) or n + 1 < N else None
                if not isinstance(n, int) or n + 2 < N:
                    rows_T(n + 2, (slot + 2) % 4, rnd + (2 if slot >= 2 else 1))
                if e_down is not None:
                    down(n - 1, (slot + 1) % 2, e_down, first and slot == 1)
                act_T(n, slot % 2, first and slot == 0)
                if turn is not None:
                    turn()
                if e_next is not None:
                    gate_up(n + 1, (slot + 1) % 2, e_next, first and slot == 0)

            turn_s(PRE - 2)
            rows_T(0, 0, 1, True)
            rows_T(1, 1, 1)
            gate_up(0, 0, ids(0), True)
            turn_s(PRE - 1)
            for s in range(4):
                stage_e(s, s, 0, True, (lambda: turn_s(PRE)) if s == 2 else None)
            with pe.Fori(1, (NSEQ - PRE) // 2) as i:
                for s in range(4):
                    stage_e(i * 4 + s, s, i, turn=None if s % 2 else lambda: turn_s(PRE - 1 + i * 2 + s // 2))
            turn_s(NSEQ - 1)
            with pe.Fori((NSEQ - PRE) // 2, E_NORM) as i:
                for s in range(4):
                    stage_e(i * 4 + s, s, i)
            for i in range(E_NORM, N // 4):
                p = i - E_NORM - 2
                turns = [None] * 4 if p < 0 else [lambda: turn_between(p), lambda: logits_between(p), None, None]
                for s in range(4):
                    stage_e(i * 4 + s, s, i, turn=turns[s])
            down(N - 1, 1, ids((N - 1) * GT))

            pe.wait_ge(e_out, N)
            pe.wait_ge(c_lgs, FSEQ // 2 - 1)

            def expert_sum(b, u, first):
                pe.wait_ge(d_hs, b + 1)
                if not first:
                    pe.wait_ge(d_fin, b)
                for j in range(2):
                    for c in range(CH1):
                        mm = pe.matmul(ps[:, 3, j * P:(j + 1) * P], hg[u][:, c, j * P:(j + 1) * P], prT[:, c, :],
                                       start=(c == 0), stop=(c == CH1 - 1))
                mm.then_inc(d_moe, 1)

            def turn_gates(k):
                pe.wait_ge(d_gate, k + 1)
                for j in range(BT):
                    mm = pe.matmul(ps[0:3 * E1, j // 4, (j % 4) * P:(j % 4 + 1) * P],
                                   gate_parts[:, j, :, :].rearrange("p a e -> p (a e)"), ident_bf[:],
                                   start=True, stop=True)
                mm.then_inc(d_gT, 1)
                pe.wait_ge(d_gTs, k + 1)

            pe.wait_ge(sel_in, 32)
            for b in range(NSEQ):
                u = b % 2
                pe.wait_ge(xr_in[u], 16 * (b // 2 + 1))
                if b:
                    pe.wait_ge(d_pTs, b)
                for j in range(2):
                    mm = pe.matmul(ps[:, 2, j * SEQ:(j + 1) * SEQ], w1T[:, j, :], xn1T[u], start=True, stop=True)
                mm.then_inc(d_qk, 1)
                if b:
                    pe.wait_ge(d_vs, b)
                if turned(b - 2) is not None:
                    gate_logits(turned(b - 2))
                for j in range(2):
                    mm = pe.matmul(ps[:, 7, j * P:(j + 1) * P], xn1T[u][:, j * P:(j + 1) * P], w1T[:, 2, :],
                                   start=True, stop=True)
                mm.then_inc(d_v, 1)
                pe.wait_ge(d_qks, b + 1)
                if b:
                    pe.wait_ge(d_os, b)
                for j in range(2):
                    mm = pe.matmul(ps[:, 6, j * SEQ:(j + 1) * SEQ], qk_sb[:, 0, j * P:(j + 1) * P], qk_sb[:, 1, :],
                                   start=True, stop=True)
                mm.then_inc(d_s, 1)
                if b:
                    pe.wait_ge(d_hg, b)
                for c in range(CH1):
                    mm = pe.matmul(ps[:, 4 + c // 2, (c % 2) * SEQ:(c % 2 + 1) * SEQ], fcT[:, c, :], xn1T[u],
                                   start=True, stop=True)
                mm.then_inc(d_h, 1)
                if turned(b - 1) is not None:
                    pe.wait_ge(d_vs, b + 1)
                    turn_xn(turned(b - 1))
                if b:
                    expert_sum(b - 1, 1 - u, b == 1)
                pe.wait_ge(d_p, b + 1)
                for k in range(2):
                    for j in range(2):
                        mm = pe.transpose(ps[:, 2, k * SEQ + j * P:k * SEQ + (j + 1) * P],
                                          pr[:, j, k * P:(k + 1) * P], ident[:])
                mm.then_inc(d_pT, 1)
                if b:
                    pe.wait_ge(d_hs, b)
                if b % NB == 0:
                    turn_gates(b // NB)
                for c in range(CH1):
                    mm = pe.matmul(ps[:, c // 2, (c % 2) * SEQ:(c % 2 + 1) * SEQ], expert_sel[:, c, :],
                                   gT[b // NB % 2][:, b % NB * SEQ:(b % NB + 1) * SEQ], start=True, stop=True)
                mm.then_inc(d_gb, 1)
                pe.wait_ge(d_pTs, b + 1)
                for j in range(2):
                    for k in range(2):
                        mm = pe.matmul(ps[:, 6, j * P:(j + 1) * P], pT[:, k, j * P:(j + 1) * P], v_sb[:, k, :],
                                       start=(k == 0), stop=(k == 1))
                mm.then_inc(d_o, 1)
            expert_sum(NSEQ - 1, 1, False)

        @block.scalar
        def _(sc):
            a = nc.scalar
            chain = Chain(sc, act_link)
            sc.wait_ge(mag_ready, 1)
            sc.wait_ge(pool_c, 7)
            a.activation(cs[:, 4:5], cs[:, 3:4], ACT.Exp).then_inc(exp_ready, 1)
            a.activation(decay_t1[:], iota_t1[:], ACT.Exp, scale=cs[:, 3:4]).then_inc(exp_ready, 1)

            def copy_logits(it):
                sc.wait_ge(lg_ps, it + 1)
                a.copy(logits[:, it * GT:(it + 1) * GT, :].rearrange("p t e -> p (t e)"),
                       bank(2 + it % 2, GT * (E0 + 1))).then_inc(lg_sb, 1)

            def exp_top(r):
                sc.wait_ge(tw_in, r + 1)
                a.activation(tw[:], tw[:], ACT.Exp).then_inc(tw_exp, 1)

            def copy_half(r):
                for it in range(r * NG // NH, (r + 1) * NG // NH):
                    sc.wait_ge(xT_ps, it + 1)
                    a.copy(xnT[:, it * GW:(it + 1) * GW], bank(it % 2)).then_inc(xT_sb, 1)
                    if it % (NG // NH):
                        copy_logits(it - 1)
                copy_logits((r + 1) * NG // NH - 1)
                sc.wait_ge(lg_sb, (r + 1) * NG // NH)
                a.activation(sh_gate_t[:, r * HT:(r + 1) * HT], logits[:, r * HT:(r + 1) * HT, E0],
                             ACT.Sigmoid).then_inc(sh_gated, 1)

            copy_half(0)
            exp_top(0)
            sc.wait_ge(wT_ps, 4)
            a.copy(w1T[:].rearrange("p a b -> p (a b)"), bank(2, 384)).then_inc(wT_sb, 1)
            a.copy(fcT[:].rearrange("p a b -> p (a b)"), bank(3)).then_inc(wT_sb, 1)
            a.copy(prT[:].rearrange("p a b -> p (a b)"), bank(4)).then_inc(wT_sb, 1)
            a.copy(g1T[:], bank(5, E1))
            a.copy(bv_all[:], ps[:, 5, P:2 * P]).then_inc(wT_sb, 1)

            def stage_s(it, u):
                sc.wait_ge(sh_ps, it + 1)
                if it >= 2:
                    sc.wait_ge(sh_hid, it - 1)
                a.activation(hs_t[u][:].rearrange("p a t -> p (a t)"), bank(2 * u), ACT.Silu).then_inc(sh_silu, 1)
            def copy_s(b):
                sc.wait_ge(s_ps, b + 1)
                a.copy(xnT[:, bass.ds(b * SEQ, SEQ)], ps[:, 7, 0:SEQ]).then_inc(s_tok, 1)

            for it in range(NSEQ):
                if it == NSEQ // NH:
                    copy_half(1)
                    for b in range(PRE - 2):
                        copy_s(b)
                stage_s(it, it % 2)
                if it == NSEQ // NH + RANKS_AFTER:
                    exp_top(1)

            def copy_xT(n, u):
                sc.wait_ge(e_xT, n + 1)
                if not (isinstance(n, int) and n < 2):
                    sc.wait_ge(e_gu, n - 1)
                a.copy(exT[u], bank(0)).then_inc(e_xTs, 1)

            def silu_gate(n, u):
                sc.wait_ge(e_gu, n + 1)
                if not (isinstance(n, int) and n < 2):
                    sc.wait_ge(e_act, n - 1)
                a.activation(sg[u][:].rearrange("p (a b) i -> p a b i", a=2),
                             ps[:, 1 + 2 * u:3 + 2 * u, :].rearrange("p a (b i) -> p a b i", b=2)[:, :, :, 0:I0],
                             ACT.Silu).then_inc(e_sg, 1)

            def copy_out(n, slot, rnd):
                sc.wait_ge(e_dn, n + 1)
                if not (isinstance(rnd, int) and rnd == 0):
                    sc.wait_ge(e_stored[slot], rnd * 16)
                a.copy(eo[slot], bank(6)).then_inc(e_out, 1)

            for r in range(NH):
                sc.wait_ge(filled[r], 16 * N_FILL)

            def copy_aT(n, u):
                sc.wait_ge(e_aT, n + 1)
                if not (isinstance(n, int) and n < 2):
                    sc.wait_ge(e_dn, n - 1)
                a.copy(actT[u][:], ps[0:I0, 5, :]).then_inc(e_aTs, 1)

            def silu_f(p):
                sc.wait_ge(c_f, 2 * p + 2)
                a.activation(f_act, f_sb, ACT.Silu).then_inc(c_fact, 1)

            def copy_xn(p):
                sc.wait_ge(c_xnT, p + 1)
                a.copy(xn1T_pair, bank(7))
                a.copy(xn_tok[:, bass.ds(p * 4, 4), :].rearrange("p a d -> p (a d)"), bank(7)).then_inc(c_xn_kept, 1)

            def copy_gate_logits(p):
                a.copy(lg1[:, bass.ds(p * 4, 4), :].rearrange("p a e -> p (a e)"),
                       ps[:, 7, 2 * SEQ - 4 * E1:2 * SEQ]).then_inc(c_lgs, 1)

            def logits_between(p, count):
                sc.wait_ge(c_lg, count)
                copy_gate_logits(p)

            N = NH * SG

            def stage_e(n, slot, rnd, turn=None, after=None):
                if not isinstance(n, int) or n + 2 < N:
                    copy_xT(n + 2, slot % 2)
                if not isinstance(n, int) or n > 0:
                    copy_out(n - 1, (slot + 3) % 4, rnd if slot else rnd - 1)
                copy_aT(n, slot % 2)
                if turn is not None:
                    turn()
                if not isinstance(n, int) or n + 1 < N:
                    silu_gate(n + 1, (slot + 1) % 2)
                if after is not None:
                    after()
            copy_s(PRE - 2)
            copy_xT(0, 0)
            copy_xT(1, 1)
            silu_gate(0, 0)
            copy_s(PRE - 1)
            for n in range(8):
                stage_e(n, n % 4, n // 4, (lambda: copy_s(PRE - 1 + n // 2)) if n and n % 2 == 0 else None)
            with sc.Fori(2, (NSEQ - PRE) // 2) as i:
                for s in range(4):
                    stage_e(i * 4 + s, s, i, None if s % 2 else lambda: copy_s(PRE - 1 + i * 2 + s // 2))
            copy_s(NSEQ - 1)
            with sc.Fori((NSEQ - PRE) // 2, E_NORM) as i:
                for s in range(4):
                    stage_e(i * 4 + s, s, i)

            def tanh_gates(k):
                sc.wait_ge(d_gd, k + 1)
                a.activation(gth[:], gd[:], ACT.Tanh, scale=0.5).then_inc(d_gth, 1)

            sc.wait_ge(sent[0], 16 * HT * TOP0)
            for i in range(E_NORM, N // 4):
                p = i - E_NORM
                turns = [None] * 4 if p < 2 else [lambda: copy_xn(p - 2), lambda: logits_between(p - 2, p - 1), None, None]
                for s in range(4):
                    after = None
                    if s == 3 and p < FSEQ // 2:
                        after = lambda: silu_f(p)
                    stage_e(i * 4 + s, s, i, turns[s], after)
            copy_out(N - 1, 3, N // 4 - 1)

            sc.wait_ge(sent[1], 16 * HT * TOP0)

            def tanh_f(p):
                sc.wait_ge(c_f, 2 * p + 2)
                a.activation(f_act, f_sb, ACT.Tanh, scale=0.5).then_inc(c_fact, 1)

            def tanh_moe(b, first):
                sc.wait_ge(d_moe, b + 1)
                if not first:
                    sc.wait_ge(d_fin, b)
                a.activation(mth[:], bank(3, SEQ), ACT.Tanh, scale=0.5).then_inc(d_mth, 1)

            tanh_gates(0)
            for b in range(NSEQ):
                u = b % 2
                sc.wait_ge(d_qk, b + 1)
                if b:
                    sc.wait_ge(d_s, b)
                for j in range(2):
                    last = a.activation(qk_sb[:, j, :], ps[:, 2, j * SEQ:(j + 1) * SEQ], ACT.Identity,
                                        bias=bqk[:, j:j + 1])
                last.then_inc(d_qks, 1)
                sc.wait_ge(d_v, b + 1)
                if b:
                    sc.wait_ge(d_o, b)
                if turned(b - 2) is not None:
                    copy_gate_logits(turned(b - 2))
                a.copy(v_sb, ps[:, 7, 0:SEQ].rearrange("p (a d) -> p a d", a=2)).then_inc(d_vs, 1)
                sc.wait_ge(d_nmx, b + 1)
                for j in range(2):
                    last = a.activation(pr[:, j, :], ps[:, 6, j * SEQ:(j + 1) * SEQ], ACT.Exp,
                                        bias=nmx[:, j:j + 1], scale=SCALE, accum_out=den[:, j:j + 1])
                last.then_inc(d_p, 1)
                if gated(b) is not None:
                    tanh_gates(gated(b))
                def gelu_hidden():
                    sc.wait_ge(d_h, b + 1)
                    if b >= 2:
                        sc.wait_ge(d_moe, b - 1)
                    a.activation(hg[u], ps[:, 4:6, :].rearrange("p a (b n) -> p (a b) n", b=2),
                                 ACT.Gelu).then_inc(d_hg, 1)

                def copy_turned():
                    sc.wait_ge(d_pT, b + 1)
                    a.copy(pT[:].rearrange("p a b -> p (a b)"), bank(2)).then_inc(d_pTs, 1)
                    if b % NB == 0:
                        sc.wait_ge(d_gT, b // NB + 1)
                        a.copy(gT[b // NB % 2], ps[0:3 * E1, 0:2, :].rearrange("p a n -> p (a n)")).then_inc(d_gTs, 1)

                for step in (copy_turned, gelu_hidden) if b % NB == 0 else (gelu_hidden, copy_turned):
                    step()
                if b:
                    tanh_moe(b - 1, b == 1)
                if turned(b + 1) is not None:
                    tanh_f(turned(b + 1))
                if turned(b - 1) is not None:
                    copy_xn(turned(b - 1))
            tanh_moe(NSEQ - 1, False)

        @block.vector
        def _(dve):
            v = nc.vector
            chain = Chain(dve, dve_link)
            link = chain.link
            v.memset(zeros[:, 0:GW], 0.0).then_inc(zero_set, 1)
            def row_stats(t):
                if t % GT == 0:
                    dve.wait_ge(x_in[t // GT], 16)
                return v.bn_stats(stats[:, t, :], x_tok[:, t, :])

            def norm0(r, beside=None):
                beside = beside or (lambda k: None)
                T0, T1 = r * HT, (r + 1) * HT
                for t in range(max(T0, stats_done), T1):
                    last = row_stats(t)
                    if t % 4 == 3:
                        beside((t - T0) // 4)
                link(last)
                m, va, t = mean[:, T0:T1], var[:, T0:T1], rtmp[:, 0:HT]
                s = stats[:, T0:T1, :]
                link(v.tensor_tensor(t, s[:, :, 1], s[:, :, 4], ALU.subtract))
                v.tensor_tensor(va, s[:, :, 2], s[:, :, 5], ALU.add)
                v.tensor_tensor(m, s[:, :, 1], s[:, :, 4], ALU.add)
                link(v.tensor_tensor(t, t, t, ALU.mult))
                v.tensor_scalar(m, m, 0.5, None, ALU.mult)
                link(v.tensor_scalar(t, t, 0.25, EPS, ALU.mult, ALU.add))
                link(v.scalar_tensor_tensor(out=va, in0=va, scalar=1.0 / P, in1=t, op0=ALU.mult, op1=ALU.add))
                rsqrt_steps(nc, link, rstd[:, T0:T1], va, rtmp[:])
                for t in range(T0, T1):
                    last = v.tensor_scalar(xn_tok[:, t, :], x_tok[:, t, :], mean[:, t:t + 1], rstd[:, t:t + 1],
                                           ALU.subtract, ALU.mult)
                    if t % GT == GT - 1:
                        last.then_inc(xn_ready, 1)
                        beside(4 + (t - T0) // 4)

            def route(r, beside=None):
                beside = beside or (lambda k: None)
                T0 = r * HT
                oh4 = onehot[:].rearrange("p (t k) e -> p t k e", k=TOP0)
                tf4 = top_f[:].rearrange("p (t k) -> p t k", k=TOP0)
                experts = iota_e[:].rearrange("p (a e) -> p a e", a=1).to_broadcast([P, GT * TOP0, E0])
                for g in range(HT // GT):
                    tiles = slice(g * GT, (g + 1) * GT)
                    rows_g = slice(g * GT * TOP0, (g + 1) * GT * TOP0)
                    dve.wait_ge(lg_sb, r * HT // GT + g + 1)
                    for t in range(g * GT, (g + 1) * GT):
                        last = v.max(top8[:, t, :], logits[:, T0 + t, 0:E0])
                    link(last)
                    for t in range(g * GT, (g + 1) * GT):
                        last = v.max_index(top8_i[:, t, :], top8[:, t, :], logits[:, T0 + t, 0:E0])
                    link(last)
                    if g == HT // GT - 1:
                        v.tensor_tensor(tw[:], top8[:, :, 0:TOP0], top8[:, :, 0:1].to_broadcast([P, HT, TOP0]),
                                        ALU.subtract).then_inc(tw_in, 1)
                    link(v.tensor_copy(tf4[:, tiles, :], top8_i[:, tiles, 0:TOP0]))
                    link(v.tensor_tensor(onehot[:, rows_g, :], experts, top_f[:, rows_g]
                                         .rearrange("p (t a) -> p t a", a=1).to_broadcast([P, GT * TOP0, E0]),
                                         ALU.is_equal))
                    with nc.allow_low_precision("sums of one 1 and zeros"):
                        last = v.tensor_reduce(mask[:, tiles, :], oh4[:, tiles, :, :].rearrange("p t k e -> p t e k"),
                                               AX.X, ALU.add)
                    if g == HT // GT - 1:
                        last.then_inc(mask_ready, 1)
                    beside(g)
                dve.wait_ge(tw_exp, r + 1)
                link(v.tensor_reduce(tsum[:], tw[:], AX.X, ALU.add))
                link(v.reciprocal(tsum[:], tsum[:]))
                v.tensor_tensor(top_w[:, T0 * TOP0:(T0 + HT) * TOP0].rearrange("p (t k) -> p t k", k=TOP0), tw[:],
                                tsum[:].rearrange("p (t a) -> p t a", a=1).to_broadcast([P, HT, TOP0]), ALU.mult)
                dve.wait_ge(rank_ps, r + 1)
                link(v.tensor_copy(tot_em, bank(7).rearrange("p (t e) -> p e t", t=HT)))
                link(v.tensor_tensor_scan(cum_em.rearrange("p e t -> p (e t)"), not_first.rearrange("p e t -> p (e t)"),
                                          tot_em.rearrange("p e t -> p (e t)"), 0.0, ALU.mult, ALU.add))
                beside(4)
                link(v.tensor_scalar(cnt_i[:], cum_em[:, :, HT - 1], float(P - 1), None, ALU.add))
                link(v.tensor_scalar(cnt_i[:], cnt_i[:], 7, None, ALU.logical_shift_right))
                link(v.tensor_copy(tiles_e[:], cnt_i[:]))
                link(v.tensor_tensor_scan(tile_end[:], ones[:, 0:E0], tiles_e[:], 0.0, ALU.mult, ALU.add))
                link(v.tensor_scalar(tile_cmp[0:ST, :], tile_end[0:ST, :], iota_p[0:ST, 0:1], None, ALU.is_le))
                link(v.tensor_reduce(tile_ex[0:ST, :], tile_cmp[0:ST, :], AX.X, ALU.add))
                v.tensor_scalar(tile_ex[0:ST, :], tile_ex[0:ST, :], float(E0 - 1), None, ALU.min).then_inc(ex_ready, 1)
                beside(5)
                link(v.tensor_tensor(tiles_e[:], tile_end[:], tiles_e[:], ALU.subtract))
                link(v.tensor_scalar(tiles_e[:], tiles_e[:], float(P), None, ALU.mult))
                link(v.tensor_tensor(cum_em, cum_em,
                                     tiles_e[:].rearrange("p (e a) -> p e a", a=1).to_broadcast([P, E0, HT]), ALU.add))
                link(v.tensor_tensor(pos, bank(6).rearrange("p (t e) -> p t e", t=HT),
                                     cum_em.rearrange("p e t -> p t e"), ALU.add))
                for c, (a, b) in enumerate(((0, GT), (GT, HT))):
                    for k in range(TOP0):
                        last = v.tensor_tensor(oh4[:, a:b, k, :], oh4[:, a:b, k, :], pos[:, a:b, :], ALU.mult)
                    link(last)
                    beside(6 + c)
                    of = slice(a * TOP0, b * TOP0)
                    link(v.tensor_reduce(top_f[:, of], onehot[:, of, :], AX.X, ALU.add))
                    sl = slot_of[:, (T0 + a) * TOP0:(T0 + b) * TOP0]
                    link(v.tensor_copy(slot_i[:, of], top_f[:, of]))
                    v.tensor_scalar(sl, slot_i[:, of], 9, 9, ALU.logical_shift_right, ALU.logical_shift_left)
                    link(v.tensor_scalar(slot_a[:, of], slot_i[:, of], P - 1, 2, ALU.bitwise_and, ALU.logical_shift_left))
                    link(v.tensor_tensor(sl, sl, slot_a[:, of], ALU.add))
                    link(v.tensor_scalar(slot_a[:, of], slot_i[:, of], 7, GT - 1, ALU.logical_shift_right, ALU.bitwise_and))
                    v.tensor_tensor(sl, sl, slot_a[:, of], ALU.add).then_inc(slots_ready, 1)
                dve.wait_ge(exT_row, r + 1)
                v.tensor_copy(tile_expert[:, r * ST:(r + 1) * ST], ps[0:1, 7, 0:ST]).then_inc(routed, 1)

            dve.wait_ge(phz_in, 64)
            stats_done = HT - 2
            lk = chain.link_beside(row_stats, stats_done)
            lk(v.tensor_tensor(cs[:, 9:10], phz[:, 1:2], phz[:, 1:2], ALU.mult))
            lk(v.scalar_tensor_tensor(out=cs[:, 0:1], in0=phz[:, 0:1], scalar=phz[:, 0:1], in1=cs[:, 9:10],
                                        op0=ALU.mult, op1=ALU.add))
            rsqrt_steps(nc, lk, cs[:, 13:14], cs[:, 0:1], cs[:, 14:16])
            v.tensor_scalar(cs[:, 1:3], phz[:, 0:2], cs[:, 13:14], None, ALU.mult)
            lk(v.tensor_tensor(cs[:, 3:4], cs[:, 0:1], cs[:, 13:14], ALU.mult))
            v.tensor_scalar(cs[:, 3:4], cs[:, 3:4], -1.0, None, ALU.mult).then_inc(mag_ready, 1)

            norm0(0)
            v.memset(ones_bf[:], 1.0)
            v.memset(ones[:], 1.0)
            link(v.memset(not_first, 1.0))
            link(v.memset(not_first[:, :, 0:1], 0.0))
            dve.wait_ge(pool_c, 7)
            route(0)

            def shared_hidden(it):
                u = it % 2
                dve.wait_ge(sh_silu, it + 1)
                if it >= 2:
                    dve.wait_ge(sh_dn, it - 1)
                v.tensor_tensor(hs_h[u][:].rearrange("p a t -> p (a t)"), hs_t[u][:].rearrange("p a t -> p (a t)"),
                                bank(2 * u + 1), ALU.mult).then_inc(sh_hid, 1)

            def shared_gated(it):
                dve.wait_ge(sh_dn, it + 1)
                v.tensor_tensor(sh_tok[:, it * 2:it * 2 + 2, :],
                                ps[:, 4 + it % 2, 0:SEQ].rearrange("p (a d) -> p a d", a=2),
                                sh_gate_t[:, it * 2:it * 2 + 2].rearrange("p (n a) -> p n a", a=1)
                                .to_broadcast([P, 2, P]), ALU.mult).then_inc(sh_done, 1)

            def shared_step(it):
                shared_hidden(it)
                if it % HS:
                    shared_gated(it - 1)

            def twice(row):
                return row.rearrange("p (a t) -> p a t", a=1).to_broadcast([P, 2, SEQ])

            def recurrence(it, turn):
                xg = xnT[:, bass.ds(it * SEQ, SEQ)]
                flat = rec[:].rearrange("p a t -> p (a t)")
                if turn == 0:
                    if not (isinstance(it, int) and it == 0):
                        dve.wait_ge(recurred, it)
                    link(v.tensor_tensor(rec[:], twice(xg), trig[:, :, 0:SEQ], ALU.mult))
                    link(v.tensor_tensor_scan(flat, decay[:].rearrange("p a t -> p (a t)"), flat, 0.0,
                                              ALU.mult, ALU.add))
                    link(v.tensor_tensor(rec[:], rec[:], out_cs[:], ALU.mult))
                else:
                    link(v.tensor_tensor(rec[:, 0, :], rec[:, 0, :], rec[:, 1, :], ALU.add))
                    if not (isinstance(it, int) and it == 0):
                        dve.wait_ge(s_ps, it)
                    v.tensor_tensor(s_rec[:], rec[:, 0, :], past[:], ALU.add).then_inc(recurred, 1)

            HS = NSEQ // NH
            dve.wait_ge(sh_gated, 1)
            norm0(1, lambda k: shared_step(k))
            shared_gated(HS - 1)
            dve.wait_ge(tables, 1)
            for b in range(PRE - 2):
                recurrence(b, 0)
                recurrence(b, 1)
            dve.wait_ge(sh_gated, 2)
            route(1, lambda k: shared_step(HS + k))
            shared_gated(NSEQ - 1)

            def hidden(n, u):
                dve.wait_ge(e_sg, n + 1)
                if not (isinstance(n, int) and n < 2):
                    dve.wait_ge(e_aT, n - 1)
                v.tensor_tensor(act[u][:].rearrange("p (a b) i -> p a b i", a=2),
                                sg[u][:].rearrange("p (a b) i -> p a b i", a=2),
                                ps[:, 1 + 2 * u:3 + 2 * u, :].rearrange("p a (b i) -> p a b i", b=2)[:, :, :, I0:2 * I0],
                                ALU.mult).then_inc(e_act, 1)

            def sum_step(b, u, fills, n, marks):
                w, j, k = f_w[u % 2], n % 2, n // 2
                if n == 0:
                    link(v.tensor_copy(w[:], top_w[:, b * 2 * TOP0:(b + 1) * 2 * TOP0]))
                    dve.wait_ge(g_in[u], 16 * 2 * TOP0 * fills)
                into = f_sb[:, 2 * (u % 2) + j, :]
                if k:
                    chain.after(marks[n - 2])
                ins = v.scalar_tensor_tensor(out=into, in0=gath[u][:, j * TOP0 + k, :],
                                             scalar=w[:, j * TOP0 + k:j * TOP0 + k + 1],
                                             in1=into if k else sh_tok[:, b * 2 + j, :], op0=ALU.mult, op1=ALU.add)
                if k < TOP0 - 1:
                    marks.append(chain.mark(ins))
                elif j:
                    ins.then_inc(c_f, 1)

            def sum_experts(b, u, fills):
                marks = []
                for n in range(2 * TOP0):
                    sum_step(b, u, fills, n, marks)

            def row(b, j):
                return x_tok[:, b * 2 + j, :]

            def mix(p, tanh):
                dve.wait_ge(c_fact, p + 1)
                if tanh:
                    link(v.scalar_tensor_tensor(out=f_sb, in0=f_act, scalar=1.0, in1=f_sb, op0=ALU.add, op1=ALU.mult))
                dve.wait_ge(s_tok, NSEQ)
                link(v.tensor_tensor(f_sb, f_sb if tanh else f_act, xnT[:, p * 2 * SEQ:(p + 1) * 2 * SEQ]
                                     .rearrange("p (a d) -> p a d", d=P), ALU.mult))
                xb = x_tok[:, p * 4:(p + 1) * 4, :]
                link(v.scalar_tensor_tensor(out=xb, in0=f_sb, scalar=0.5 if tanh else 1.0, in1=xb,
                                            op0=ALU.mult, op1=ALU.add))

            def stats1(p):
                for j in range(4):
                    last = v.bn_stats(st1[:, j, :], row(p * 2, j))
                link(last)
                for j in range(4):
                    last = v.bn_aggr(mv1[:, j, :], st1[:, j, :])
                link(last)

            def rstd1(summed=None):
                marks = []
                lk = link if summed is None else chain.link_beside(lambda n: sum_step(*summed, n, marks), 2 * TOP0)
                lk(v.tensor_scalar(v1[:], mv1[:, :, 1], EPS, None, ALU.add))
                rsqrt_steps(nc, lk, r1[:], v1[:], t1[:])

            def norm1(p):
                if p:
                    dve.wait_ge(c_xnT, p)
                for j in range(4):
                    last = v.tensor_scalar(xn1[:, j, :], row(p * 2, j), mv1[:, j, 0:1], r1[:, j:j + 1],
                                           ALU.subtract, ALU.mult)
                last.then_inc(c_xn, 1)

            N = NH * SG
            for b in range(PRE - 2, PRE):
                recurrence(b, 0)
                recurrence(b, 1)
            hidden(0, 0)
            start = chain.n
            recurrence(PRE, 0)
            hidden(1, 1)
            recurrence(PRE, 1)
            hidden(2, 0)
            per = chain.n - start
            with dve.Fori(1, NSEQ - PRE) as i:
                chain.n, chain.base = start, i * per
                recurrence(i + PRE, 0)
                hidden(i * 2 + 1, 1)
                recurrence(i + PRE, 1)
                hidden(i * 2 + 2, 0)
            chain.n, chain.base = start + (NSEQ - PRE) * per, 0
            with dve.Fori(NSEQ - PRE, 2 * E_NORM) as i:
                for s in range(2):
                    hidden(i * 2 + s + 1, 1 - s)

            def gating(k):
                def each(w):
                    return w.rearrange("p (t a) -> p t a", a=1).to_broadcast([P, BT, E1])

                experts = iota_e[:, 0:E1].rearrange("p (a e) -> p a e", a=1).to_broadcast([P, BT, E1])
                dve.wait_ge(c_lgs, (k + 1) * NB // 2)
                for t in range(BT):
                    last = v.max(g8[:, t, :], lg1[:, k * BT + t, :])
                link(last)
                for t in range(BT):
                    last = v.max_index(g8_i[:, t, :], g8[:, t, :], lg1[:, k * BT + t, :])
                link(last)
                v.tensor_tensor(gd[:], g8[:, :, 0], g8[:, :, 1], ALU.subtract).then_inc(d_gd, 1)
                link(v.tensor_copy(g8_f[:], g8_i[:, :, 0:2]))
                v.tensor_tensor(gates[:], experts, each(g8_f[:, :, 0]), ALU.is_equal)
                link(v.tensor_tensor(gates2[:], experts, each(g8_f[:, :, 1]), ALU.is_equal))
                dve.wait_ge(d_gth, k + 1)
                v.tensor_scalar(gw2[:, :, 0], gth[:], 0.5, 0.5, ALU.mult, ALU.add)
                link(v.tensor_scalar(gw2[:, :, 1], gth[:], -0.5, 0.5, ALU.mult, ALU.add))
                v.tensor_tensor(gates[:], gates[:], each(gw2[:, :, 0]), ALU.mult)
                link(v.tensor_tensor(gates2[:], gates2[:], each(gw2[:, :, 1]), ALU.mult))
                link(v.tensor_tensor(gates[:], gates[:], gates2[:], ALU.add))
                if k:
                    dve.wait_ge(d_gT, k)
                with nc.allow_low_precision("three bfloat16 parts hold a float32 exactly"):
                    link(v.tensor_copy(gate_parts[:, :, 0, :], gates[:]))
                    link(v.tensor_tensor(gates[:], gates[:], gate_parts[:, :, 0, :], ALU.subtract))
                    link(v.tensor_copy(gate_parts[:, :, 1, :], gates[:]))
                    v.tensor_tensor(gate_parts[:, :, 2, :], gates[:], gate_parts[:, :, 1, :],
                                    ALU.subtract).then_inc(d_gate, 1)

            for i in range(E_NORM, N // 4):
                p, n = i - E_NORM, 4 * i
                summed = [(2 * p + k, 2 * (p % 2) + k, p // 2 + 1) for k in range(2)]
                more = p < FSEQ // 2
                if p:
                    mix(p - 1, False)
                hidden(n + 1, 1)
                if p:
                    stats1(p - 1)
                hidden(n + 2, 0)
                if p:
                    rstd1(summed[0] if more else None)
                else:
                    sum_experts(*summed[0])
                hidden(n + 3, 1)
                if p:
                    norm1(p - 1)
                if more:
                    sum_experts(*summed[1])
                    hidden(n + 4, 0)
            gating(0)

            def finish(b, u, first, used):
                dve.wait_ge(d_mth, b + 1)
                link(v.scalar_tensor_tensor(out=mg[:].rearrange("p a d -> p (a d)"), in0=mth[:], scalar=1.0,
                                            in1=bank(3, SEQ), op0=ALU.add, op1=ALU.mult))
                dve.wait_ge(d_os, b + 1)
                link(v.tensor_tensor(mg[:], mg[:], o_sb[u][:], ALU.mult))
                if not first:
                    dve.wait_ge(stored[u], 16 * used)
                v.scalar_tensor_tensor(out=fin[u], in0=mg[:], scalar=0.5, in1=x_tok[:, bass.ds(b * 2, 2), :],
                                       op0=ALU.mult, op1=ALU.add).then_inc(d_fin, 1)

            for b in range(NSEQ):
                u = b % 2
                dve.wait_ge(d_s, b + 1)
                link(v.tensor_reduce(mx[:], ps[:, 6, :].rearrange("p (a n) -> p a n", a=2), AX.X, ALU.max))
                v.tensor_scalar(nmx[:], mx[:], -SCALE, None, ALU.mult).then_inc(d_nmx, 1)
                if gated(b) is not None:
                    gating(gated(b))
                summed = (b - 2 + FSEQ, u, (b - 2) // 2 + FSEQ // 4 + 1) if 2 <= b < 2 + NSEQ - FSEQ else None
                if turned(b) is not None:
                    rstd1(summed)
                elif summed is not None:
                    sum_experts(*summed)
                dve.wait_ge(d_p, b + 1)
                link(v.reciprocal(rden[:], den[:]))
                dve.wait_ge(d_gb, b + 1)
                dve.wait_ge(d_hg, b + 1)
                v.tensor_tensor(hg[u], hg[u], ps[:, 0:2, :].rearrange("p a (b n) -> p (a b) n", b=2),
                                ALU.mult).then_inc(d_hs, 1)
                if b:
                    finish(b - 1, 1 - u, b <= 2, (b - 1) // 2)
                dve.wait_ge(d_o, b + 1)
                for j in range(2):
                    last = v.scalar_tensor_tensor(out=o_sb[u][:, j, :], in0=ps[:, 6, j * P:(j + 1) * P],
                                                  scalar=rden[:, j:j + 1], in1=bv_all[:], op0=ALU.mult, op1=ALU.add)
                last.then_inc(d_os, 1)
                if turned(b) is not None:
                    norm1(turned(b))
                if turned(b + 1) is not None:
                    mix(turned(b + 1), True)
                    stats1(turned(b + 1))
            finish(NSEQ - 1, 1, False, NSEQ // 2 - 1)


_INS = ['L0_attn_x', 'L0_attn_phazor', 'L0_attn_phazor_init', 'L0_attn_last_conv_re', 'L0_attn_last_conv_im',
        'L0_ffn_router_w', 'L0_ffn_w_gate', 'L0_ffn_w_up', 'L0_ffn_w_down', 'L0_ffn_sh_gate', 'L0_ffn_sh_up',
        'L0_ffn_sh_down', 'L0_ffn_sh_gate_w', 'L1_attn_wq', 'L1_attn_bq', 'L1_attn_wk', 'L1_attn_bk',
        'L1_attn_wv', 'L1_attn_bv', 'L1_ffn_w_gate', 'L1_ffn_w_fc', 'L1_ffn_w_proj']
_OUTS = [((NSEQ, SEQ, P), 'float32')]


def kernel(**inputs):
    import numpy as _np
    import concourse.bacc as _bacc
    from concourse import mybir as _mybir
    from concourse.bass_utils import run_bass_kernel_spmd as _run

    nc = _bacc.Bacc("TRN2", target_bir_lowering=False, num_devices=1)
    arrays, args = {}, []
    for name in _INS:
        a = _np.ascontiguousarray(inputs[name])
        arrays[f"in_{name}_dram"] = a
        args.append(nc.dram_tensor(f"in_{name}_dram", a.shape, _mybir.dt.from_np(a.dtype), kind="ExternalInput").ap())
    for i, (shape, dtype) in enumerate(_OUTS):
        dt = _mybir.dt.from_np(_np.dtype(dtype))
        args.append(nc.dram_tensor(f"out_{i}_dram", shape, dt, kind="ExternalOutput").ap())
    build(nc, *args)
    r = _run(nc, [arrays], core_ids=[0])
    got = tuple(r.results[0][f"out_{i}_dram"] for i in range(len(_OUTS)))
    return got[0]
```

```python
from contextlib import ExitStack

import concourse.bass as bass
from concourse import mybir

ALU = mybir.AluOpType
ACT = mybir.ActivationFunctionType
AX = mybir.AxisListType
F32 = mybir.dt.float32
BF16 = mybir.dt.bfloat16
I32 = mybir.dt.int32
U32 = mybir.dt.uint32

P = 128
SEQ = 256
NSEQ = 16
NT = NSEQ * SEQ // P
GT = 4
NG = NT // GT
GW = GT * P
E0, I0, TOP0 = 32, 96, 4
ISH = 256
E1, I1 = 8, 64
CH1 = E1 * I1 // P
NH = 2
HT = NT // NH
ST = -(-(HT * P * TOP0 + E0 * (P - 1)) // P // GT) * GT
SG = ST // GT
FSEQ = NSEQ // 2
NORM_AT = {-1: 3, 3: 4, 5: 5, 8: 6, 10: 7}
BATCHES = ((0, 2), (2, 2), (4, 1), (5, 1), (6, 1), (7, 1))
BT = 8
PRE = 2
EPS = 1e-5
SCALE = float(P) ** -0.5


class Chain:

    def __init__(self, eng, sem):
        self.eng, self.sem, self.n, self.base = eng, sem, 0, 0

    def mark(self, ins):
        self.n += 1
        ins.then_inc(self.sem, 1)
        return self.base + self.n

    def after(self, mark):
        self.eng.wait_ge(self.sem, mark)

    def link(self, ins):
        self.after(self.mark(ins))

    def link_beside(self, step, count):
        done = [0]

        def link(ins):
            m = self.mark(ins)
            if done[0] < count:
                step(done[0])
                done[0] += 1
            self.after(m)
        return link


def turned(b):
    return NORM_AT.get(b)


def summed(b):
    for ahead in (2, 1):
        if b >= 0 and turned(b + ahead) is not None:
            return 2 * turned(b + ahead) + 2 - ahead
    return None


def gated(b):
    if b == -1:
        return 0
    for k, (first, count) in enumerate(BATCHES[1:], 1):
        if turned(b - 2) == first + count - 1:
            return k
    return None


def batch_of(b):
    for k, (first, count) in enumerate(BATCHES):
        if first <= b // 2 < first + count:
            return k, b - 2 * first


def rsqrt_steps(nc, link, y, v, h):
    w = y.shape[-1]
    yi, vi, half, t = y.bitcast(I32), v.bitcast(I32), h[:, 0:w], h[:, w:2 * w]
    link(nc.vector.tensor_scalar(yi, vi, 1, None, ALU.logical_shift_right))
    nc.vector.tensor_scalar(half, v, -0.5, None, ALU.mult)
    link(nc.vector.tensor_scalar(yi, yi, -1.0, float(0x5F3759DF), ALU.mult, ALU.add))
    for _ in range(3):
        link(nc.vector.tensor_tensor(t, y, y, ALU.mult))
        link(nc.vector.tensor_tensor(t, t, half, ALU.mult))
        link(nc.vector.scalar_tensor_tensor(out=y, in0=t, scalar=1.5, in1=y, op0=ALU.add, op1=ALU.mult))


def build(nc, x, phazor, phazor_init, last_re, last_im, router_w, w_gate, w_up, w_down, sh_gate, sh_up,
          sh_down, sh_gate_w, wq, bq, wk, bk, wv, bv, w_gate1, w_fc, w_proj, out):
    slot_rows = [nc.dram_tensor(f"slot_rows{r}", [ST * P, P], F32, kind="Internal").ap() for r in range(NH)]
    expert_rows = [nc.dram_tensor(f"expert_rows{r}", [ST * P, P], F32, kind="Internal").ap() for r in range(NH)]
    slot_groups = [t.rearrange("(g p j) d -> g p (j d)", p=P, j=GT) for t in slot_rows]
    expert_groups = [t.rearrange("(g p j) d -> g p (j d)", p=P, j=GT) for t in expert_rows]
    x_rows = x.rearrange("b (t p) d -> p (b t) d", p=P)
    out_rows = out.rearrange("b (t p) d -> b p t d", p=P)

    ctx = ExitStack()
    with ctx:
        def sb(name, shape, dt=F32):
            return ctx.enter_context(nc.sbuf_tensor(name, shape, dt))

        def sem(name):
            return ctx.enter_context(nc.semaphore(name))

        x_tok = sb("x_tok", [P, NT, P])
        xn_tok = sb("xn_tok", [P, NT, P])
        xnT = sb("xnT", [P, NT * P])
        sh_tok = sb("sh_tok", [P, NT, P])
        w_gu = sb("w_gu", [P, E0, 2 * I0])
        w_dn = sb("w_dn", [I0, E0 * P])
        logits = sb("logits", [P, NT, E0 + 1])
        top_w = sb("top_w", [P, NT * TOP0])
        slot_of = sb("slot_of", [P, NT * TOP0], I32)
        tile_expert = sb("tile_expert", [1, NH * ST], I32)
        ident = sb("ident", [P, P])
        ones = sb("ones", [P, P])
        rw = sb("rw", [P, E0 + 1])
        shg = sb("shg", [P, ISH])
        shu = sb("shu", [P, ISH])
        shd = sb("shd", [P, ISH // P, P])
        sh_gate_t = sb("sh_gate_t", [P, NT])
        raw1 = sb("raw1", [P, 3, P])
        raw_fc = sb("raw_fc", [P, CH1, P])
        raw_pr = sb("raw_pr", [P, E1, I1])
        raw_g1 = sb("raw_g1", [E1, P])
        w1T = sb("w1T", [P, 3, P])
        fcT = sb("fcT", [P, CH1, P])
        prT = sb("prT", [P, CH1, P])
        g1T = sb("g1T", [P, E1])
        bqk = sb("bqk", [P, 2])
        bv_r = sb("bv_r", [1, P])
        bv_all = sb("bv_all", [P, P])
        expert_sel = sb("expert_sel", [3 * E1, CH1, P], BF16)
        ident_bf = sb("ident_bf", [P, P], BF16)
        zeros = sb("zeros", [P, 2048])
        iota_e = sb("iota_e", [P, E0])
        iota_t1 = sb("iota_t1", [P, SEQ])
        iota_p = sb("iota_p", [P, 1])
        not_before = sb("not_before", [P, P], BF16)
        ones_bf = sb("ones_bf", [P, P], BF16)
        phz = sb("phz", [P, 6])
        cs = sb("cs", [P, 20])
        trig = sb("trig", [P, 2, SEQ + 1])
        out_cs = sb("out_cs", [P, 2, SEQ])
        past = sb("past", [P, SEQ])
        decay_t1 = sb("decay_t1", [P, SEQ])
        decay = sb("decay", [P, 2, SEQ])
        tab_tmp = sb("tab_tmp", [P, SEQ])
        stats = sb("stats", [P, NT, 6])
        mean = sb("mean", [P, NT])
        var = sb("var", [P, NT])
        rstd = sb("rstd", [P, NT])
        rtmp = sb("rtmp", [P, 2 * NT])
        top8 = sb("top8", [P, HT, 8])
        top8_i = sb("top8_i", [P, HT, 8], U32)
        top_f = sb("top_f", [P, HT * TOP0])
        tw = sb("tw", [P, HT, TOP0])
        tsum = sb("tsum", [P, HT])
        onehot = sb("onehot", [P, HT * TOP0, E0])
        mask = sb("mask", [P, HT, E0], BF16)
        route_tmp = sb("route_tmp", [P, 4, HT * E0])
        tot_em = route_tmp[:, 0, :].rearrange("p (e t) -> p e t", e=E0)
        cum_em = route_tmp[:, 1, :].rearrange("p (e t) -> p e t", e=E0)
        pos = route_tmp[:, 2, :].rearrange("p (t e) -> p t e", t=HT)
        not_first = route_tmp[:, 3, :].rearrange("p (e t) -> p e t", e=E0)
        cnt_i = sb("cnt_i", [P, E0], I32)
        tiles_e = sb("tiles_e", [P, E0])
        tile_end = sb("tile_end", [P, E0])
        tile_cmp = sb("tile_cmp", [P, E0])
        tile_ex = sb("tile_ex", [P, 1])
        slot_i = sb("slot_i", [P, HT * TOP0], I32)
        slot_a = sb("slot_a", [P, HT * TOP0], I32)
        hs_t = [sb(f"hs_t{u}", [P, 2, SEQ]) for u in range(2)]
        hs_h = [sb(f"hs_h{u}", [P, 2, SEQ]) for u in range(2)]
        rec = sb("rec", [P, 2, SEQ])
        rows_4 = sb("rows_4", [P, 4, GT * P])
        rows = [rows_4[:, u, :] for u in range(4)]
        eo = [zeros[:, u * GT * P:(u + 1) * GT * P] for u in range(4)]
        exT = [raw_fc[:].rearrange("p c d -> p (c d)"), raw_pr[:].rearrange("p e i -> p (e i)")]
        sg = [sb(f"sg{u}", [P, GT, I0]) for u in range(2)]
        act = [sb(f"act{u}", [P, GT, I0]) for u in range(2)]
        actT = [sb(f"actT{u}", [I0, GT * P]) for u in range(2)]
        gath = [buf[:, u * 2 * TOP0 * P:(u + 1) * 2 * TOP0 * P].rearrange("p (n d) -> p n d", d=P)
                for buf in (onehot[:].rearrange("p n e -> p (n e)"), route_tmp[:].rearrange("p a n -> p (a n)"))
                for u in range(2)]
        hg = [rows_4[:, 2 * u:2 * u + 2, :].rearrange("p a (b n) -> p (a b) n", n=SEQ) for u in range(2)]
        s_rec = tab_tmp
        xn1 = rec[:].rearrange("p c (a d) -> p (c a) d", d=P)
        xn1T = [hs_t[0][:, u, :] for u in range(2)]
        xn1T_pair = decay[:].rearrange("p a t -> p (a t)")
        f_sb = trig[:].rearrange("p a t -> p (a t)")[:, 0:2 * SEQ].rearrange("p (a d) -> p a d", d=P)
        f_act = out_cs[:].rearrange("p c (a d) -> p (c a) d", d=P)
        f_w = [sb(f"f_w{u}", [P, 2 * TOP0]) for u in range(2)]
        st1 = sb("st1", [P, 4, 6])
        mv1 = sb("mv1", [P, 4, 2])
        v1 = sb("v1", [P, 4])
        r1 = sb("r1", [P, 4])
        t1 = sb("t1", [P, 8])
        qk_sb = hs_h[0]
        v_sb = decay_t1[:].rearrange("p (a d) -> p a d", a=2)
        lg1 = sb("lg1", [P, NT, E1])
        g8, g8_i = top8[:, 0:BT, :], top8_i[:, 0:BT, :]
        g8_f = sb("g8_f", [P, BT, 2])
        gd = sb("gd", [P, BT])
        gth = sb("gth", [P, BT])
        gw2 = sb("gw2", [P, BT, 2])
        gates = sb("gates", [P, BT, E1])
        gates2 = sb("gates2", [P, BT, E1])
        gate_parts = sb("gate_parts", [P, BT, 3, E1], BF16)
        gT = [logits[:].rearrange("p t e -> p (t e)").bitcast(BF16)[0:3 * E1, u * BT * P:(u + 1) * BT * P]
              for u in range(2)]
        mx = sb("mx", [P, 2])
        nmx = sb("nmx", [P, 2])
        den = sb("den", [P, 2])
        rden = sb("rden", [P, 2])
        pr = hs_h[1]
        pT = hs_t[1]
        mth = sb("mth", [P, SEQ])
        mg = sb("mg", [P, 2, P])
        o_sb = [sb(f"o_sb{u}", [P, 2, P]) for u in range(2)]
        fin = [raw_fc[:, 2 * u:2 * u + 2, :] for u in range(2)]

        ps = ctx.enter_context(nc.psum_tensor("ps", [P, 8, 512], F32))

        def bank(n, width=512):
            return ps[:, n, 0:width]

        x_in = [sem(f"x_in{g}") for g in range(NG)]
        phz_in = sem("phz_in")
        rw_in = sem("rw_in")
        w_in = sem("w_in")
        we_in = sem("we_in")
        zero_set = sem("zero_set")
        filled = [sem(f"filled{r}") for r in range(NH)]
        pool_c = sem("pool_c")
        sel_in = sem("sel_in")
        dve_link = sem("dve_link")
        act_link = sem("act_link")
        pool_link = sem("pool_link")
        wT_ps = sem("wT_ps")
        wT_sb = sem("wT_sb")
        xn_ready = sem("xn_ready")
        xT_ps = sem("xT_ps")
        xT_sb = sem("xT_sb")
        lg_ps = sem("lg_ps")
        lg_sb = sem("lg_sb")
        tw_in = sem("tw_in")
        tw_exp = sem("tw_exp")
        mask_ready = sem("mask_ready")
        rank_ps = sem("rank_ps")
        ex_ready = sem("ex_ready")
        exT_row = sem("exT_row")
        routed = sem("routed")
        slots_ready = sem("slots_ready")
        sent = [sem(f"sent{r}") for r in range(NH)]
        mag_ready = sem("mag_ready")
        tables = sem("tables")
        exp_ready = sem("exp_ready")
        sh_ps = sem("sh_ps")
        sh_silu = sem("sh_silu")
        sh_gated = sem("sh_gated")
        sh_hid = sem("sh_hid")
        sh_dn = sem("sh_dn")
        sh_done = sem("sh_done")
        recurred = sem("recurred")
        s_ps = sem("s_ps")
        s_tok = sem("s_tok")
        rows_in = [sem(f"rows_in{u}") for u in range(4)]
        e_xT = sem("e_xT")
        e_xTs = sem("e_xTs")
        e_gu = sem("e_gu")
        e_sg = sem("e_sg")
        e_act = sem("e_act")
        e_aT = sem("e_aT")
        e_aTs = sem("e_aTs")
        e_dn = sem("e_dn")
        e_out = sem("e_out")
        e_stored = [sem(f"e_stored{u}") for u in range(4)]
        g_in = [sem(f"g_in{u}") for u in range(4)]
        xr_in = [sem(f"xr_in{u}") for u in range(2)]
        c_f = sem("c_f")
        c_fact = sem("c_fact")
        c_xn = sem("c_xn")
        c_xnT = sem("c_xnT")
        c_xn_kept = sem("c_xn_kept")
        c_lg = sem("c_lg")
        c_lgs = sem("c_lgs")
        d_qk = sem("d_qk")
        d_v = sem("d_v")
        d_h = sem("d_h")
        d_qks = sem("d_qks")
        d_vs = sem("d_vs")
        d_hg = sem("d_hg")
        d_gd = sem("d_gd")
        d_gth = sem("d_gth")
        d_gate = sem("d_gate")
        d_gT = sem("d_gT")
        d_gTs = sem("d_gTs")
        d_gb = sem("d_gb")
        d_hs = sem("d_hs")
        d_s = sem("d_s")
        d_nmx = sem("d_nmx")
        d_p = sem("d_p")
        d_pT = sem("d_pT")
        d_pTs = sem("d_pTs")
        d_o = sem("d_o")
        d_os = sem("d_os")
        d_moe = sem("d_moe")
        d_mth = sem("d_mth")
        d_fin = sem("d_fin")
        stored = [sem(f"stored{u}") for u in range(2)]

        N_W = 12
        N_FILL = 6
        RANKS_AFTER, IDS_AFTER = 2, 4
        E_NORM = NH * SG // 4 - FSEQ // 2 - 1

        assert E_NORM == (NSEQ - PRE) // 2

        def norm_step(n):
            since = n - (NH * SG + 1 - 5 * FSEQ // 2)
            return (since // 5, since % 5) if since >= 0 else (0, -1)
        block = ctx.enter_context(nc.Block())

        @block.sync
        def _(sp):
            for t, (a, b, src) in enumerate(((0, 2, phazor), (2, 4, phazor_init),
                                             (4, 5, last_re.rearrange("(d a) -> d a", a=1)),
                                             (5, 6, last_im.rearrange("(d a) -> d a", a=1)))):
                sp.dma_start(phz[:, a:b], src).then_inc(phz_in, 16)
            for g in range(NG):
                sp.dma_start(x_tok[:, g * GT:(g + 1) * GT, :],
                             x_rows[:, g * GT:(g + 1) * GT, :]).then_inc(x_in[g], 16)
            sp.dma_start(rw[:, 0:E0], router_w).then_inc(rw_in, 16)
            sp.dma_start(rw[:, E0:E0 + 1], sh_gate_w).then_inc(rw_in, 16)
            n = 0
            for dst, src in (
                (raw_g1[:], w_gate1),
                (shg[:], sh_gate),
                (shu[:], sh_up),
                (shd[:], sh_down.rearrange("(c p) h -> p c h", p=P)),
                (raw1[:, 0, :], wq),
                (raw1[:, 1, :], wk),
                (raw1[:, 2, :], wv),
                (bqk[:, 0:1], bq.rearrange("(d a) -> d a", a=1)),
                (bqk[:, 1:2], bk.rearrange("(d a) -> d a", a=1)),
                (bv_r[:], bv.rearrange("(a d) -> a d", a=1)),
                (raw_fc[:], w_fc.rearrange("(c e) i h -> (e i) c h", c=CH1)),
                (raw_pr[:], w_proj.rearrange("e h i -> h e i")),
            ):
                sp.dma_start(dst, src).then_inc(w_in, 16)
                n += 1
            assert n == N_W
            sp.wait_ge(pool_c, 7)
            for k in (1, 2):
                sp.dma_start(expert_sel[k * E1:(k + 1) * E1, :, :], expert_sel[0:E1, :, :]).then_inc(sel_in, 16)
            sp.wait_ge(zero_set, 1)
            for r in range(NH):
                flat = slot_rows[r].rearrange("(p c a n) d -> p c a (n d)", p=P, c=N_FILL, n=GT)
                for c in range(N_FILL):
                    sp.dma_start(flat[:, c, :, :], zeros[:, 0:GW].rearrange("p (a n) -> p a n", a=1)
                                 .to_broadcast([P, ST // GT // N_FILL, GW])).then_inc(filled[r], 16)
                if r == 0:
                    sp.dma_start(w_gu[:, :, 0:I0], w_gate.rearrange("e h i -> h e i")).then_inc(we_in, 16)
                    sp.dma_start(w_gu[:, :, I0:2 * I0], w_up.rearrange("e h i -> h e i")).then_inc(we_in, 16)
                    sp.dma_start(w_dn[:].rearrange("i (e h) -> i e h", e=E0),
                                 w_down.rearrange("e i h -> i e h")).then_inc(we_in, 16)

            def store(r, it, slot):
                sp.wait_ge(e_out, r * SG + it + 1)
                sp.dma_start(expert_groups[r][bass.ds(it, 1), :, :].rearrange("a p n -> (a p) n"),
                             eo[slot]).then_inc(e_stored[slot], 16)

            def load(r, it, slot):
                if not (isinstance(it, int) and it < 4 and r == 0):
                    sp.wait_ge(e_xT, r * SG + it - 4 + 1)
                sp.dma_start(rows[slot], slot_groups[r][bass.ds(it, 1), :, :]
                             .rearrange("a p n -> (a p) n")).then_inc(rows_in[slot], 16)

            for r in range(NH):
                sp.wait_ge(sent[r], 16 * HT * TOP0)
                for s in range(4):
                    load(r, s, s)
                    if r:
                        store(r - 1, SG - 4 + s, s)
                with sp.Fori(1, SG // 4) as i:
                    for s in range(4):
                        load(r, i * 4 + s, s)
                        store(r, (i - 1) * 4 + s, s)
            def load_xn(b, u):
                if isinstance(b, int) and b < 2:
                    sp.wait_ge(c_xn_kept, 1)
                else:
                    sp.wait_ge(d_h, b - 1)
                sp.dma_start(xn1T[u], xn_tok[:, bass.ds(b * 2, 2), :].rearrange("p a d -> p (a d)")).then_inc(xr_in[u], 16)

            def store_out(b, u):
                sp.wait_ge(d_fin, b + 1)
                sp.dma_start(out_rows[bass.ds(b, 1), :, :, :].rearrange("a p t d -> (a p) t d"),
                             fin[u]).then_inc(stored[u], 16)
            load_xn(0, 0)
            load_xn(1, 1)
            for s in range(4):
                store(NH - 1, SG - 4 + s, s)
            with sp.Fori(0, NSEQ // 2 - 1) as i:
                for u in range(2):
                    load_xn(i * 2 + u + 2, u)
                    store_out(i * 2 + u, u)
            for u in range(2):
                store_out(NSEQ - 2 + u, u)
            for s in range(2):
                sp.wait_ge(stored[s], 16 * NSEQ // 2)

        @block.gpsimd
        def _(pool):
            chain = Chain(pool, pool_link)
            g = nc.gpsimd
            chain.link(g.memset(ident[:], 0.0))
            g.affine_select(out=ident[:], in_=ident[:], compare_op=ALU.not_equal, fill=1.0, base=0,
                            pattern=[[-1, P]], channel_multiplier=1).then_inc(pool_c, 1)
            pool.wait_ge(pool_c, 1)
            chain.link(g.memset(not_before[:], 0.0))
            g.affine_select(out=not_before[:], in_=not_before[:], compare_op=ALU.is_gt, fill=-1.0, base=0,
                            pattern=[[1, P]], channel_multiplier=-1).then_inc(pool_c, 1)
            g.iota(iota_e[:], [[1, E0]], base=0, channel_multiplier=0,
                   allow_small_or_imprecise_dtypes=True).then_inc(pool_c, 1)
            g.iota(iota_t1[:], [[1, SEQ]], base=1, channel_multiplier=0,
                   allow_small_or_imprecise_dtypes=True).then_inc(pool_c, 1)
            g.iota(iota_p[:], [[1, 1]], base=0, channel_multiplier=1,
                   allow_small_or_imprecise_dtypes=True).then_inc(pool_c, 1)
            g.tensor_copy(ident_bf[:], ident[:]).then_inc(pool_c, 1)
            chain.link(g.memset(expert_sel[0:E1], 1.0))
            chain.link(g.affine_select(out=expert_sel[0:E1], in_=expert_sel[0:E1], compare_op=ALU.is_ge, fill=0.0,
                                       base=0, pattern=[[P, CH1], [1, P]], channel_multiplier=-I1))
            g.affine_select(out=expert_sel[0:E1], in_=expert_sel[0:E1], compare_op=ALU.is_ge, fill=0.0,
                            base=I1 - 1, pattern=[[-P, CH1], [-1, P]], channel_multiplier=I1).then_inc(pool_c, 1)

            def scaled(dst, table, by):
                return g.tensor_scalar(dst, table, by, None, ALU.mult)

            def cmul(re, im, ar, ai, br, bi, t0, t1):
                scaled(re, ar, br)
                scaled(im, ai, br)
                scaled(t0, ai, bi)
                chain.link(scaled(t1, ar, bi))
                g.tensor_tensor(re, re, t0, ALU.subtract)
                chain.link(g.tensor_tensor(im, im, t1, ALU.add))

            pool.wait_ge(phz_in, 64)
            pool.wait_ge(mag_ready, 1)
            g.memset(trig[:, 0, 0:1], 1.0)
            g.memset(trig[:, 1, 0:1], 0.0)
            g.memset(decay[:], 1.0)
            g.tensor_copy(trig[:, 0, 1:2], cs[:, 1:2])
            chain.link(g.tensor_copy(trig[:, 1, 1:2], cs[:, 2:3]))
            n = 1
            while n < SEQ:
                cmul(trig[:, 0, n + 1:2 * n + 1], trig[:, 1, n + 1:2 * n + 1],
                     trig[:, 0, 1:n + 1], trig[:, 1, 1:n + 1], trig[:, 0, n:n + 1], trig[:, 1, n:n + 1],
                     tab_tmp[:, 0:n], tab_tmp[:, n:2 * n])
                n *= 2
            cmul(out_cs[:, 0, :], out_cs[:, 1, :], trig[:, 0, 0:SEQ], trig[:, 1, 0:SEQ], phz[:, 2:3], phz[:, 3:4],
                 rec[:, 0, :], rec[:, 1, :])
            scaled(past[:], trig[:, 0, 1:SEQ + 1], phz[:, 4:5])
            chain.link(scaled(tab_tmp[:], trig[:, 1, 1:SEQ + 1], phz[:, 5:6]))
            chain.link(g.tensor_tensor(past[:], past[:], tab_tmp[:], ALU.subtract))
            pool.wait_ge(exp_ready, 2)
            g.tensor_tensor(past[:], past[:], decay_t1[:], ALU.mult)
            chain.link(scaled(decay[:], decay[:], cs[:, 4:5]))
            g.memset(decay[:, :, 0:1], 0.0).then_inc(tables, 1)

            for r in range(NH):
                pool.wait_ge(filled[r], 16 * N_FILL)
                for t in range(HT):
                    if t in (0, GT):
                        pool.wait_ge(slots_ready, r * 2 + 1 + t // GT)
                    for k in range(TOP0):
                        n = (r * HT + t) * TOP0 + k
                        g.indirect_dma_start(
                            out=slot_rows[r], out_offset=bass.IndirectOffsetOnAxis(ap=slot_of[:, n:n + 1], axis=0),
                            in_=xn_tok[:, r * HT + t, :], in_offset=None).then_inc(sent[r], 16)

            for b in range(NSEQ):
                r = b // (NSEQ // NH)
                if b % (NSEQ // NH) == 0:
                    for u in range(4):
                        pool.wait_ge(e_stored[u], 16 * (r + 1) * SG // 4)
                if b >= 4:
                    pool.wait_ge(c_f, b - 3)
                for j in range(2 * TOP0):
                    n = b * 2 * TOP0 + j
                    g.indirect_dma_start(
                        out=gath[b % 4][:, j, :], out_offset=None, in_=expert_rows[r],
                        in_offset=bass.IndirectOffsetOnAxis(ap=slot_of[:, n:n + 1], axis=0)).then_inc(g_in[b % 4], 16)

        @block.tensor
        def _(pe):
            pe.wait_ge(pool_c, 1)
            pe.wait_ge(rw_in, 32)

            def logits_of(it):
                pe.wait_ge(xT_sb, it + 1)
                if it >= 2:
                    pe.wait_ge(lg_sb, it - 1)
                for j in range(GT):
                    mm = pe.matmul(ps[:, 2 + it % 2, j * (E0 + 1):(j + 1) * (E0 + 1)],
                                   xnT[:, (it * GT + j) * P:(it * GT + j + 1) * P], rw[:], start=True, stop=True)
                mm.then_inc(lg_ps, 1)

            def ranks(r):
                pe.wait_ge(pool_c, 7)
                pe.wait_ge(mask_ready, r + 1)
                pe.matmul(bank(6), not_before[:], mask[:].rearrange("p t e -> p (t e)"), start=True, stop=True)
                pe.matmul(bank(7), ones_bf[:], mask[:].rearrange("p t e -> p (t e)"),
                          start=True, stop=True).then_inc(rank_ps, 1)

            def tile_ids(r):
                pe.wait_ge(ex_ready, r + 1)
                pe.transpose(ps[0:1, 7, 0:ST], tile_ex[0:ST, :], ident[0:ST, 0:ST]).then_inc(exT_row, 1)

            def turn_half(r):
                for it in range(r * NG // NH, (r + 1) * NG // NH):
                    pe.wait_ge(xn_ready, it + 1)
                    if it >= 2:
                        pe.wait_ge(xT_sb, it - 1)
                    for j in range(GT):
                        mm = pe.transpose(ps[:, it % 2, j * P:(j + 1) * P], xn_tok[:, it * GT + j, :], ident[:])
                    mm.then_inc(xT_ps, 1)
                    if it % (NG // NH):
                        logits_of(it - 1)
                logits_of((r + 1) * NG // NH - 1)

            turn_half(0)
            ranks(0)
            tile_ids(0)

            pe.wait_ge(w_in, 16 * N_W)
            pe.wait_ge(lg_sb, NG // NH)
            for j in range(3):
                last = pe.transpose(ps[:, 2, j * P:(j + 1) * P], raw1[:, j, :], ident[:])
            last.then_inc(wT_ps, 1)
            for j in range(CH1):
                last = pe.transpose(ps[:, 3, j * P:(j + 1) * P], raw_fc[:, j, :], ident[:])
            last.then_inc(wT_ps, 1)
            for j in range(CH1):
                last = pe.transpose(ps[:, 4, j * P:(j + 1) * P],
                                    raw_pr[:].rearrange("h e i -> h (e i)")[:, j * P:(j + 1) * P], ident[:])
            last.then_inc(wT_ps, 1)
            pe.transpose(ps[:, 5, 0:E1], raw_g1[:], ident[0:E1, 0:E1])
            pe.matmul(ps[:, 5, P:2 * P], ones[0:1, :], bv_r[:], start=True, stop=True).then_inc(wT_ps, 1)

            pe.wait_ge(wT_sb, 4)

            def shared_in(it, u, first=False):
                if not first:
                    pe.wait_ge(sh_hid, it - 1)
                xg = xnT[:, bass.ds(it * SEQ, SEQ)]
                for c in range(2):
                    pe.matmul(ps[:, 2 * u, c * SEQ:(c + 1) * SEQ], shg[:, c * P:(c + 1) * P], xg,
                              start=True, stop=True)
                for c in range(2):
                    mm = pe.matmul(ps[:, 2 * u + 1, c * SEQ:(c + 1) * SEQ], shu[:, c * P:(c + 1) * P], xg,
                                   start=True, stop=True)
                mm.then_inc(sh_ps, 1)

            def shared_out(it, u):
                pe.wait_ge(sh_hid, it + 1)
                if not (isinstance(it, int) and it < 2):
                    pe.wait_ge(sh_done, it - 1)
                for j in range(2):
                    for c in range(2):
                        mm = pe.matmul(ps[:, 4 + u, j * P:(j + 1) * P], hs_h[u][:, c, j * P:(j + 1) * P],
                                       shd[:, c, :], start=(c == 0), stop=(c == 1))
                mm.then_inc(sh_dn, 1)

            def turn_s(b):
                pe.wait_ge(recurred, b + 1)
                if not (isinstance(b, int) and b == 0):
                    pe.wait_ge(s_tok, b)
                for j in range(2):
                    mm = pe.transpose(ps[:, 7, j * P:(j + 1) * P], s_rec[:, j * P:(j + 1) * P], ident[:])
                mm.then_inc(s_ps, 1)

            HS = NSEQ // NH
            shared_in(0, 0, True)
            for it in range(HS):
                if it + 1 < HS:
                    shared_in(it + 1, (it + 1) % 2, it == 0)
                shared_out(it, it % 2)
            turn_half(1)
            for b in range(PRE):
                turn_s(b)
            pe.wait_ge(xT_sb, NG)
            pe.wait_ge(lg_sb, NG)
            shared_in(HS, 0)
            for it in range(HS, NSEQ):
                if it + 1 < NSEQ:
                    shared_in(it + 1, (it + 1) % 2)
                shared_out(it, it % 2)
                if it == HS + RANKS_AFTER:
                    pe.wait_ge(s_tok, PRE)
                    ranks(1)
                if it == HS + IDS_AFTER:
                    tile_ids(1)

            pe.wait_ge(sh_done, NSEQ)
            pe.wait_ge(we_in, 48)
            pe.wait_ge(routed, NH)

            def ids(at):
                _, v = nc.values_load_multi_w_load_instructions(
                    tile_expert[0:1, bass.ds(at, GT)], engines=[mybir.EngineType.PE], min_val=0, max_val=E0 - 1,
                    skip_runtime_bounds_check_because="VectorE clamps the ids to E0 - 1")
                return v

            N = NH * SG

            def rows_T(n, slot, fills, first=False):
                pe.wait_ge(rows_in[slot], fills * 16)
                if not first:
                    pe.wait_ge(e_xTs, n)
                for j in range(GT):
                    mm = pe.transpose(ps[:, 0, j * P:(j + 1) * P], rows[slot][:, j * P:(j + 1) * P], ident[:])
                mm.then_inc(e_xT, 1)

            def act_T(n, u, first=False):
                pe.wait_ge(e_act, n + 1)
                if not first:
                    pe.wait_ge(e_aTs, n)
                for j in range(GT):
                    mm = pe.transpose(ps[0:I0, 5, j * P:(j + 1) * P], act[u][:, j, :], ident[:])
                mm.then_inc(e_aT, 1)

            def down(n, u, e, first=False):
                pe.wait_ge(e_aTs, n + 1)
                if not first:
                    pe.wait_ge(e_out, n)
                for j in range(GT):
                    mm = pe.matmul(ps[:, 6, j * P:(j + 1) * P], actT[u][:, j * P:(j + 1) * P],
                                   w_dn[:, bass.ds(e[j] * P, P)], start=True, stop=True)
                mm.then_inc(e_dn, 1)

            def gate_up(n, u, e, first=False):
                pe.wait_ge(e_xTs, n + 1)
                if not first:
                    pe.wait_ge(e_act, n - 1)
                for j in range(GT):
                    mm = pe.matmul(ps[:, 1 + 2 * u + j // 2, (j % 2) * 256:(j % 2) * 256 + 2 * I0],
                                   exT[u][:, j * P:(j + 1) * P],
                                   w_gu[:, bass.ds(e[j], 1), :].rearrange("p a n -> p (a n)"),
                                   start=True, stop=True)
                mm.then_inc(e_gu, 1)

            def turn_xn(p):
                pe.wait_ge(c_xn, p + 1)
                for j in range(4):
                    mm = pe.transpose(ps[:, 7, j * P:(j + 1) * P], xn1[:, j, :], ident[:])
                mm.then_inc(c_xnT, 1)

            def gate_logits(p):
                pe.wait_ge(c_xn_kept, p + 1)
                for j in range(4):
                    mm = pe.matmul(ps[:, 7, 2 * SEQ - (4 - j) * E1:2 * SEQ - (3 - j) * E1],
                                   xn1T_pair[:, j * P:(j + 1) * P], g1T[:], start=True, stop=True)
                return mm

            def turn_between(p):
                if p:
                    pe.wait_ge(c_lgs, p)
                turn_xn(p)

            def logits_between(p):
                gate_logits(p).then_inc(c_lg, 1)

            def stage_e(n, slot, rnd, first=False, turn=None):
                e_down = None if first and slot == 0 else ids((n - 1) * GT)
                e_next = ids((n + 1) * GT) if not isinstance(n, int) or n + 1 < N else None
                if not isinstance(n, int) or n + 2 < N:
                    rows_T(n + 2, (slot + 2) % 4, rnd + (2 if slot >= 2 else 1))
                if e_down is not None:
                    down(n - 1, (slot + 1) % 2, e_down, first and slot == 1)
                act_T(n, slot % 2, first and slot == 0)
                if turn is not None:
                    turn()
                if e_next is not None:
                    gate_up(n + 1, (slot + 1) % 2, e_next, first and slot == 0)

            rows_T(0, 0, 1, True)
            rows_T(1, 1, 1)
            gate_up(0, 0, ids(0), True)
            for s in range(4):
                stage_e(s, s, 0, True, (lambda: turn_s(PRE)) if s == 2 else None)
            with pe.Fori(1, (NSEQ - PRE) // 2) as i:
                for s in range(4):
                    stage_e(i * 4 + s, s, i, turn=None if s % 2 else lambda: turn_s(PRE - 1 + i * 2 + s // 2))
            turn_s(NSEQ - 1)
            for n in range(4 * E_NORM, N):
                q, step = norm_step(n)
                turn = None
                if q and step == 1:
                    turn = lambda: turn_between(q - 1)
                if q and step == 2:
                    turn = lambda: logits_between(q - 1)
                stage_e(n, n % 4, n // 4, turn=turn)
            down(N - 1, 1, ids((N - 1) * GT))

            pe.wait_ge(e_out, N)
            pe.wait_ge(c_lgs, FSEQ // 2 - 1)

            def expert_sum(b, u, first):
                pe.wait_ge(d_hs, b + 1)
                if not first:
                    pe.wait_ge(d_fin, b)
                for j in range(2):
                    for c in range(CH1):
                        mm = pe.matmul(ps[:, 3, j * P:(j + 1) * P], hg[u][:, c, j * P:(j + 1) * P], prT[:, c, :],
                                       start=(c == 0), stop=(c == CH1 - 1))
                mm.then_inc(d_moe, 1)

            def turn_gates(k):
                pe.wait_ge(d_gate, k + 1)
                for j in range(4 * BATCHES[k][1]):
                    mm = pe.matmul(ps[0:3 * E1, j // 4, (j % 4) * P:(j % 4 + 1) * P],
                                   gate_parts[:, j, :, :].rearrange("p a e -> p (a e)"), ident_bf[:],
                                   start=True, stop=True)
                mm.then_inc(d_gT, 1)

            pe.wait_ge(sel_in, 32)
            for b in range(NSEQ):
                u = b % 2
                pe.wait_ge(xr_in[u], 16 * (b // 2 + 1))
                if b:
                    pe.wait_ge(d_pTs, b)
                for j in range(2):
                    mm = pe.matmul(ps[:, 2, j * SEQ:(j + 1) * SEQ], w1T[:, j, :], xn1T[u], start=True, stop=True)
                mm.then_inc(d_qk, 1)
                if b:
                    pe.wait_ge(d_vs, b)
                if turned(b - 2) is not None:
                    gate_logits(turned(b - 2))
                for j in range(2):
                    mm = pe.matmul(ps[:, 7, j * P:(j + 1) * P], xn1T[u][:, j * P:(j + 1) * P], w1T[:, 2, :],
                                   start=True, stop=True)
                mm.then_inc(d_v, 1)
                pe.wait_ge(d_qks, b + 1)
                if b:
                    pe.wait_ge(d_os, b)
                for j in range(2):
                    mm = pe.matmul(ps[:, 6, j * SEQ:(j + 1) * SEQ], qk_sb[:, 0, j * P:(j + 1) * P], qk_sb[:, 1, :],
                                   start=True, stop=True)
                mm.then_inc(d_s, 1)
                if b:
                    pe.wait_ge(d_hg, b)
                for c in range(CH1):
                    mm = pe.matmul(ps[:, 4 + c // 2, (c % 2) * SEQ:(c % 2 + 1) * SEQ], fcT[:, c, :], xn1T[u],
                                   start=True, stop=True)
                mm.then_inc(d_h, 1)
                if b:
                    pe.wait_ge(d_hs, b)
                batch, place = batch_of(b)
                if place == 0:
                    turn_gates(batch)
                if turned(b - 1) is not None:
                    pe.wait_ge(d_vs, b + 1)
                    turn_xn(turned(b - 1))
                if b:
                    expert_sum(b - 1, 1 - u, b == 1)
                pe.wait_ge(d_p, b + 1)
                for k in range(2):
                    for j in range(2):
                        mm = pe.transpose(ps[:, 2, k * SEQ + j * P:k * SEQ + (j + 1) * P],
                                          pr[:, j, k * P:(k + 1) * P], ident[:])
                mm.then_inc(d_pT, 1)
                pe.wait_ge(d_gTs, batch + 1)
                for c in range(CH1):
                    mm = pe.matmul(ps[:, c // 2, (c % 2) * SEQ:(c % 2 + 1) * SEQ], expert_sel[:, c, :],
                                   gT[batch % 2][:, place * SEQ:(place + 1) * SEQ], start=True, stop=True)
                mm.then_inc(d_gb, 1)
                pe.wait_ge(d_pTs, b + 1)
                for j in range(2):
                    for k in range(2):
                        mm = pe.matmul(ps[:, 6, j * P:(j + 1) * P], pT[:, k, j * P:(j + 1) * P], v_sb[:, k, :],
                                       start=(k == 0), stop=(k == 1))
                mm.then_inc(d_o, 1)
            expert_sum(NSEQ - 1, 1, False)

        @block.scalar
        def _(sc):
            a = nc.scalar
            chain = Chain(sc, act_link)
            sc.wait_ge(mag_ready, 1)
            sc.wait_ge(pool_c, 7)
            a.activation(cs[:, 4:5], cs[:, 3:4], ACT.Exp).then_inc(exp_ready, 1)
            a.activation(decay_t1[:], iota_t1[:], ACT.Exp, scale=cs[:, 3:4]).then_inc(exp_ready, 1)

            def copy_logits(it):
                sc.wait_ge(lg_ps, it + 1)
                a.copy(logits[:, it * GT:(it + 1) * GT, :].rearrange("p t e -> p (t e)"),
                       bank(2 + it % 2, GT * (E0 + 1))).then_inc(lg_sb, 1)

            def exp_top(r):
                sc.wait_ge(tw_in, r + 1)
                a.activation(tw[:], tw[:], ACT.Exp).then_inc(tw_exp, 1)

            def copy_half(r):
                for it in range(r * NG // NH, (r + 1) * NG // NH):
                    sc.wait_ge(xT_ps, it + 1)
                    a.copy(xnT[:, it * GW:(it + 1) * GW], bank(it % 2)).then_inc(xT_sb, 1)
                    if it % (NG // NH):
                        copy_logits(it - 1)
                copy_logits((r + 1) * NG // NH - 1)
                sc.wait_ge(lg_sb, (r + 1) * NG // NH)
                a.activation(sh_gate_t[:, r * HT:(r + 1) * HT], logits[:, r * HT:(r + 1) * HT, E0],
                             ACT.Sigmoid).then_inc(sh_gated, 1)

            copy_half(0)
            exp_top(0)
            sc.wait_ge(wT_ps, 4)
            a.copy(w1T[:].rearrange("p a b -> p (a b)"), bank(2, 384)).then_inc(wT_sb, 1)
            a.copy(fcT[:].rearrange("p a b -> p (a b)"), bank(3)).then_inc(wT_sb, 1)
            a.copy(prT[:].rearrange("p a b -> p (a b)"), bank(4)).then_inc(wT_sb, 1)
            a.copy(g1T[:], bank(5, E1))
            a.copy(bv_all[:], ps[:, 5, P:2 * P]).then_inc(wT_sb, 1)

            def stage_s(it, u):
                sc.wait_ge(sh_ps, it + 1)
                if it >= 2:
                    sc.wait_ge(sh_hid, it - 1)
                a.activation(hs_t[u][:].rearrange("p a t -> p (a t)"), bank(2 * u), ACT.Silu).then_inc(sh_silu, 1)
            def copy_s(b):
                sc.wait_ge(s_ps, b + 1)
                a.copy(xnT[:, bass.ds(b * SEQ, SEQ)], ps[:, 7, 0:SEQ]).then_inc(s_tok, 1)

            for it in range(NSEQ):
                if it == NSEQ // NH:
                    copy_half(1)
                    for b in range(PRE):
                        copy_s(b)
                stage_s(it, it % 2)
                if it == NSEQ // NH + RANKS_AFTER:
                    exp_top(1)

            def copy_xT(n, u):
                sc.wait_ge(e_xT, n + 1)
                if not (isinstance(n, int) and n < 2):
                    sc.wait_ge(e_gu, n - 1)
                a.copy(exT[u], bank(0)).then_inc(e_xTs, 1)

            def silu_gate(n, u):
                sc.wait_ge(e_gu, n + 1)
                if not (isinstance(n, int) and n < 2):
                    sc.wait_ge(e_act, n - 1)
                a.activation(sg[u][:].rearrange("p (a b) i -> p a b i", a=2),
                             ps[:, 1 + 2 * u:3 + 2 * u, :].rearrange("p a (b i) -> p a b i", b=2)[:, :, :, 0:I0],
                             ACT.Silu).then_inc(e_sg, 1)

            def copy_out(n, slot, rnd):
                sc.wait_ge(e_dn, n + 1)
                if not (isinstance(rnd, int) and rnd == 0):
                    sc.wait_ge(e_stored[slot], rnd * 16)
                a.copy(eo[slot], bank(6)).then_inc(e_out, 1)

            for r in range(NH):
                sc.wait_ge(filled[r], 16 * N_FILL)

            def copy_aT(n, u):
                sc.wait_ge(e_aT, n + 1)
                if not (isinstance(n, int) and n < 2):
                    sc.wait_ge(e_dn, n - 1)
                a.copy(actT[u][:], ps[0:I0, 5, :]).then_inc(e_aTs, 1)

            def silu_f(p):
                sc.wait_ge(c_f, 2 * p + 2)
                a.activation(f_act, f_sb, ACT.Silu).then_inc(c_fact, 1)

            def copy_xn(p):
                sc.wait_ge(c_xnT, p + 1)
                a.copy(xn1T_pair, bank(7))
                a.copy(xn_tok[:, bass.ds(p * 4, 4), :].rearrange("p a d -> p (a d)"), bank(7)).then_inc(c_xn_kept, 1)

            def copy_gate_logits(p):
                a.copy(lg1[:, bass.ds(p * 4, 4), :].rearrange("p a e -> p (a e)"),
                       ps[:, 7, 2 * SEQ - 4 * E1:2 * SEQ]).then_inc(c_lgs, 1)

            def logits_between(p, count):
                sc.wait_ge(c_lg, count)
                copy_gate_logits(p)

            N = NH * SG

            def stage_e(n, slot, rnd, turn=None, after=None):
                if not isinstance(n, int) or n + 2 < N:
                    copy_xT(n + 2, slot % 2)
                if not isinstance(n, int) or n > 0:
                    copy_out(n - 1, (slot + 3) % 4, rnd if slot else rnd - 1)
                copy_aT(n, slot % 2)
                if turn is not None:
                    turn()
                if not isinstance(n, int) or n + 1 < N:
                    silu_gate(n + 1, (slot + 1) % 2)
                if after is not None:
                    after()
            copy_xT(0, 0)
            copy_xT(1, 1)
            silu_gate(0, 0)
            for n in range(8):
                stage_e(n, n % 4, n // 4, (lambda: copy_s(PRE - 1 + n // 2)) if n and n % 2 == 0 else None)
            with sc.Fori(2, (NSEQ - PRE) // 2) as i:
                for s in range(4):
                    stage_e(i * 4 + s, s, i, None if s % 2 else lambda: copy_s(PRE - 1 + i * 2 + s // 2))
            copy_s(NSEQ - 1)

            def tanh_gates(k):
                sc.wait_ge(d_gd, k + 1)
                a.activation(gth[:], gd[:], ACT.Tanh, scale=0.5).then_inc(d_gth, 1)

            sc.wait_ge(sent[0], 16 * HT * TOP0)
            for n in range(4 * E_NORM, N):
                q, step = norm_step(n)
                turn = after = None
                if q and step == 1:
                    turn = lambda: copy_xn(q - 1)
                if q and step == 2:
                    turn = lambda: logits_between(q - 1, q)
                if step == 2:
                    after = lambda: silu_f(q)
                if step == 0 and q == FSEQ // 2 - 1:
                    after = lambda: tanh_gates(0)
                stage_e(n, n % 4, n // 4, turn, after)
            copy_out(N - 1, 3, N // 4 - 1)

            sc.wait_ge(sent[1], 16 * HT * TOP0)

            def tanh_f(p):
                sc.wait_ge(c_f, 2 * p + 2)
                a.activation(f_act, f_sb, ACT.Tanh, scale=0.5).then_inc(c_fact, 1)

            def tanh_moe(b, first):
                sc.wait_ge(d_moe, b + 1)
                if not first:
                    sc.wait_ge(d_fin, b)
                a.activation(mth[:], bank(3, SEQ), ACT.Tanh, scale=0.5).then_inc(d_mth, 1)

            for b in range(NSEQ):
                u = b % 2
                sc.wait_ge(d_qk, b + 1)
                if b:
                    sc.wait_ge(d_s, b)
                for j in range(2):
                    last = a.activation(qk_sb[:, j, :], ps[:, 2, j * SEQ:(j + 1) * SEQ], ACT.Identity,
                                        bias=bqk[:, j:j + 1])
                last.then_inc(d_qks, 1)
                sc.wait_ge(d_v, b + 1)
                if b:
                    sc.wait_ge(d_o, b)
                if turned(b - 2) is not None:
                    copy_gate_logits(turned(b - 2))
                a.copy(v_sb, ps[:, 7, 0:SEQ].rearrange("p (a d) -> p a d", a=2)).then_inc(d_vs, 1)
                sc.wait_ge(d_nmx, b + 1)
                for j in range(2):
                    last = a.activation(pr[:, j, :], ps[:, 6, j * SEQ:(j + 1) * SEQ], ACT.Exp,
                                        bias=nmx[:, j:j + 1], scale=SCALE, accum_out=den[:, j:j + 1])
                last.then_inc(d_p, 1)
                batch, place = batch_of(b)
                if place == 0:
                    sc.wait_ge(d_gT, batch + 1)
                    n = BATCHES[batch][1]
                    a.copy(gT[batch % 2][:, 0:n * 2 * SEQ],
                           ps[0:3 * E1, 0:n, :].rearrange("p a n -> p (a n)")).then_inc(d_gTs, 1)
                sc.wait_ge(d_h, b + 1)
                if b >= 2:
                    sc.wait_ge(d_moe, b - 1)
                a.activation(hg[u], ps[:, 4:6, :].rearrange("p a (b n) -> p (a b) n", b=2),
                             ACT.Gelu).then_inc(d_hg, 1)
                sc.wait_ge(d_pT, b + 1)
                a.copy(pT[:].rearrange("p a b -> p (a b)"), bank(2)).then_inc(d_pTs, 1)
                if b:
                    tanh_moe(b - 1, b == 1)
                if gated(b) is not None:
                    tanh_gates(gated(b))
                if turned(b + 1) is not None:
                    tanh_f(turned(b + 1))
                if turned(b - 1) is not None:
                    copy_xn(turned(b - 1))
            tanh_moe(NSEQ - 1, False)

        @block.vector
        def _(dve):
            v = nc.vector
            chain = Chain(dve, dve_link)
            link = chain.link
            v.memset(zeros[:, 0:GW], 0.0).then_inc(zero_set, 1)
            def row_stats(t):
                if t % GT == 0:
                    dve.wait_ge(x_in[t // GT], 16)
                return v.bn_stats(stats[:, t, :], x_tok[:, t, :])

            def norm0(r, beside=None):
                beside = beside or (lambda k: None)
                T0, T1 = r * HT, (r + 1) * HT
                for t in range(max(T0, stats_done), T1):
                    last = row_stats(t)
                    if t % 4 == 3:
                        beside((t - T0) // 4)
                link(last)
                m, va, t = mean[:, T0:T1], var[:, T0:T1], rtmp[:, 0:HT]
                s = stats[:, T0:T1, :]
                link(v.tensor_tensor(t, s[:, :, 1], s[:, :, 4], ALU.subtract))
                v.tensor_tensor(va, s[:, :, 2], s[:, :, 5], ALU.add)
                v.tensor_tensor(m, s[:, :, 1], s[:, :, 4], ALU.add)
                link(v.tensor_tensor(t, t, t, ALU.mult))
                v.tensor_scalar(m, m, 0.5, None, ALU.mult)
                link(v.tensor_scalar(t, t, 0.25, EPS, ALU.mult, ALU.add))
                link(v.scalar_tensor_tensor(out=va, in0=va, scalar=1.0 / P, in1=t, op0=ALU.mult, op1=ALU.add))
                rsqrt_steps(nc, link, rstd[:, T0:T1], va, rtmp[:])
                for t in range(T0, T1):
                    last = v.tensor_scalar(xn_tok[:, t, :], x_tok[:, t, :], mean[:, t:t + 1], rstd[:, t:t + 1],
                                           ALU.subtract, ALU.mult)
                    if t % GT == GT - 1:
                        last.then_inc(xn_ready, 1)
                        beside(4 + (t - T0) // 4)

            def route(r, beside=None):
                beside = beside or (lambda k: None)
                T0 = r * HT
                oh4 = onehot[:].rearrange("p (t k) e -> p t k e", k=TOP0)
                tf4 = top_f[:].rearrange("p (t k) -> p t k", k=TOP0)
                experts = iota_e[:].rearrange("p (a e) -> p a e", a=1).to_broadcast([P, GT * TOP0, E0])
                for g in range(HT // GT):
                    tiles = slice(g * GT, (g + 1) * GT)
                    rows_g = slice(g * GT * TOP0, (g + 1) * GT * TOP0)
                    dve.wait_ge(lg_sb, r * HT // GT + g + 1)
                    for t in range(g * GT, (g + 1) * GT):
                        last = v.max(top8[:, t, :], logits[:, T0 + t, 0:E0])
                    link(last)
                    for t in range(g * GT, (g + 1) * GT):
                        last = v.max_index(top8_i[:, t, :], top8[:, t, :], logits[:, T0 + t, 0:E0])
                    link(last)
                    if g == HT // GT - 1:
                        v.tensor_tensor(tw[:], top8[:, :, 0:TOP0], top8[:, :, 0:1].to_broadcast([P, HT, TOP0]),
                                        ALU.subtract).then_inc(tw_in, 1)
                    link(v.tensor_copy(tf4[:, tiles, :], top8_i[:, tiles, 0:TOP0]))
                    link(v.tensor_tensor(onehot[:, rows_g, :], experts, top_f[:, rows_g]
                                         .rearrange("p (t a) -> p t a", a=1).to_broadcast([P, GT * TOP0, E0]),
                                         ALU.is_equal))
                    with nc.allow_low_precision("sums of one 1 and zeros"):
                        last = v.tensor_reduce(mask[:, tiles, :], oh4[:, tiles, :, :].rearrange("p t k e -> p t e k"),
                                               AX.X, ALU.add)
                    if g == HT // GT - 1:
                        last.then_inc(mask_ready, 1)
                    beside(g)
                dve.wait_ge(tw_exp, r + 1)
                link(v.tensor_reduce(tsum[:], tw[:], AX.X, ALU.add))
                link(v.reciprocal(tsum[:], tsum[:]))
                v.tensor_tensor(top_w[:, T0 * TOP0:(T0 + HT) * TOP0].rearrange("p (t k) -> p t k", k=TOP0), tw[:],
                                tsum[:].rearrange("p (t a) -> p t a", a=1).to_broadcast([P, HT, TOP0]), ALU.mult)
                dve.wait_ge(rank_ps, r + 1)
                link(v.tensor_copy(tot_em, bank(7).rearrange("p (t e) -> p e t", t=HT)))
                link(v.tensor_tensor_scan(cum_em.rearrange("p e t -> p (e t)"), not_first.rearrange("p e t -> p (e t)"),
                                          tot_em.rearrange("p e t -> p (e t)"), 0.0, ALU.mult, ALU.add))
                beside(4)
                link(v.tensor_scalar(cnt_i[:], cum_em[:, :, HT - 1], float(P - 1), None, ALU.add))
                link(v.tensor_scalar(cnt_i[:], cnt_i[:], 7, None, ALU.logical_shift_right))
                link(v.tensor_copy(tiles_e[:], cnt_i[:]))
                link(v.tensor_tensor_scan(tile_end[:], ones[:, 0:E0], tiles_e[:], 0.0, ALU.mult, ALU.add))
                link(v.tensor_scalar(tile_cmp[0:ST, :], tile_end[0:ST, :], iota_p[0:ST, 0:1], None, ALU.is_le))
                link(v.tensor_reduce(tile_ex[0:ST, :], tile_cmp[0:ST, :], AX.X, ALU.add))
                v.tensor_scalar(tile_ex[0:ST, :], tile_ex[0:ST, :], float(E0 - 1), None, ALU.min).then_inc(ex_ready, 1)
                beside(5)
                link(v.tensor_tensor(tiles_e[:], tile_end[:], tiles_e[:], ALU.subtract))
                link(v.tensor_scalar(tiles_e[:], tiles_e[:], float(P), None, ALU.mult))
                link(v.tensor_tensor(cum_em, cum_em,
                                     tiles_e[:].rearrange("p (e a) -> p e a", a=1).to_broadcast([P, E0, HT]), ALU.add))
                link(v.tensor_tensor(pos, bank(6).rearrange("p (t e) -> p t e", t=HT),
                                     cum_em.rearrange("p e t -> p t e"), ALU.add))
                for c, (a, b) in enumerate(((0, GT), (GT, HT))):
                    for k in range(TOP0):
                        last = v.tensor_tensor(oh4[:, a:b, k, :], oh4[:, a:b, k, :], pos[:, a:b, :], ALU.mult)
                    link(last)
                    beside(6 + c)
                    of = slice(a * TOP0, b * TOP0)
                    link(v.tensor_reduce(top_f[:, of], onehot[:, of, :], AX.X, ALU.add))
                    sl = slot_of[:, (T0 + a) * TOP0:(T0 + b) * TOP0]
                    link(v.tensor_copy(slot_i[:, of], top_f[:, of]))
                    v.tensor_scalar(sl, slot_i[:, of], 9, 9, ALU.logical_shift_right, ALU.logical_shift_left)
                    link(v.tensor_scalar(slot_a[:, of], slot_i[:, of], P - 1, 2, ALU.bitwise_and, ALU.logical_shift_left))
                    link(v.tensor_tensor(sl, sl, slot_a[:, of], ALU.add))
                    link(v.tensor_scalar(slot_a[:, of], slot_i[:, of], 7, GT - 1, ALU.logical_shift_right, ALU.bitwise_and))
                    v.tensor_tensor(sl, sl, slot_a[:, of], ALU.add).then_inc(slots_ready, 1)
                dve.wait_ge(exT_row, r + 1)
                v.tensor_copy(tile_expert[:, r * ST:(r + 1) * ST], ps[0:1, 7, 0:ST]).then_inc(routed, 1)

            dve.wait_ge(phz_in, 64)
            stats_done = HT - 2
            lk = chain.link_beside(row_stats, stats_done)
            lk(v.tensor_tensor(cs[:, 9:10], phz[:, 1:2], phz[:, 1:2], ALU.mult))
            lk(v.scalar_tensor_tensor(out=cs[:, 0:1], in0=phz[:, 0:1], scalar=phz[:, 0:1], in1=cs[:, 9:10],
                                        op0=ALU.mult, op1=ALU.add))
            rsqrt_steps(nc, lk, cs[:, 13:14], cs[:, 0:1], cs[:, 14:16])
            v.tensor_scalar(cs[:, 1:3], phz[:, 0:2], cs[:, 13:14], None, ALU.mult)
            lk(v.tensor_tensor(cs[:, 3:4], cs[:, 0:1], cs[:, 13:14], ALU.mult))
            v.tensor_scalar(cs[:, 3:4], cs[:, 3:4], -1.0, None, ALU.mult).then_inc(mag_ready, 1)

            norm0(0)
            v.memset(ones_bf[:], 1.0)
            v.memset(ones[:], 1.0)
            link(v.memset(not_first, 1.0))
            link(v.memset(not_first[:, :, 0:1], 0.0))
            dve.wait_ge(pool_c, 7)
            route(0)

            def shared_hidden(it):
                u = it % 2
                dve.wait_ge(sh_silu, it + 1)
                if it >= 2:
                    dve.wait_ge(sh_dn, it - 1)
                v.tensor_tensor(hs_h[u][:].rearrange("p a t -> p (a t)"), hs_t[u][:].rearrange("p a t -> p (a t)"),
                                bank(2 * u + 1), ALU.mult).then_inc(sh_hid, 1)

            def shared_gated(it):
                dve.wait_ge(sh_dn, it + 1)
                v.tensor_tensor(sh_tok[:, it * 2:it * 2 + 2, :],
                                ps[:, 4 + it % 2, 0:SEQ].rearrange("p (a d) -> p a d", a=2),
                                sh_gate_t[:, it * 2:it * 2 + 2].rearrange("p (n a) -> p n a", a=1)
                                .to_broadcast([P, 2, P]), ALU.mult).then_inc(sh_done, 1)

            def shared_step(it):
                shared_hidden(it)
                if it % HS:
                    shared_gated(it - 1)

            def twice(row):
                return row.rearrange("p (a t) -> p a t", a=1).to_broadcast([P, 2, SEQ])

            def recurrence(it, turn):
                xg = xnT[:, bass.ds(it * SEQ, SEQ)]
                flat = rec[:].rearrange("p a t -> p (a t)")
                if turn == 0:
                    if not (isinstance(it, int) and it == 0):
                        dve.wait_ge(recurred, it)
                    link(v.tensor_tensor(rec[:], twice(xg), trig[:, :, 0:SEQ], ALU.mult))
                    link(v.tensor_tensor_scan(flat, decay[:].rearrange("p a t -> p (a t)"), flat, 0.0,
                                              ALU.mult, ALU.add))
                    link(v.tensor_tensor(rec[:], rec[:], out_cs[:], ALU.mult))
                else:
                    link(v.tensor_tensor(rec[:, 0, :], rec[:, 0, :], rec[:, 1, :], ALU.add))
                    if not (isinstance(it, int) and it == 0):
                        dve.wait_ge(s_ps, it)
                    v.tensor_tensor(s_rec[:], rec[:, 0, :], past[:], ALU.add).then_inc(recurred, 1)

            HS = NSEQ // NH
            dve.wait_ge(sh_gated, 1)
            norm0(1, lambda k: shared_step(k))
            shared_gated(HS - 1)
            dve.wait_ge(tables, 1)
            for b in range(PRE):
                recurrence(b, 0)
                recurrence(b, 1)
            dve.wait_ge(sh_gated, 2)
            route(1, lambda k: shared_step(HS + k))
            shared_gated(NSEQ - 1)

            def hidden(n, u):
                dve.wait_ge(e_sg, n + 1)
                if not (isinstance(n, int) and n < 2):
                    dve.wait_ge(e_aT, n - 1)
                v.tensor_tensor(act[u][:].rearrange("p (a b) i -> p a b i", a=2),
                                sg[u][:].rearrange("p (a b) i -> p a b i", a=2),
                                ps[:, 1 + 2 * u:3 + 2 * u, :].rearrange("p a (b i) -> p a b i", b=2)[:, :, :, I0:2 * I0],
                                ALU.mult).then_inc(e_act, 1)

            def sum_step(b, n, marks):
                w, j, k = f_w[b % 2], n % 2, n // 2
                if n == 0:
                    link(v.tensor_copy(w[:], top_w[:, b * 2 * TOP0:(b + 1) * 2 * TOP0]))
                    dve.wait_ge(g_in[b % 4], 16 * 2 * TOP0 * (b // 4 + 1))
                into = f_sb[:, 2 * (b % 2) + j, :]
                if k:
                    chain.after(marks[n - 2])
                ins = v.scalar_tensor_tensor(out=into, in0=gath[b % 4][:, j * TOP0 + k, :],
                                             scalar=w[:, j * TOP0 + k:j * TOP0 + k + 1],
                                             in1=into if k else sh_tok[:, b * 2 + j, :], op0=ALU.mult, op1=ALU.add)
                if k < TOP0 - 1:
                    marks.append(chain.mark(ins))
                elif j:
                    ins.then_inc(c_f, 1)

            def sum_experts(b):
                marks = []
                for n in range(2 * TOP0):
                    sum_step(b, n, marks)

            def row(b, j):
                return x_tok[:, b * 2 + j, :]

            def mix(p, tanh):
                dve.wait_ge(c_fact, p + 1)
                if tanh:
                    link(v.scalar_tensor_tensor(out=f_sb, in0=f_act, scalar=1.0, in1=f_sb, op0=ALU.add, op1=ALU.mult))
                dve.wait_ge(s_tok, NSEQ)
                link(v.tensor_tensor(f_sb, f_sb if tanh else f_act, xnT[:, p * 2 * SEQ:(p + 1) * 2 * SEQ]
                                     .rearrange("p (a d) -> p a d", d=P), ALU.mult))
                xb = x_tok[:, p * 4:(p + 1) * 4, :]
                link(v.scalar_tensor_tensor(out=xb, in0=f_sb, scalar=0.5 if tanh else 1.0, in1=xb,
                                            op0=ALU.mult, op1=ALU.add))

            def stats1(p):
                for j in range(4):
                    last = v.bn_stats(st1[:, j, :], row(p * 2, j))
                link(last)
                for j in range(4):
                    last = v.bn_aggr(mv1[:, j, :], st1[:, j, :])
                link(last)

            def rstd1(beside=None):
                marks = []
                lk = link if beside is None else chain.link_beside(lambda n: sum_step(beside, n, marks), 2 * TOP0)
                lk(v.tensor_scalar(v1[:], mv1[:, :, 1], EPS, None, ALU.add))
                rsqrt_steps(nc, lk, r1[:], v1[:], t1[:])

            def norm1(p):
                if p:
                    dve.wait_ge(c_xnT, p)
                for j in range(4):
                    last = v.tensor_scalar(xn1[:, j, :], row(p * 2, j), mv1[:, j, 0:1], r1[:, j:j + 1],
                                           ALU.subtract, ALU.mult)
                last.then_inc(c_xn, 1)

            N = NH * SG
            hidden(0, 0)
            start = chain.n
            recurrence(PRE, 0)
            hidden(1, 1)
            recurrence(PRE, 1)
            hidden(2, 0)
            per = chain.n - start
            with dve.Fori(1, NSEQ - PRE) as i:
                chain.n, chain.base = start, i * per
                recurrence(i + PRE, 0)
                hidden(i * 2 + 1, 1)
                recurrence(i + PRE, 1)
                hidden(i * 2 + 2, 0)
            chain.n, chain.base = start + (NSEQ - PRE) * per, 0

            def each(w, nt):
                return w.rearrange("p (t a) -> p t a", a=1).to_broadcast([P, nt, E1])

            def top_gates(k):
                first, count = BATCHES[k]
                nt = 4 * count
                dve.wait_ge(c_lgs, first + count)
                for t in range(nt):
                    last = v.max(g8[:, t, :], lg1[:, 4 * first + t, :])
                link(last)
                for t in range(nt):
                    last = v.max_index(g8_i[:, t, :], g8[:, t, :], lg1[:, 4 * first + t, :])
                link(last)
                v.tensor_tensor(gd[:, 0:nt], g8[:, 0:nt, 0], g8[:, 0:nt, 1], ALU.subtract).then_inc(d_gd, 1)
                link(v.tensor_copy(g8_f[:, 0:nt, :], g8_i[:, 0:nt, 0:2]))

            def make_gates(k):
                nt = 4 * BATCHES[k][1]
                experts = iota_e[:, 0:E1].rearrange("p (a e) -> p a e", a=1).to_broadcast([P, nt, E1])
                ga, gb, pa = gates[:, 0:nt, :], gates2[:, 0:nt, :], gate_parts[:, 0:nt, :, :]
                v.tensor_tensor(ga, experts, each(g8_f[:, 0:nt, 0], nt), ALU.is_equal)
                link(v.tensor_tensor(gb, experts, each(g8_f[:, 0:nt, 1], nt), ALU.is_equal))
                dve.wait_ge(d_gth, k + 1)
                v.tensor_scalar(gw2[:, 0:nt, 0], gth[:, 0:nt], 0.5, 0.5, ALU.mult, ALU.add)
                link(v.tensor_scalar(gw2[:, 0:nt, 1], gth[:, 0:nt], -0.5, 0.5, ALU.mult, ALU.add))
                v.tensor_tensor(ga, ga, each(gw2[:, 0:nt, 0], nt), ALU.mult)
                link(v.tensor_tensor(gb, gb, each(gw2[:, 0:nt, 1], nt), ALU.mult))
                link(v.tensor_tensor(ga, ga, gb, ALU.add))
                if k:
                    dve.wait_ge(d_gT, k)
                with nc.allow_low_precision("three bfloat16 parts hold a float32 exactly"):
                    link(v.tensor_copy(pa[:, :, 0, :], ga))
                    link(v.tensor_tensor(ga, ga, pa[:, :, 0, :], ALU.subtract))
                    link(v.tensor_copy(pa[:, :, 1, :], ga))
                    v.tensor_tensor(pa[:, :, 2, :], ga, pa[:, :, 1, :], ALU.subtract).then_inc(d_gate, 1)

            for n in range(4 * E_NORM, N):
                q, step = norm_step(n)
                if q and step == 0:
                    norm1(q - 1)
                if q == FSEQ // 2 - 1 and step == 0:
                    top_gates(0)
                if step == 1:
                    sum_experts(2 * q)
                if step == 2:
                    sum_experts(2 * q + 1)
                if step == 3:
                    mix(q, False)
                    stats1(q)
                if step == 4:
                    rstd1()
                if n + 1 < N:
                    hidden(n + 1, (n + 1) % 2)
            rstd1()
            norm1(FSEQ // 2 - 1)

            def finish(b, u, first, used):
                dve.wait_ge(d_mth, b + 1)
                link(v.scalar_tensor_tensor(out=mg[:].rearrange("p a d -> p (a d)"), in0=mth[:], scalar=1.0,
                                            in1=bank(3, SEQ), op0=ALU.add, op1=ALU.mult))
                dve.wait_ge(d_os, b + 1)
                link(v.tensor_tensor(mg[:], mg[:], o_sb[u][:], ALU.mult))
                if not first:
                    dve.wait_ge(stored[u], 16 * used)
                v.scalar_tensor_tensor(out=fin[u], in0=mg[:], scalar=0.5, in1=x_tok[:, bass.ds(b * 2, 2), :],
                                       op0=ALU.mult, op1=ALU.add).then_inc(d_fin, 1)

            for b in range(NSEQ):
                u = b % 2
                dve.wait_ge(d_s, b + 1)
                link(v.tensor_reduce(mx[:], ps[:, 6, :].rearrange("p (a n) -> p a n", a=2), AX.X, ALU.max))
                v.tensor_scalar(nmx[:], mx[:], -SCALE, None, ALU.mult).then_inc(d_nmx, 1)
                if gated(b - 1) is not None:
                    make_gates(gated(b - 1))
                if turned(b) is not None:
                    stats1(turned(b))
                if gated(b) is not None:
                    top_gates(gated(b))
                if turned(b) is not None:
                    rstd1(summed(b))
                elif summed(b) is not None:
                    sum_experts(summed(b))
                dve.wait_ge(d_p, b + 1)
                link(v.reciprocal(rden[:], den[:]))
                def gate_hidden():
                    dve.wait_ge(d_gb, b + 1)
                    dve.wait_ge(d_hg, b + 1)
                    v.tensor_tensor(hg[u], hg[u], ps[:, 0:2, :].rearrange("p a (b n) -> p (a b) n", b=2),
                                    ALU.mult).then_inc(d_hs, 1)
                    if b:
                        finish(b - 1, 1 - u, b <= 2, (b - 1) // 2)

                def weigh_output():
                    dve.wait_ge(d_o, b + 1)
                    for j in range(2):
                        last = v.scalar_tensor_tensor(out=o_sb[u][:, j, :], in0=ps[:, 6, j * P:(j + 1) * P],
                                                      scalar=rden[:, j:j + 1], in1=bv_all[:], op0=ALU.mult, op1=ALU.add)
                    last.then_inc(d_os, 1)

                if turned(b) is not None:
                    weigh_output()
                    gate_hidden()
                else:
                    gate_hidden()
                    weigh_output()
                if turned(b) is not None:
                    norm1(turned(b))
                if turned(b + 1) is not None:
                    mix(turned(b + 1), True)
            finish(NSEQ - 1, 1, False, NSEQ // 2 - 1)


_INS = ['L0_attn_x', 'L0_attn_phazor', 'L0_attn_phazor_init', 'L0_attn_last_conv_re', 'L0_attn_last_conv_im',
        'L0_ffn_router_w', 'L0_ffn_w_gate', 'L0_ffn_w_up', 'L0_ffn_w_down', 'L0_ffn_sh_gate', 'L0_ffn_sh_up',
        'L0_ffn_sh_down', 'L0_ffn_sh_gate_w', 'L1_attn_wq', 'L1_attn_bq', 'L1_attn_wk', 'L1_attn_bk',
        'L1_attn_wv', 'L1_attn_bv', 'L1_ffn_w_gate', 'L1_ffn_w_fc', 'L1_ffn_w_proj']
_OUTS = [((NSEQ, SEQ, P), 'float32')]


def kernel(**inputs):
    import numpy as _np
    import concourse.bacc as _bacc
    from concourse import mybir as _mybir
    from concourse.bass_utils import run_bass_kernel_spmd as _run

    nc = _bacc.Bacc("TRN2", target_bir_lowering=False, num_devices=1)
    arrays, args = {}, []
    for name in _INS:
        a = _np.ascontiguousarray(inputs[name])
        arrays[f"in_{name}_dram"] = a
        args.append(nc.dram_tensor(f"in_{name}_dram", a.shape, _mybir.dt.from_np(a.dtype), kind="ExternalInput").ap())
    for i, (shape, dtype) in enumerate(_OUTS):
        dt = _mybir.dt.from_np(_np.dtype(dtype))
        args.append(nc.dram_tensor(f"out_{i}_dram", shape, dt, kind="ExternalOutput").ap())
    build(nc, *args)
    r = _run(nc, [arrays], core_ids=[0])
    got = tuple(r.results[0][f"out_{i}_dram"] for i in range(len(_OUTS)))
    return got[0]
```
